# Optimizing a Trainium2 kernel written in Bass

```python
import numpy as np
import jax
import jax.numpy as jnp

def _softmax(x, axis=-1):
    return jax.nn.softmax(x, axis=axis)

def _gelu(x):
    return jax.nn.gelu(x, approximate=True)

def _silu(x):
    return jax.nn.silu(x)

def _sigmoid(x):
    return jax.nn.sigmoid(x)

def _layernorm(x, axis=-1, eps=1e-05):
    m = jnp.mean(x, axis=axis, keepdims=True)
    v = jnp.var(x, axis=axis, keepdims=True)
    return (x - m) / jnp.sqrt(v + eps)

def _scatter_add(tgt, idx, src, axis=0):
    return tgt.at[idx].add(src)

def _segment_sum(src, seg, n):
    return jax.ops.segment_sum(src, seg, n)
kernel_name = 'mk_adaln_ffn_d2_seqx_r4_0c89f5'

def setup_inputs(seed: int=0):
    np.random.seed(seed)
    _w = jnp.asarray

    def _rec_inputs():
        import jax
        import jax.numpy as jnp
        _rk = jax.random.key(seed)
        x = -0.000125 + 0.9999 * jax.random.normal(jax.random.fold_in(_rk, 1), (4, 512, 512), jnp.float32)
        _lenS = 512 - jax.random.randint(jax.random.fold_in(_rk, 7), (4,), 0, max(1, 512 // 4) + 1, jnp.int32)
        _lenS2 = 512 - jax.random.randint(jax.random.fold_in(_rk, 8), (4,), 0, max(1, 512 // 4) + 1, jnp.int32)
        fside_BxSxS_0 = -1.52775e-05 + 0.999936 * jax.random.normal(jax.random.fold_in(_rk, 11), (4, 512, 512), jnp.float32)
        cond_512 = -5.03954e-05 + 1.00559 * jax.random.normal(jax.random.fold_in(_rk, 12), (4, 128), jnp.float32)
        return (x, fside_BxSxS_0, cond_512)
    x, fside_BxSxS_0, cond_512 = _rec_inputs()

    def _L0_cond_setup():
        import jax, jax.numpy as jnp
        from jax import lax
        import numpy as np
        B, T, C, TD = (8, 512, 512, 128)

        def _bi_wkv(r, k, v, w, u, time_emb):
            tf = jax.nn.sigmoid(jnp.sum(time_emb, axis=-1))[:, None, None]
            decay = jnp.exp(-jnp.exp(w.astype(jnp.float32)))[None, :] * (0.5 + 0.5 * tf[:, :, 0])
            kf = k.astype(jnp.float32)
            vf = v.astype(jnp.float32)
            ek = jnp.exp(jnp.minimum(kf, 30.0))
            ekv = ek * vf

            def step(carry, x):
                a, b = carry
                ekv_t, ek_t = x
                a = a * decay + ekv_t
                b = b * decay + ek_t
                return ((a, b), (a, b))
            ekv_t = jnp.swapaxes(ekv, 0, 1)
            ek_t = jnp.swapaxes(ek, 0, 1)
            init = (jnp.zeros_like(decay), jnp.zeros_like(decay))
            _, (nf, df) = lax.scan(step, init, (ekv_t, ek_t))
            _, (nb, db) = lax.scan(step, init, (ekv_t, ek_t), reverse=True)
            nf = jnp.swapaxes(nf, 0, 1)
            df = jnp.swapaxes(df, 0, 1)
            nb = jnp.swapaxes(nb, 0, 1)
            db = jnp.swapaxes(db, 0, 1)
            euk = jnp.exp(jnp.minimum(u.astype(jnp.float32)[None, None, :] + kf, 30.0))
            num = nf + nb - ekv + euk * vf
            den = df + db - ek + euk
            base = jax.nn.sigmoid(r.astype(jnp.float32)) * (num / jnp.maximum(den, 1e-08))
            out = base * (0.8 + 0.2 * tf)
            return out.astype(r.dtype)
        key = jax.random.key(seed)
        ks = jax.random.split(key, 6)
        return {'r': jax.random.normal(ks[0], (B, T, C), dtype=jnp.float32), 'k': jax.random.normal(ks[1], (B, T, C), dtype=jnp.float32), 'v': jax.random.normal(ks[2], (B, T, C), dtype=jnp.float32), 'w': jax.random.normal(ks[3], (C,), dtype=jnp.float32), 'u': jax.random.normal(ks[4], (C,), dtype=jnp.float32), 'time_emb': jax.random.normal(ks[5], (B, TD), dtype=jnp.float32)}
    _L0_cond_all = _L0_cond_setup()
    _L0_cond_in = {k: v for k, v in _L0_cond_all.items() if k in ('w', 'u')}
    del _L0_cond_all

    def _L0_ffn_setup():
        import jax, jax.numpy as jnp
        import numpy as np
        E = 8
        K = 2
        DIM = 512
        INTER = 352
        N_SHARED = 2
        STD = 0.02
        key = jax.random.key(seed)
        ks = jax.random.split(key, 9)
        B, S = (2, 512)
        return {'x': jax.random.normal(ks[0], (B, S, DIM), dtype=jnp.float32), 'gate_w': jax.random.normal(ks[1], (E, DIM), dtype=jnp.float32) * STD, 'router_bias': jnp.zeros((E,), dtype=jnp.float32), 'W1': jax.random.normal(ks[2], (E, DIM, INTER), dtype=jnp.float32) * STD, 'W3': jax.random.normal(ks[3], (E, DIM, INTER), dtype=jnp.float32) * STD, 'W2': jax.random.normal(ks[4], (E, INTER, DIM), dtype=jnp.float32) * STD, 'sw1': jax.random.normal(ks[5], (N_SHARED * INTER, DIM), dtype=jnp.float32) * STD, 'sw3': jax.random.normal(ks[6], (N_SHARED * INTER, DIM), dtype=jnp.float32) * STD, 'sw2': jax.random.normal(ks[7], (DIM, N_SHARED * INTER), dtype=jnp.float32) * STD}
    _L0_ffn_all = _L0_ffn_setup()
    _L0_ffn_in = {k: v for k, v in _L0_ffn_all.items() if k in ('gate_w', 'router_bias', 'W1', 'W3', 'W2', 'sw1', 'sw3', 'sw2')}
    del _L0_ffn_all

    def _L1_cond_setup():
        import jax, jax.numpy as jnp
        from jax import lax
        import numpy as np
        B, T, C, TD = (8, 512, 512, 128)

        def _bi_wkv(r, k, v, w, u, time_emb):
            tf = jax.nn.sigmoid(jnp.sum(time_emb, axis=-1))[:, None, None]
            decay = jnp.exp(-jnp.exp(w.astype(jnp.float32)))[None, :] * (0.5 + 0.5 * tf[:, :, 0])
            kf = k.astype(jnp.float32)
            vf = v.astype(jnp.float32)
            ek = jnp.exp(jnp.minimum(kf, 30.0))
            ekv = ek * vf

            def step(carry, x):
                a, b = carry
                ekv_t, ek_t = x
                a = a * decay + ekv_t
                b = b * decay + ek_t
                return ((a, b), (a, b))
            ekv_t = jnp.swapaxes(ekv, 0, 1)
            ek_t = jnp.swapaxes(ek, 0, 1)
            init = (jnp.zeros_like(decay), jnp.zeros_like(decay))
            _, (nf, df) = lax.scan(step, init, (ekv_t, ek_t))
            _, (nb, db) = lax.scan(step, init, (ekv_t, ek_t), reverse=True)
            nf = jnp.swapaxes(nf, 0, 1)
            df = jnp.swapaxes(df, 0, 1)
            nb = jnp.swapaxes(nb, 0, 1)
            db = jnp.swapaxes(db, 0, 1)
            euk = jnp.exp(jnp.minimum(u.astype(jnp.float32)[None, None, :] + kf, 30.0))
            num = nf + nb - ekv + euk * vf
            den = df + db - ek + euk
            base = jax.nn.sigmoid(r.astype(jnp.float32)) * (num / jnp.maximum(den, 1e-08))
            out = base * (0.8 + 0.2 * tf)
            return out.astype(r.dtype)
        key = jax.random.key(seed)
        ks = jax.random.split(key, 6)
        return {'r': jax.random.normal(ks[0], (B, T, C), dtype=jnp.float32), 'k': jax.random.normal(ks[1], (B, T, C), dtype=jnp.float32), 'v': jax.random.normal(ks[2], (B, T, C), dtype=jnp.float32), 'w': jax.random.normal(ks[3], (C,), dtype=jnp.float32), 'u': jax.random.normal(ks[4], (C,), dtype=jnp.float32), 'time_emb': jax.random.normal(ks[5], (B, TD), dtype=jnp.float32)}
    _L1_cond_all = _L1_cond_setup()
    _L1_cond_in = {k: v for k, v in _L1_cond_all.items() if k in ('w', 'u')}
    del _L1_cond_all

    def _L1_ffn_setup():
        import jax, jax.numpy as jnp
        import numpy as np
        TOPK = 2
        HID, INTER, E, SHARED_INTER = (512, 352, 14, 704)
        key = jax.random.key(seed)
        ks = jax.random.split(key, 11)
        s = 0.02
        return {'x': jax.random.normal(ks[0], (4, 128, HID), jnp.float32), 'gate_w': jax.random.normal(ks[1], (E, HID), jnp.float32) * s, 'cls_w': jax.random.normal(ks[2], (E, HID), jnp.float32) * s, 'extra_scale': jax.random.normal(ks[3], (E,), jnp.float32) * 0.1, 'extra_bias': jax.random.normal(ks[4], (E,), jnp.float32) * 0.01, 'wg': jax.random.normal(ks[5], (E, INTER, HID), jnp.float32) * s, 'wu': jax.random.normal(ks[6], (E, INTER, HID), jnp.float32) * s, 'wd': jax.random.normal(ks[7], (E, HID, INTER), jnp.float32) * s, 'sg': jax.random.normal(ks[8], (SHARED_INTER, HID), jnp.float32) * s, 'su': jax.random.normal(ks[9], (SHARED_INTER, HID), jnp.float32) * s, 'sd': jax.random.normal(ks[10], (HID, SHARED_INTER), jnp.float32) * s}
    _L1_ffn_all = _L1_ffn_setup()
    _L1_ffn_in = {k: v for k, v in _L1_ffn_all.items() if k in ('gate_w', 'cls_w', 'extra_scale', 'extra_bias', 'wg', 'wu', 'wd', 'sg', 'su', 'sd')}
    del _L1_ffn_all
    return {'x': x, 'fside_BxSxS_0': fside_BxSxS_0, 'cond_512': cond_512, 'L0_cond_w': _L0_cond_in['w'], 'L0_cond_u': _L0_cond_in['u'], 'L0_ffn_gate_w': _L0_ffn_in['gate_w'], 'L0_ffn_router_bias': _L0_ffn_in['router_bias'], 'L0_ffn_W1': _L0_ffn_in['W1'], 'L0_ffn_W3': _L0_ffn_in['W3'], 'L0_ffn_W2': _L0_ffn_in['W2'], 'L0_ffn_sw1': _L0_ffn_in['sw1'], 'L0_ffn_sw3': _L0_ffn_in['sw3'], 'L0_ffn_sw2': _L0_ffn_in['sw2'], 'L1_cond_w': _L1_cond_in['w'], 'L1_cond_u': _L1_cond_in['u'], 'L1_ffn_gate_w': _L1_ffn_in['gate_w'], 'L1_ffn_cls_w': _L1_ffn_in['cls_w'], 'L1_ffn_extra_scale': _L1_ffn_in['extra_scale'], 'L1_ffn_extra_bias': _L1_ffn_in['extra_bias'], 'L1_ffn_wg': _L1_ffn_in['wg'], 'L1_ffn_wu': _L1_ffn_in['wu'], 'L1_ffn_wd': _L1_ffn_in['wd'], 'L1_ffn_sg': _L1_ffn_in['sg'], 'L1_ffn_su': _L1_ffn_in['su'], 'L1_ffn_sd': _L1_ffn_in['sd']}

def reference(x, fside_BxSxS_0, cond_512, L0_cond_w, L0_cond_u, L0_ffn_gate_w, L0_ffn_router_bias, L0_ffn_W1, L0_ffn_W3, L0_ffn_W2, L0_ffn_sw1, L0_ffn_sw3, L0_ffn_sw2, L1_cond_w, L1_cond_u, L1_ffn_gate_w, L1_ffn_cls_w, L1_ffn_extra_scale, L1_ffn_extra_bias, L1_ffn_wg, L1_ffn_wu, L1_ffn_wd, L1_ffn_sg, L1_ffn_su, L1_ffn_sd):
    import jax
    import jax.numpy as jnp

    def _L0_cond_ref(r, k, v, w, u, time_emb):
        import jax, jax.numpy as jnp
        from jax import lax
        import numpy as np
        B, T, C, TD = (8, 512, 512, 128)

        def _bi_wkv(r, k, v, w, u, time_emb):
            tf = jax.nn.sigmoid(jnp.sum(time_emb, axis=-1))[:, None, None]
            decay = jnp.exp(-jnp.exp(w.astype(jnp.float32)))[None, :] * (0.5 + 0.5 * tf[:, :, 0])
            kf = k.astype(jnp.float32)
            vf = v.astype(jnp.float32)
            ek = jnp.exp(jnp.minimum(kf, 30.0))
            ekv = ek * vf

            def step(carry, x):
                a, b = carry
                ekv_t, ek_t = x
                a = a * decay + ekv_t
                b = b * decay + ek_t
                return ((a, b), (a, b))
            ekv_t = jnp.swapaxes(ekv, 0, 1)
            ek_t = jnp.swapaxes(ek, 0, 1)
            init = (jnp.zeros_like(decay), jnp.zeros_like(decay))
            _, (nf, df) = lax.scan(step, init, (ekv_t, ek_t))
            _, (nb, db) = lax.scan(step, init, (ekv_t, ek_t), reverse=True)
            nf = jnp.swapaxes(nf, 0, 1)
            df = jnp.swapaxes(df, 0, 1)
            nb = jnp.swapaxes(nb, 0, 1)
            db = jnp.swapaxes(db, 0, 1)
            euk = jnp.exp(jnp.minimum(u.astype(jnp.float32)[None, None, :] + kf, 30.0))
            num = nf + nb - ekv + euk * vf
            den = df + db - ek + euk
            base = jax.nn.sigmoid(r.astype(jnp.float32)) * (num / jnp.maximum(den, 1e-08))
            out = base * (0.8 + 0.2 * tf)
            return out.astype(r.dtype)
        return _bi_wkv(r, k, v, w, u, time_emb)

    def _L0_ffn_ref(x, gate_w, router_bias, W1, W3, W2, sw1, sw3, sw2):
        import jax, jax.numpy as jnp
        import numpy as np
        E = 8
        K = 2
        DIM = 512
        INTER = 352
        N_SHARED = 2
        STD = 0.02
        B, S, D = x.shape
        X = x.reshape(-1, D)
        T = X.shape[0]
        logits = jnp.einsum('td,ed->te', X, gate_w)
        scores = jax.nn.sigmoid(logits)
        sel = scores + router_bias[None, :]
        _, idx = jax.lax.top_k(sel, K)
        w = jnp.take_along_axis(scores, idx, axis=1)
        w = w / jnp.clip(jnp.sum(w, axis=-1, keepdims=True), 1e-12)
        gate_full = jnp.zeros((T, E), dtype=w.dtype).at[jnp.arange(T)[:, None], idx].set(w)
        h1 = jnp.einsum('td,edh->eth', X, W1)
        h3 = jnp.einsum('td,edh->eth', X, W3)
        y = jnp.einsum('eth,ehd->etd', jax.nn.silu(h1) * h3, W2)
        out = jnp.einsum('etd,te->td', y, gate_full)
        shared = jnp.einsum('th,dh->td', jax.nn.silu(jnp.einsum('td,hd->th', X, sw1)) * jnp.einsum('td,hd->th', X, sw3), sw2)
        out = out + shared
        return out.reshape(B, S, D)

    def _L1_cond_ref(r, k, v, w, u, time_emb):
        import jax, jax.numpy as jnp
        from jax import lax
        import numpy as np
        B, T, C, TD = (8, 512, 512, 128)

        def _bi_wkv(r, k, v, w, u, time_emb):
            tf = jax.nn.sigmoid(jnp.sum(time_emb, axis=-1))[:, None, None]
            decay = jnp.exp(-jnp.exp(w.astype(jnp.float32)))[None, :] * (0.5 + 0.5 * tf[:, :, 0])
            kf = k.astype(jnp.float32)
            vf = v.astype(jnp.float32)
            ek = jnp.exp(jnp.minimum(kf, 30.0))
            ekv = ek * vf

            def step(carry, x):
                a, b = carry
                ekv_t, ek_t = x
                a = a * decay + ekv_t
                b = b * decay + ek_t
                return ((a, b), (a, b))
            ekv_t = jnp.swapaxes(ekv, 0, 1)
            ek_t = jnp.swapaxes(ek, 0, 1)
            init = (jnp.zeros_like(decay), jnp.zeros_like(decay))
            _, (nf, df) = lax.scan(step, init, (ekv_t, ek_t))
            _, (nb, db) = lax.scan(step, init, (ekv_t, ek_t), reverse=True)
            nf = jnp.swapaxes(nf, 0, 1)
            df = jnp.swapaxes(df, 0, 1)
            nb = jnp.swapaxes(nb, 0, 1)
            db = jnp.swapaxes(db, 0, 1)
            euk = jnp.exp(jnp.minimum(u.astype(jnp.float32)[None, None, :] + kf, 30.0))
            num = nf + nb - ekv + euk * vf
            den = df + db - ek + euk
            base = jax.nn.sigmoid(r.astype(jnp.float32)) * (num / jnp.maximum(den, 1e-08))
            out = base * (0.8 + 0.2 * tf)
            return out.astype(r.dtype)
        return _bi_wkv(r, k, v, w, u, time_emb)

    def _L1_ffn_ref(x, gate_w, cls_w, extra_scale, extra_bias, wg, wu, wd, sg, su, sd):
        import jax, jax.numpy as jnp
        import numpy as np
        TOPK = 2
        HID, INTER, E, SHARED_INTER = (512, 352, 14, 704)
        shape = x.shape
        d = shape[-1]
        xf = x.reshape(-1, d)
        T = xf.shape[0]
        n_exp = gate_w.shape[0]
        logits = xf @ cls_w.T * jax.nn.silu(xf @ gate_w.T)
        scores = jax.nn.softmax(jnp.abs(logits).astype(jnp.float32), axis=-1)
        biased = scores + extra_bias[None, :]
        _, idx = jax.lax.top_k(biased, TOPK)
        orig = 1.0 + scores * extra_scale[None, :]
        w = jnp.take_along_axis(orig, idx, axis=1).astype(x.dtype)
        combine = jnp.zeros((T, n_exp), x.dtype).at[jnp.arange(T)[:, None], idx].add(w)
        g = jax.nn.silu(jnp.einsum('td,efd->etf', xf, wg))
        u = jnp.einsum('td,efd->etf', xf, wu)
        o = jnp.einsum('etf,edf->etd', g * u, wd)
        y = jnp.einsum('etd,te->td', o, combine)
        z = jax.nn.silu(xf @ sg.T) * (xf @ su.T) @ sd.T
        return (y + z).reshape(shape)
    x = x + _L0_ffn_ref(_L0_cond_ref(x, fside_BxSxS_0, fside_BxSxS_0, L0_cond_w, L0_cond_u, cond_512), L0_ffn_gate_w, L0_ffn_router_bias, L0_ffn_W1, L0_ffn_W3, L0_ffn_W2, L0_ffn_sw1, L0_ffn_sw3, L0_ffn_sw2)
    x = x + _L1_ffn_ref(_L1_cond_ref(x, fside_BxSxS_0, fside_BxSxS_0, L1_cond_w, L1_cond_u, cond_512), L1_ffn_gate_w, L1_ffn_cls_w, L1_ffn_extra_scale, L1_ffn_extra_bias, L1_ffn_wg, L1_ffn_wu, L1_ffn_wd, L1_ffn_sg, L1_ffn_su, L1_ffn_sd)
    return x

_drawn_inputs = setup_inputs


def setup_inputs(seed=0):
    import zlib

    import numpy as np

    out = dict(_drawn_inputs(seed))
    spreads = {'L0_ffn_router_bias': (0.0, 0.8)}
    factors = {'fside_BxSxS_0': 2.966,
     'cond_512': 8.0,
     'L0_cond_w': 7.171,
     'L0_cond_u': 8.0,
     'L0_ffn_gate_w': 8.0,
     'L0_ffn_W1': 8.0,
     'L0_ffn_W3': 8.0,
     'L0_ffn_W2': 8.0,
     'L0_ffn_sw1': 4.995,
     'L0_ffn_sw3': 4.746,
     'L0_ffn_sw2': 4.929,
     'L1_cond_w': 5.547,
     'L1_cond_u': 8.0,
     'L1_ffn_gate_w': 8.0,
     'L1_ffn_cls_w': 8.0,
     'L1_ffn_extra_scale': 8.0,
     'L1_ffn_extra_bias': 5.296,
     'L1_ffn_wg': 4.962,
     'L1_ffn_wu': 4.968,
     'L1_ffn_wd': 4.92,
     'L1_ffn_sg': 5.007,
     'L1_ffn_su': 4.954,
     'L1_ffn_sd': 4.946}
    for name, (base, spread) in spreads.items():
        noise = np.random.default_rng([zlib.crc32(name.encode()), seed]).standard_normal(out[name].shape)
        drawn = base * np.exp(spread * noise) if base else spread * noise
        out[name] = jnp.asarray(drawn.astype(out[name].dtype))
    for name, factor in factors.items():
        out[name] = (out[name] * factor).astype(out[name].dtype)
    return out
```

```python
from contextlib import ExitStack

import numpy as np
import concourse.bass as bass
from concourse import mybir

P = 128
B, T, D = 4, 512, 512
N = B * T
NT = N // P
C = D // P
F = 352
FC = -(-F // P)
EXPERTS = (8, 14)
K = 2
SLOTS = tuple(N * K // P + e for e in EXPERTS)
UP = C * 2 * F
WC = UP + FC * D
EM, SM = max(EXPERTS), max(SLOTS)
LAYERS = len(EXPERTS)
NW = LAYERS * B * C
E30 = float(np.float32(np.exp(np.float32(30.0))))


def build(nc, x, kt, cond, wdec, ub, gates, bias, scale1, wts, out):
    f32, i32 = mybir.dt.float32, mybir.dt.int32
    ALU, ACT, AX = mybir.AluOpType, mybir.ActivationFunctionType, mybir.AxisListType
    ds = bass.ds
    ctx = ExitStack()
    with ctx:
        def sb(name, shape, dt=f32):
            return ctx.enter_context(nc.sbuf_tensor(name, shape, dt))

        def ps(name):
            return ctx.enter_context(nc.psum_tensor(name, [P, 512], f32))

        def sem(name):
            return ctx.enter_context(nc.semaphore(name))

        slot_x = nc.dram_tensor("slot_x", [SM * P, D], f32, kind="Internal").ap()
        slot_y = [nc.dram_tensor(f"slot_y{l}", [SLOTS[l] * P, D], f32, kind="Internal").ap() for l in range(LAYERS)]
        base_d = nc.dram_tensor("base_d", [N, D], f32, kind="Internal").ap()

        xacc = sb("xacc", [P, NT, D])
        ratio = sb("ratio", [P, B, C, T])
        wbuf = [sb(f"wbuf{i}", [P, WC]) for i in range(2)]
        ident = sb("ident", [P, P])
        before = sb("before", [P, P])
        ones = sb("ones", [P, P])
        xin = [sb(f"xin{i}", [P, D]) for i in range(2)]
        tnh = [sb(f"tnh{i}", [P, D]) for i in range(2)]
        bT = [sb(f"bT{i}", [P, C, P]) for i in range(4)]
        btok = [sb(f"btok{i}", [P, D]) for i in range(2)]
        xs = [sb(f"xs{i}", [P, D]) for i in range(2)]
        xT = [sb(f"xT{i}", [P, C, P]) for i in range(2)]
        th = [sb(f"th{i}", [P, F]) for i in range(2)]
        g = [sb(f"g{i}", [P, FC * P]) for i in range(2)]
        gT = sb("gT", [P, FC, P])
        yb = [sb(f"yb{i}", [P, D]) for i in range(2)]
        kb = [sb(f"kb{i}", [P, T]) for i in range(2)]
        ek = [sb(f"ek{i}", [P, T]) for i in range(2)]
        euk = [sb(f"euk{i}", [P, T]) for i in range(2)]
        ekv, eukv = sb("ekv", [P, T]), sb("eukv", [P, T])
        fwd = sb("fwd", [P, T])
        bwd = sb("bwd", [P, T + 1])
        rec = sb("rec", [P, T])
        ga, gb = ek, euk
        condb = sb("condb", [P, B, P])
        wl = sb("wl", [P, LAYERS, C])
        ul = sb("ul", [P, NW])
        dec = sb("dec", [P, LAYERS, B, C])
        osc = sb("osc", [P, LAYERS, B, C])
        tf = sb("tf", [P, B])
        dfac, sfac = sb("dfac", [P, B]), sb("sfac", [P, B])
        gw = [sb("gw0", [P, C, EXPERTS[0]]), sb("gw1", [P, C, 2 * EXPERTS[1]])]
        biasb = [sb(f"biasb{l}", [P, NT, EXPERTS[l]]) for l in range(LAYERS)]
        scaleb = sb("scaleb", [P, NT, EXPERTS[1]])
        iota_e = sb("iota_e", [P, NT, EM])
        rows_j = sb("rows_j", [P, EM, NT])
        iota_s = sb("iota_s", [P, SM, EM])
        seg = sb("seg", [P, EM, NT])
        rA = sb("rA", [P, NT * 2 * EM])
        rB = sb("rB", [P, NT * EM])
        rC = sb("rC", [P, NT * EM])
        rD = sb("rD", [P, SM * EM])
        oh = [sb(f"oh{i}", [P, NT * EM]) for i in range(2)]
        both = sb("both", [P, NT * EM])
        m16 = [sb(f"m16{i}", [P, NT]) for i in range(3)]
        cnt = [sb(f"cnt{i}", [P, EM]) for i in range(3)]
        wsel = [sb(f"wsel{i}", [P, NT]) for i in range(2)]
        pos = [sb(f"pos{i}", [P, NT], i32) for i in range(2)]
        expert_of = sb("expert_of", [P, SM], i32)

        h1 = [ps(f"h1_{i}") for i in range(2)]
        h3 = [ps(f"h3_{i}") for i in range(2)]
        XT, GT, Y, LG = ps("XT"), ps("GT"), ps("Y"), ps("LG")

        params_in = sem("params_in")
        wkv_p_in = sem("wkv_p_in")
        xacc_in = sem("xacc_in")
        consts = sem("consts")
        zeroed = sem("zeroed")
        x_in = [sem(f"x_in{i}") for i in range(2)]
        w_in = [sem(f"w_in{i}") for i in range(2)]
        xs_in = [sem(f"xs_in{i}") for i in range(2)]
        y_out = [sem(f"y_out{i}") for i in range(2)]
        k_in = [sem(f"k_in{i}") for i in range(2)]
        base_out = [sem(f"base_out{i}") for i in range(2)]
        d_in = [sem(f"d_in{i}") for i in range(2)]
        scattered = [sem(f"scattered{i}") for i in range(2)]
        gathered = [sem(f"gathered{i}") for i in range(2)]
        out_st = [sem(f"out_st{i}") for i in range(2)]
        h1_ps, h3_ps = sem("h1_ps"), sem("h3_ps")
        tanh_sb = sem("tanh_sb")
        g_sb = sem("g_sb")
        gT_ps, gT_sb = sem("gT_ps"), sem("gT_sb")
        unit_done = sem("unit_done")
        y_added = sem("y_added")
        y_copied = sem("y_copied")
        xT_ps, xT_sb = sem("xT_ps"), sem("xT_sb")
        bT_sb = sem("bT_sb")
        logits = sem("logits")
        xnew = sem("xnew")
        xcopied = sem("xcopied")
        exp_k, exp_u = sem("exp_k"), sem("exp_u")
        min_k, min_u = sem("min_k"), sem("min_u")
        kv, ukv = sem("kv"), sem("ukv")
        wkv = sem("wkv")
        step = sem("step")
        astep = sem("astep")
        rt_dve, rt_act, rt_pe = sem("rt_dve"), sem("rt_act"), sem("rt_pe")
        routed = sem("routed")
        spd = sem("spd")

        U = [0, 2 * NT + SLOTS[0]]
        X = [0, 2 * NT + SLOTS[0]]
        WL = [0, 1 + SLOTS[0] // 2]

        block = ctx.enter_context(nc.Block())

        @block.sync
        def _(sp):
            def load_x(t, par):
                sp.dma_start(xin[par][:, :], x[ds(t * P, P), :]).then_inc(x_in[par], 16)

            def load_w(l, e, par):
                sp.dma_start(wbuf[par][:, :], wts[l][ds(e, 1), :, :].rearrange("e p n -> (e p) n")).then_inc(w_in[par], 16)

            def load_slot(l, s, par):
                sp.dma_start(xs[par][:, :], slot_x[ds(s * P, P), :]).then_inc(xs_in[par], 16)

            def store_y(l, s, par):
                sp.wait_ge(y_copied, (SLOTS[0] if l else 0) + s + 1)
                sp.dma_start(slot_y[l][ds(s * P, P), :], yb[par][:, :]).then_inc(y_out[par], 16)

            def store_base(l, t, par):
                sp.wait_ge(xT_sb, X[l] + 2 * t + 2)
                sp.dma_start(base_d[ds(t * P, P), :], btok[par][:, :]).then_inc(base_out[par], 16)

            for l in range(LAYERS):
                E, NS = EXPERTS[l], SLOTS[l]
                if l == 0:
                    sp.dma_start(condb[:, :, :], cond.rearrange("p (b n) -> p b n", b=B)).then_inc(wkv_p_in, 16)
                    sp.dma_start(wl[:, :, :], wdec.rearrange("p (l c) -> p l c", l=LAYERS)).then_inc(wkv_p_in, 16)
                    sp.dma_start(ul[:, :], ub).then_inc(wkv_p_in, 16)
                    for t in range(2):
                        load_x(t, t)
                    for i in range(2):
                        sp.dma_start(gw[i][:, :, :], gates[i].rearrange("p (c e) -> p c e", c=C)).then_inc(params_in, 16)
                        sp.dma_start(biasb[i][:, :, :], bias[i].rearrange("p (t e) -> p t e", t=NT)).then_inc(params_in, 16)
                    sp.dma_start(scaleb[:, :, :], scale1.rearrange("p (t e) -> p t e", t=NT)).then_inc(params_in, 16)
                for par in range(2):
                    if l:
                        sp.wait_ge(unit_done, U[l] - 1 + par)
                    load_w(l, E + par, par)
                if l == 0:
                    for b in range(B):
                        sp.dma_start(xacc[:, 4 * b:4 * b + 4, :],
                                     x[b * T:(b + 1) * T, :].rearrange("(t p) n -> p t n", p=P)).then_inc(xacc_in, 16)
                with sp.Fori(0, NT // 2 - 1) as i:
                    for par in range(2):
                        t = 2 * i + par
                        store_base(l, t, par)
                        if l == 0:
                            load_x(t + 2, par)
                for par in range(2):
                    store_base(l, NT - 2 + par, par)
                for par in range(2):
                    sp.wait_ge(scattered[par], 16 * K * (NT // 2) * (l + 1))
                sp.wait_ge(routed, l + 1)
                for s in range(2):
                    load_slot(l, s, s)
                for s in range(2):
                    e = sp.value_load(expert_of[0:1, s:s + 1], min_val=0, max_val=E - 1)
                    sp.wait_ge(unit_done, U[l] + 2 * NT + s - 1)
                    load_w(l, e, s)
                with sp.Fori(0, NS // 2 - 1) as i:
                    for par in range(2):
                        s = 2 * i + par
                        sp.wait_ge(xT_ps, X[l] + 2 * NT + s + 1)
                        load_slot(l, s + 2, par)
                        e = sp.value_load(expert_of[0:1, ds(s + 2, 1)], min_val=0, max_val=E - 1)
                        sp.wait_ge(unit_done, U[l] + 2 * NT + s + 1)
                        load_w(l, e, par)
                        store_y(l, s, par)
                for par in range(2):
                    store_y(l, NS - 2 + par, par)
            with sp.Fori(0, NT // 2) as i:
                for par in range(2):
                    t = 2 * i + par
                    sp.wait_ge(xnew, NT + t + 1)
                    sp.dma_start(out[ds(t * P, P), :], xin[par][:, :]).then_inc(out_st[par], 16)
            for par in range(2):
                sp.wait_ge(out_st[par], 16 * (NT // 2))

        @block.gpsimd
        def _(pool):
            nc.gpsimd.memset(ones[:, :], 1.0).then_inc(consts, 1)
            nc.gpsimd.memset(ident[:, :], 0.0).then_inc(consts, 1)
            nc.gpsimd.memset(rD[:, 0:D], 0.0).then_inc(consts, 1)
            for n in range(2):
                pool.dma_start(kb[n][:, :], kt[n, :, :]).then_inc(k_in[n], 16)
            pool.wait_ge(consts, 3)
            pool.dma_start(slot_x.rearrange("(s p) n -> p s n", p=P),
                           rD[:, 0:D].rearrange("p (s n) -> p s n", s=1).to_broadcast([P, SM, D])).then_inc(zeroed, 16)
            nc.gpsimd.affine_select(out=ident[:, :], in_=ident[:, :], compare_op=ALU.not_equal, fill=1.0, base=0,
                                    pattern=[[-1, P]], channel_multiplier=1).then_inc(consts, 1)
            nc.gpsimd.affine_select(out=before[:, :], in_=ones[:, :], compare_op=ALU.is_gt, fill=0.0, base=0,
                                    pattern=[[1, P]], channel_multiplier=-1).then_inc(consts, 1)
            def iota(dst, pattern):
                nc.gpsimd.iota(dst, pattern, base=0, channel_multiplier=0,
                               allow_small_or_imprecise_dtypes=True).then_inc(consts, 1)
            iota(iota_e[:, :, :], [[0, NT], [1, EM]])
            iota(rows_j[:, :, :], [[0, EM], [P, NT]])
            iota(iota_s[:, :, :], [[1, SM], [0, EM]])
            iota(seg[:, :, :], [[0, EM], [1, NT]])

            def products(n, par, load=True):
                pool.wait_ge(min_k, n + 1)
                if not (isinstance(n, int) and n == 0):
                    pool.wait_ge(wkv, n)
                nc.gpsimd.tensor_tensor(ekv[:, :], ek[par][:, :], kb[par][:, :], ALU.mult).then_inc(kv, 1)
                pool.wait_ge(min_u, n + 1)
                nc.gpsimd.tensor_tensor(eukv[:, :], euk[par][:, :], kb[par][:, :], ALU.mult).then_inc(ukv, 1)
                if load:
                    pool.wait_ge(ukv, n + 1)
                    pool.wait_ge(kv, n + 1)
                    pool.dma_start(kb[par][:, :], kt[ds(n + 2, 1), :, :].rearrange("n p t -> (n p) t")).then_inc(k_in[par], 16)

            def dispatch(l, t, par, first):
                if not first:
                    pool.wait_ge(scattered[par], 16 * K * (l * (NT // 2) + t // 2))
                pool.wait_ge(base_out[par], 16 * (l * (NT // 2) + t // 2 + 1))
                pool.dma_start(yb[par][:, :], base_d[t * P:(t + 1) * P, :]).then_inc(d_in[par], 16)
                pool.wait_ge(d_in[par], 16 * (l * (NT // 2) + t // 2 + 1))
                for j in range(K):
                    nc.gpsimd.indirect_dma_start(slot_x[:, :], bass.IndirectOffsetOnAxis(ap=pos[j][:, t:t + 1], axis=0),
                                                 yb[par][:, :], None).then_inc(scattered[par], 16)

            def gather(l, t, par):
                if t >= 2:
                    pool.wait_ge(xnew, NT * l + t - 1)
                for j, dst in enumerate((ga, gb)):
                    nc.gpsimd.indirect_dma_start(dst[par][:, :], None, slot_y[l][:, :],
                                                 bass.IndirectOffsetOnAxis(ap=pos[j][:, t:t + 1], axis=0)
                                                 ).then_inc(gathered[par], 16)

            for c in range(C):
                products(c, c % 2)
            with pool.Fori(0, B - 1) as b:
                for c in range(C):
                    products(b * C + C + c, c % 2)
            for l in range(LAYERS):
                if l == 0:
                    pool.wait_ge(zeroed, 16)
                pool.wait_ge(routed, l + 1)
                if l:
                    pool.wait_ge(unit_done, U[1] + 2 * NT - 8)
                for t in range(NT):
                    dispatch(l, t, t % 2, t < 2)
                if l == 0:
                    with pool.Fori(0, NW // 4 - 1) as i:
                        for j in range(2):
                            products(2 * i + NW // 2 + j, j)
                    for j in range(2):
                        products(NW - 2 + j, j, load=False)
                for par in range(2):
                    pool.wait_ge(y_out[par], 16 * (sum(SLOTS[:l + 1]) // 2))
                if l == 0:
                    pool.wait_ge(wkv, NW)
                for t in range(NT):
                    gather(l, t, t % 2)

        @block.scalar
        def _(act):
            def exps(n, par):
                act.wait_ge(k_in[par], 16 * (n // 2 + 1) if isinstance(n, int) else n * 8 + (16 - 8 * par))
                if not (isinstance(n, int) and n < 2):
                    act.wait_ge(wkv, n - 1)
                nc.scalar.activation(ek[par][:, :], kb[par][:, :], ACT.Exp).then_inc(exp_k, 1)
                nc.scalar.activation(euk[par][:, :], kb[par][:, :], ACT.Exp, bias=ul[:, ds(n, 1)]).then_inc(exp_u, 1)

            def prep(l, t, par):
                if l:
                    act.wait_ge(xnew, t + 1)
                    nc.scalar.activation(xacc[:, ds(t, 1), :].rearrange("p a n -> p (a n)"), xin[par][:, :], ACT.Copy).then_inc(xcopied, 1)
                act.wait_ge(xT_ps, X[l] + 2 * t + 1)
                nc.scalar.activation(tnh[par][:, :], XT[:, :], ACT.Tanh, scale=0.5).then_inc(xT_sb, 1)
                act.wait_ge(xT_ps, X[l] + 2 * t + 2)
                if not (isinstance(t, int) and l == 0 and t < 2):
                    act.wait_ge(base_out[par], (t - par) * 8 + 16 * l * (NT // 2))
                nc.scalar.activation(btok[par][:, :], XT[:, :], ACT.Copy).then_inc(xT_sb, 1)

            def tanh(u, par):
                act.wait_ge(h1_ps, u + 1)
                nc.scalar.activation(th[par][:, :], h1[par][:, 0:F], ACT.Tanh, scale=0.5).then_inc(tanh_sb, 1)

            def copy_gT(u, par):
                act.wait_ge(gT_ps, u + 1)
                nc.scalar.activation(gT[:, :, :].rearrange("p a b -> p (a b)"), GT[:, 0:FC * P], ACT.Copy).then_inc(gT_sb, 1)

            def copy_xT(l, s, par):
                act.wait_ge(xT_ps, X[l] + 2 * NT + s + 1)
                nc.scalar.activation(xT[par][:, :, :].rearrange("p a b -> p (a b)"), XT[:, :], ACT.Copy).then_inc(xT_sb, 1)

            def copy_y(l, s, par, first=False):
                act.wait_ge(unit_done, U[l] + 2 * NT + s + 1)
                if first:
                    act.wait_ge(scattered[par], 16 * K * (NT // 2) * (l + 1))
                else:
                    act.wait_ge(y_out[par], 16 * (l * SLOTS[0] // 2) + 8 * (s - par))
                nc.scalar.activation(yb[par][:, :], Y[:, :], ACT.Copy).then_inc(y_copied, 1)

            act.wait_ge(wkv_p_in, 48)
            nc.scalar.activation(wl[:, :, :], wl[:, :, :], ACT.Exp).then_inc(astep, 1)
            act.wait_ge(astep, 1)
            nc.scalar.activation(wl[:, :, :], wl[:, :, :], ACT.Exp, scale=-1.0).then_inc(astep, 1)
            act.wait_ge(step, 1)
            nc.scalar.activation(tf[:, :], tf[:, :], ACT.Tanh, scale=0.5).then_inc(astep, 1)
            for n in range(C + 1):
                exps(n, n % 2)
            for l in range(LAYERS):
                NS = SLOTS[l]
                for t in range(4):
                    prep(l, t, t % 2)
                tanh(U[l], 0)
                with act.Fori(0, B - 1) as b:
                    for k in range(8):
                        u = b * 8 + (U[l] + k)
                        if k == 7:
                            for i in range(4):
                                prep(l, b * 4 + 4 + i, i % 2)
                        tanh(u + 1, (k + 1) % 2)
                        copy_gT(u, k % 2)
                        if l == 0 and k % 2:
                            exps(b * C + (C + (k + 1) // 2), (k + 1) // 2 % 2)
                act.wait_ge(rt_dve, 2 * l + 1)
                if l == 0:
                    nc.scalar.activation(rB[:, 0:NT * EXPERTS[0]], rA[:, 0:NT * EXPERTS[0]], ACT.Tanh, scale=0.5).then_inc(rt_act, 1)
                else:
                    nc.scalar.activation(rB[:, :].rearrange("p (t e) -> p t e", t=NT),
                                         rA[:, :].rearrange("p (t e) -> p t e", t=NT)[:, :, EM:], ACT.Tanh, scale=0.5).then_inc(rt_act, 1)
                    act.wait_ge(rt_dve, 4)
                    nc.scalar.activation(rB[:, :], rB[:, :], ACT.Exp).then_inc(rt_act, 1)
                for k in range(8):
                    u = U[l] + 8 * (B - 1) + k
                    if k < 7:
                        tanh(u + 1, (k + 1) % 2)
                    copy_gT(u, k % 2)
                for s in range(2):
                    copy_xT(l, s, s)
                u0 = U[l] + 2 * NT
                tanh(u0, 0)

                def slot(s, par, up=True, ahead=True, first=False):
                    if up:
                        tanh(s + (u0 + 1), 1 - par)
                    copy_gT(s + u0, par)
                    if ahead:
                        copy_xT(l, s + 2, par)
                    copy_y(l, s, par, first)

                for s in range(2):
                    slot(s, s, first=True)
                if l == 0:
                    with act.Fori(0, NW // 4 - 1) as i:
                        for k in range(4):
                            slot(i * 4 + (2 + k), k % 2)
                            if k % 2:
                                exps(i * 2 + (NW // 2 + 1 + k // 2), (k // 2 + 1) % 2)
                    for k in range(4):
                        slot(2 + NW - 4 + k, k % 2)
                        if k == 1:
                            exps(NW - 1, 1)
                    done = 2 + NW
                else:
                    done = 2
                with act.Fori(done // 2, NS // 2 - 1) as i:
                    for k in range(2):
                        slot(i * 2 + k, k)
                slot(NS - 2, 0, ahead=False)
                slot(NS - 1, 1, up=False, ahead=False)

        @block.vector
        def _(dve):
            done = {"n": 0}

            def link(ins):
                done["n"] += 1
                ins.then_inc(step, 1)
                dve.wait_ge(step, done["at"] + done["n"])

            done["at"] = 0

            def enter(i, per_round):
                done["base"], done["outer"], done["n"] = done["n"], done["at"], 0
                done["at"] = i * per_round + done["base"]

            def leave(rounds, per_round):
                assert done["n"] == per_round, done["n"]
                done["at"], done["n"] = done["outer"], done["base"] + rounds * per_round

            def wkv_den(n, par):
                dec_n = dec[:, :, :, :].rearrange("p l b c -> p (l b c)")[:, ds(n, 1)]
                dve.wait_ge(exp_k, n + 1)
                nc.vector.tensor_scalar(ek[par][:, :], ek[par][:, :], E30, None, ALU.min).then_inc(min_k, 1)
                dve.wait_ge(exp_u, n + 1)
                nc.vector.tensor_scalar(euk[par][:, :], euk[par][:, :], E30, None, ALU.min).then_inc(min_u, 1)
                dve.wait_ge(min_k, n + 1)
                nc.vector.tensor_tensor_scan(fwd[:, :], dec_n.to_broadcast([P, T]), ek[par][:, :], 0.0, ALU.mult, ALU.add)
                link(nc.vector.tensor_tensor_scan(bwd[:, 0:T][:, ::-1], dec_n.to_broadcast([P, T]),
                                                  ek[par][:, ::-1], 0.0, ALU.mult, ALU.add))
                link(nc.vector.scalar_tensor_tensor(fwd[:, :], bwd[:, 1:T + 1], dec_n, fwd[:, :], ALU.mult, ALU.add))
                dve.wait_ge(min_u, n + 1)
                link(nc.vector.tensor_tensor(fwd[:, :], fwd[:, :], euk[par][:, :], ALU.add))
                link(nc.vector.tensor_scalar(fwd[:, :], fwd[:, :], 1e-8, None, ALU.max))
                link(nc.vector.reciprocal(rec[:, :], fwd[:, :]))

            def wkv_num(n, par, q):
                flat = dec[:, :, :, :].rearrange("p l b c -> p (l b c)")
                dec_n, osc_n = flat[:, ds(n, 1)], osc[:, :, :, :].rearrange("p l b c -> p (l b c)")[:, ds(n, 1)]
                dve.wait_ge(kv, n + 1)
                nc.vector.tensor_tensor_scan(fwd[:, :], dec_n.to_broadcast([P, T]), ekv[:, :], 0.0, ALU.mult, ALU.add)
                link(nc.vector.tensor_tensor_scan(bwd[:, 0:T][:, ::-1], dec_n.to_broadcast([P, T]),
                                                  ekv[:, ::-1], 0.0, ALU.mult, ALU.add))
                link(nc.vector.scalar_tensor_tensor(fwd[:, :], bwd[:, 1:T + 1], dec_n, fwd[:, :], ALU.mult, ALU.add))
                dve.wait_ge(ukv, n + 1)
                link(nc.vector.tensor_tensor(fwd[:, :], fwd[:, :], eukv[:, :], ALU.add))
                flat_ratio = ratio[:, :, :, :].rearrange("p b c t -> p (b c t)")
                nc.vector.scalar_tensor_tensor(flat_ratio[:, ds(q * T, T)], fwd[:, :], osc_n, rec[:, :],
                                               ALU.mult, ALU.mult).then_inc(wkv, 1)

            def prep(l, t, b, i, par):
                if l:
                    combine(0, t, par)
                dve.wait_ge(xT_sb, X[l] + 2 * t + 1)
                if l == 0:
                    dve.wait_ge(wkv, b * C + C)
                else:
                    dve.wait_ge(wkv, NW)
                if not (isinstance(t, int) and t < 4):
                    dve.wait_ge(h3_ps, b * 8 + (U[l] - 6 + 2 * i))
                nc.vector.scalar_tensor_tensor(bT[i][:, :, :], tnh[par][:, :].rearrange("p (c t) -> p c t", c=C), 1.0,
                                               ratio[:, ds(b, 1), :, i * P:(i + 1) * P].rearrange("p a c t -> p (a c) t"),
                                               ALU.add, ALU.mult).then_inc(bT_sb, 1)

            def gate(u, par):
                dve.wait_ge(tanh_sb, u + 1)
                link(nc.vector.scalar_tensor_tensor(th[par][:, :], th[par][:, :], 1.0, h1[par][:, 0:F], ALU.add, ALU.mult))
                dve.wait_ge(h3_ps, u + 1)
                nc.vector.scalar_tensor_tensor(g[par][:, 0:F], th[par][:, :], 0.5, h3[par][:, 0:F], ALU.mult, ALU.mult).then_inc(g_sb, 1)

            def add_shared(l, t):
                dve.wait_ge(unit_done, U[l] + 2 * t + 2)
                if l == 0:
                    dve.wait_ge(xacc_in, 16 * B)
                else:
                    dve.wait_ge(xcopied, t + 1)
                acc = xacc[:, ds(t, 1), :].rearrange("p a n -> p (a n)")
                nc.vector.tensor_tensor(acc, acc, Y[:, :], ALU.add).then_inc(y_added, 1)

            def combine(l, t, par):
                acc = xacc[:, ds(t, 1), :].rearrange("p a n -> p (a n)")
                dve.wait_ge(gathered[par], (t - par) * 16 + (32 + 32 * l * (NT // 2)))
                if l == 0:
                    if not (isinstance(t, int) and t < 2):
                        dve.wait_ge(xcopied, t - 1)
                        dve.wait_ge(xT_ps, X[1] + 2 * t - 3)
                    dve.wait_ge(y_added, NT)
                elif t >= 2:
                    dve.wait_ge(out_st[par], 8 * (t - par))
                link(nc.vector.scalar_tensor_tensor(acc, ga[par][:, :], wsel[0][:, ds(t, 1)], acc, ALU.mult, ALU.add))
                nc.vector.scalar_tensor_tensor(xin[par][:, :], gb[par][:, :], wsel[1][:, ds(t, 1)], acc, ALU.mult, ALU.add).then_inc(xnew, 1)

            def route_choose(l):
                E = EXPERTS[l]
                v3 = lambda a: a[:, 0:NT * E].rearrange("p (t e) -> p t e", t=NT)
                wide = lambda a: a[:, :].rearrange("p (t a) -> p t a", a=1).to_broadcast([P, NT, E])
                ie = iota_e[:, :, 0:E]
                dve.wait_ge(logits, NT * (l + 1))
                if l == 0:
                    nc.vector.tensor_copy(rA[:, 0:NT * E], LG[:, 0:NT * E]).then_inc(rt_dve, 1)
                    dve.wait_ge(rt_act, 1)
                    link(nc.vector.tensor_scalar(v3(rB), v3(rB), 0.5, 0.5, ALU.mult, ALU.add))
                    score, weight = rB, rB
                    link(nc.vector.tensor_tensor(v3(rA), v3(rB), biasb[0][:, :, :], ALU.add))
                else:
                    both3 = rA[:, :].rearrange("p (t e) -> p t e", t=NT)
                    nc.vector.tensor_copy(rA[:, :], LG[:, 0:NT * 2 * E]).then_inc(rt_dve, 1)
                    dve.wait_ge(rt_act, 2)
                    link(nc.vector.scalar_tensor_tensor(v3(rB), v3(rB), 1.0, both3[:, :, E:], ALU.add, ALU.mult))
                    link(nc.vector.scalar_tensor_tensor(v3(rB), v3(rB), 0.5, both3[:, :, 0:E], ALU.mult, ALU.mult))
                    link(nc.vector.scalar_tensor_tensor(rB[:, :], rB[:, :], -1.0, rB[:, :], ALU.mult, ALU.max))
                    link(nc.vector.tensor_reduce(m16[0][:, :], v3(rB), AX.X, ALU.max))
                    nc.vector.tensor_tensor(v3(rB), v3(rB), wide(m16[0]), ALU.subtract).then_inc(rt_dve, 2)
                    dve.wait_ge(rt_act, 3)
                    link(nc.vector.tensor_reduce(m16[0][:, :], v3(rB), AX.X, ALU.add))
                    link(nc.vector.reciprocal(m16[1][:, :], m16[0][:, :]))
                    link(nc.vector.tensor_tensor(v3(rB), v3(rB), wide(m16[1]), ALU.mult))
                    link(nc.vector.tensor_tensor(v3(rA), v3(rB), biasb[1][:, :, :], ALU.add))
                    link(nc.vector.tensor_tensor(v3(rC), v3(rB), scaleb[:, :, :], ALU.mult))
                    link(nc.vector.tensor_scalar(rB[:, :], rC[:, :], 1.0, None, ALU.add))
                for j in range(K):
                    link(nc.vector.tensor_reduce(m16[0][:, :], v3(rA), AX.X, ALU.max))
                    link(nc.vector.tensor_tensor(v3(rC), v3(rA), wide(m16[0]), ALU.is_equal))
                    link(nc.vector.tensor_scalar(v3(rC), v3(rC), -float(EM), float(EM), ALU.mult, ALU.add))
                    link(nc.vector.tensor_tensor(v3(rC), v3(rC), ie, ALU.add))
                    link(nc.vector.tensor_reduce(m16[1][:, :], v3(rC), AX.X, ALU.min))
                    link(nc.vector.tensor_tensor(v3(oh[j]), ie, wide(m16[1]), ALU.is_equal))
                    if j + 1 < K:
                        link(nc.vector.scalar_tensor_tensor(v3(rA), v3(oh[j]), -3e38, v3(rA), ALU.mult, ALU.add))
                    link(nc.vector.tensor_tensor(v3(rC), v3(oh[j]), v3(rB), ALU.mult))
                    link(nc.vector.tensor_reduce(wsel[j][:, :], v3(rC), AX.X, ALU.add))
                if l == 0:
                    link(nc.vector.tensor_tensor(m16[0][:, :], wsel[0][:, :], wsel[1][:, :], ALU.add))
                    link(nc.vector.tensor_scalar(m16[0][:, :], m16[0][:, :], 1e-12, None, ALU.max))
                    link(nc.vector.reciprocal(m16[1][:, :], m16[0][:, :]))
                    nc.vector.tensor_tensor(wsel[0][:, :], wsel[0][:, :], m16[1][:, :], ALU.mult)
                    link(nc.vector.tensor_tensor(wsel[1][:, :], wsel[1][:, :], m16[1][:, :], ALU.mult))
                nc.vector.tensor_tensor(v3(both), v3(oh[0]), v3(oh[1]), ALU.add).then_inc(rt_dve, 1)

            def route_place(l):
                E, NS = EXPERTS[l], SLOTS[l]
                te = lambda a: a[:, 0:NT * E].rearrange("p (t e) -> p t e", t=NT)
                et = lambda a: a[:, 0:NT * E].rearrange("p (e t) -> p e t", e=E)
                swap = lambda a: a[:, 0:NT * E].rearrange("p (e t) -> p t e", e=E)
                dve.wait_ge(rt_pe, l + 1)
                link(nc.vector.tensor_copy(et(rA), LG[:, 256:256 + NT * E].rearrange("p (t e) -> p e t", t=NT)))
                link(nc.vector.tensor_tensor_scan(rC[:, 0:NT * E], seg[:, :, :].rearrange("p e t -> p (e t)")[:, 0:NT * E],
                                                  rA[:, 0:NT * E], 0.0, ALU.mult, ALU.add))
                link(nc.vector.tensor_copy(cnt[0][:, 0:E], et(rC)[:, :, NT - 1]))
                link(nc.vector.tensor_tensor(et(rB), cnt[0][:, 0:E].rearrange("p (e a) -> p e a", a=1).to_broadcast([P, E, NT]),
                                             rows_j[:, 0:E, :], ALU.is_gt))
                link(nc.vector.tensor_reduce(cnt[1][:, 0:E], et(rB), AX.X, ALU.add))
                link(nc.vector.tensor_tensor_scan(cnt[2][:, 0:E], ones[:, 0:E], cnt[1][:, 0:E], 0.0, ALU.mult, ALU.add))
                rs = rD[:, 0:NS * E].rearrange("p (s e) -> p s e", s=NS)
                link(nc.vector.tensor_tensor(rs, iota_s[:, 0:NS, 0:E],
                                             cnt[2][:, 0:E].rearrange("p (a e) -> p a e", a=1).to_broadcast([P, NS, E]), ALU.is_ge))
                link(nc.vector.tensor_reduce(rB[:, 0:NS], rs, AX.X, ALU.add))
                nc.vector.tensor_scalar(expert_of[:, 0:NS], rB[:, 0:NS], float(E - 1), None, ALU.min)
                link(nc.vector.tensor_tensor(cnt[1][:, 0:E], cnt[2][:, 0:E], cnt[1][:, 0:E], ALU.subtract))
                link(nc.vector.tensor_tensor(et(rC), et(rC), et(rA), ALU.subtract))
                link(nc.vector.tensor_tensor(te(rB), swap(rC), LG[:, 0:NT * E].rearrange("p (t e) -> p t e", t=NT), ALU.add))
                link(nc.vector.scalar_tensor_tensor(te(rB), cnt[1][:, 0:E].rearrange("p (a e) -> p a e", a=1).to_broadcast([P, NT, E]),
                                                    float(P), te(rB), ALU.mult, ALU.add))
                for j in range(K):
                    link(nc.vector.tensor_tensor(te(rC), te(oh[j]), te(rB), ALU.mult))
                    ins = nc.vector.tensor_reduce(m16[j][:, :], te(rC), AX.X, ALU.add)
                    link(ins)
                    last = nc.vector.tensor_copy(pos[j][:, :], m16[j][:, :])
                last.then_inc(routed, 1)

            nc.vector.memset(bwd[:, T:T + 1], 0.0)
            for i in range(2):
                nc.vector.memset(g[i][:, F:FC * P], 0.0)
            dve.wait_ge(wkv_p_in, 48)
            link(nc.vector.tensor_reduce(tf[:, :], condb[:, :, :], AX.X, ALU.add))
            dve.wait_ge(astep, 3)
            link(nc.vector.tensor_scalar(tf[:, :], tf[:, :], 0.5, 0.5, ALU.mult, ALU.add))
            nc.vector.tensor_scalar(dfac[:, :], tf[:, :], 0.5, 0.5, ALU.mult, ALU.add)
            link(nc.vector.tensor_scalar(sfac[:, :], tf[:, :], 0.1, 0.4, ALU.mult, ALU.add))
            over_c = lambda a: a[:, :].rearrange("p (b a) -> p b a", a=1).to_broadcast([P, B, C])
            for l in range(LAYERS):
                nc.vector.tensor_tensor(dec[:, l, :, :], over_c(dfac),
                                        wl[:, l, :].rearrange("p (a c) -> p a c", a=1).to_broadcast([P, B, C]), ALU.mult)
                last = nc.vector.tensor_copy(osc[:, l, :, :], over_c(sfac))
            link(last)
            dve.wait_ge(consts, 9)
            nc.vector.tensor_scalar(seg[:, :, :], seg[:, :, :], 1.0, None, ALU.min)
            for c in range(C):
                wkv_den(c, c % 2)
                wkv_num(c, c % 2, c)
            for l in range(LAYERS):
                NS = SLOTS[l]
                if l == 0:
                    dve.wait_ge(params_in, 80)
                else:
                    dve.wait_ge(wkv, NW)
                for t in range(4):
                    prep(l, t, 0, t, t % 2)
                gate(U[l], 0)
                per = 8 * 1 + (4 * 8 if l == 0 else 4)
                with dve.Fori(0, B - 1) as b:
                    enter(b, per)
                    for k in range(8):
                        u = b * 8 + (U[l] + k)
                        if k == 7:
                            for i in range(4):
                                prep(l, b * 4 + 4 + i, b + 1, i, i % 2)
                        gate(u + 1, (k + 1) % 2)
                        if k % 2:
                            add_shared(l, b * 4 + k // 2)
                        if l == 0:
                            for piece in ((0, 1), (2,), (3, 4), (5,), (6, 7), (), (), ())[k]:
                                c = piece // 2
                                if piece % 2 == 0:
                                    wkv_den(b * C + (C + c), c % 2)
                                else:
                                    wkv_num(b * C + (C + c), c % 2, b * C + (C + c))
                leave(B - 1, per)
                route_choose(l)
                for k in range(8):
                    if k == 1:
                        route_place(l)
                    u = U[l] + 8 * (B - 1) + k
                    if k < 7:
                        gate(u + 1, (k + 1) % 2)
                    if k % 2:
                        add_shared(l, 4 * (B - 1) + k // 2)
                u0 = U[l] + 2 * NT
                gate(u0, 0)

                def slot(s, par):
                    gate(s + (u0 + 1), 1 - par)

                for s in range(2):
                    slot(s, s)
                if l == 0:
                    per = 4 + 16
                    with dve.Fori(0, NW // 4 - 1) as i:
                        enter(i, per)
                        for k in range(4):
                            slot(i * 4 + (2 + k), k % 2)
                            n = i * 2 + (NW // 2 + k // 2)
                            if k % 2 == 0:
                                wkv_den(n, k // 2)
                            else:
                                wkv_num(n, k // 2, i * 2 + k // 2)
                    leave(NW // 4 - 1, per)
                    for k in range(4):
                        slot(2 + NW - 4 + k, k % 2)
                        n = NW - 2 + k // 2
                        if k % 2 == 0:
                            wkv_den(n, k // 2)
                        else:
                            wkv_num(n, k // 2, n - NW // 2)
                    first = 2 + NW
                else:
                    first = 2
                rounds = NS // 2 - 1 - first // 2
                with dve.Fori(0, rounds) as i:
                    enter(i, 2)
                    for k in range(2):
                        slot(i * 2 + (first + k), k)
                leave(rounds, 2)
                slot(NS - 2, 0)
            for t in range(NT):
                combine(1, t, t % 2)

        @block.tensor
        def _(pe):
            def xtr(l, t, par):
                if l == 0:
                    pe.wait_ge(x_in[par], (t - par) * 8 + 16)
                else:
                    pe.wait_ge(xnew, t + 1)
                if not (isinstance(t, int) and l == 0 and t == 0):
                    pe.wait_ge(xT_sb, X[l] + 2 * t)
                for c in range(C):
                    last = nc.tensor.transpose(XT[:, c * P:(c + 1) * P], xin[par][:, c * P:(c + 1) * P], ident[:, :])
                last.then_inc(xT_ps, 1)

            def finish(l, t, i):
                n = EXPERTS[0] if l == 0 else 2 * EXPERTS[1]
                pe.wait_ge(bT_sb, NT * l + t + 1)
                for c in range(C):
                    last = nc.tensor.matmul(LG[:, ds(t * n, n)], bT[i][:, c, :], gw[l][:, c, :], start=(c == 0), stop=(c == C - 1))
                last.then_inc(logits, 1)
                pe.wait_ge(xT_sb, X[l] + 2 * t + 1)
                for c in range(C):
                    last = nc.tensor.transpose(XT[:, c * P:(c + 1) * P], bT[i][:, c, :], ident[:, :])
                last.then_inc(xT_ps, 1)

            def prep(l, t, i):
                xtr(l, t, i % 2)
                finish(l, t, i)

            def up(u, par, lhs):
                if not (isinstance(u, int) and u < 2):
                    pe.wait_ge(g_sb, u - 1)
                for ps_, off, s in ((h1, 0, h1_ps), (h3, F, h3_ps)):
                    for c in range(C):
                        last = nc.tensor.matmul(ps_[par][:, 0:F], lhs[:, c, :],
                                                wbuf[par][:, c * 2 * F + off:c * 2 * F + off + F], start=(c == 0), stop=(c == C - 1))
                    last.then_inc(s, 1)

            def transpose_g(u, par):
                pe.wait_ge(g_sb, u + 1)
                if not (isinstance(u, int) and u == 0):
                    pe.wait_ge(gT_sb, u)
                for j in range(FC):
                    last = nc.tensor.transpose(GT[:, j * P:(j + 1) * P], g[par][:, j * P:(j + 1) * P], ident[:, :])
                last.then_inc(gT_ps, 1)

            def down(u, par, first, last_of):
                pe.wait_ge(gT_sb, u + 1)
                for j in range(FC):
                    last = nc.tensor.matmul(Y[:, :], gT[:, j, :], wbuf[par][:, UP + j * D:UP + (j + 1) * D],
                                            start=(first and j == 0), stop=(last_of and j == FC - 1))
                last.then_inc(unit_done, 1)

            def transpose_slot(l, s, par):
                pe.wait_ge(xs_in[par], 8 * (s - par) + 16 + 16 * (l * SLOTS[0] // 2))
                pe.wait_ge(xT_sb, s + (X[l] + 2 * NT))
                for c in range(C):
                    last = nc.tensor.transpose(XT[:, c * P:(c + 1) * P], xs[par][:, c * P:(c + 1) * P], ident[:, :])
                last.then_inc(xT_ps, 1)

            pe.wait_ge(consts, 9)
            pe.wait_ge(params_in, 80)
            for l in range(LAYERS):
                NS = SLOTS[l]
                if l:
                    pe.wait_ge(rt_dve, 1)
                for t in range(4):
                    prep(l, t, t)
                for par in range(2):
                    pe.wait_ge(w_in[par], 16 * (WL[l] + 1))
                up(U[l], 0, bT[0])

                def y_free(l, t):
                    if isinstance(t, int) and t == 0:
                        if l:
                            pe.wait_ge(y_copied, SLOTS[0])
                    else:
                        pe.wait_ge(y_added, t + NT * l)

                def shared(b, k, nxt):
                    u = b * 8 + (U[l] + k)
                    if nxt:
                        up(u + 1, (k + 1) % 2, bT[(k + 1) // 2 % 4])
                    transpose_g(u, k % 2)
                    if k % 2 == 0:
                        if isinstance(b, int) or k:
                            y_free(l, b * 4 + k // 2)
                        elif l:
                            pe.wait_ge(y_copied, SLOTS[0])
                            pe.wait_ge(y_added, b * 4 + NT)
                        else:
                            pe.wait_ge(y_added, b * 4)
                    down(u, k % 2, k % 2 == 0, k % 2 == 1)

                with pe.Fori(0, B - 1) as b:
                    for k in range(8):
                        if k == 7:
                            for i in range(4):
                                prep(l, b * 4 + 4 + i, i)
                        shared(b, k, True)
                pe.wait_ge(rt_dve, 2 if l == 0 else 6)
                n = NT * EXPERTS[l]
                nc.tensor.matmul(LG[:, 0:n], before[:, :], both[:, 0:n], start=True, stop=True)
                nc.tensor.matmul(LG[:, 256:256 + n], ones[:, :], both[:, 0:n], start=True, stop=True).then_inc(rt_pe, 1)
                for k in range(8):
                    shared(B - 1, k, k < 7)

                for s in range(2):
                    transpose_slot(l, s, s)
                u0 = U[l] + 2 * NT

                def slot_up(s, par):
                    pe.wait_ge(w_in[par], 8 * (s - par) + 16 * (WL[l] + 2))
                    pe.wait_ge(xT_sb, s + (X[l] + 2 * NT + 1))
                    up(s + u0, par, xT[par])

                def slot(s, par, ahead_up=True, ahead_x=True, first=False):
                    if ahead_up:
                        slot_up(s + 1, 1 - par)
                    transpose_g(s + u0, par)
                    if ahead_x:
                        transpose_slot(l, s + 2, par)
                    if first:
                        pe.wait_ge(y_added, NT * (l + 1))
                    else:
                        pe.wait_ge(y_copied, s + SLOTS[0] * l)
                    down(s + u0, par, True, True)

                slot_up(0, 0)
                slot(0, 0, first=True)
                slot(1, 1)
                with pe.Fori(1, NS // 2 - 1) as i:
                    for k in range(2):
                        slot(i * 2 + k, k)
                slot(NS - 2, 0, ahead_x=False)
                slot(NS - 1, 1, ahead_up=False, ahead_x=False)


def pack_experts(up, gate, down):
    e = up.shape[0]
    both = np.concatenate([gate, up], axis=2).reshape(e, C, P, 2 * F).transpose(0, 2, 1, 3).reshape(e, P, UP)
    padded = np.zeros((e, FC * P, D), np.float32)
    padded[:, :F] = down
    low = padded.reshape(e, FC, P, D).transpose(0, 2, 1, 3).reshape(e, P, FC * D)
    return np.ascontiguousarray(np.concatenate([both, low], axis=2))


def kernel(x, fside_BxSxS_0, cond_512, L0_cond_w, L0_cond_u, L0_ffn_gate_w, L0_ffn_router_bias, L0_ffn_W1,
           L0_ffn_W3, L0_ffn_W2, L0_ffn_sw1, L0_ffn_sw3, L0_ffn_sw2, L1_cond_w, L1_cond_u, L1_ffn_gate_w,
           L1_ffn_cls_w, L1_ffn_extra_scale, L1_ffn_extra_bias, L1_ffn_wg, L1_ffn_wu, L1_ffn_wd, L1_ffn_sg,
           L1_ffn_su, L1_ffn_sd):
    import concourse.bacc as bacc
    from concourse.bass_utils import run_bass_kernel_spmd

    a = lambda v: np.asarray(v)
    chan = lambda v: a(v).reshape(C, P).T
    rep = lambda v, n: np.ascontiguousarray(np.broadcast_to(np.tile(a(v), n), (P, n * a(v).size)))
    halves = lambda w: a(w).reshape(2, F, D)
    gate_cols = lambda w: a(w).T.reshape(C, P, -1).transpose(1, 0, 2).reshape(P, -1)
    k = a(fside_BxSxS_0).transpose(0, 2, 1).reshape(B * C, P, T)
    ins = {
        "x": a(x).reshape(N, D),
        "kt": np.ascontiguousarray(np.concatenate([k] * LAYERS)),
        "cond": rep(a(cond_512).reshape(-1), 1),
        "wdec": np.ascontiguousarray(np.concatenate([chan(L0_cond_w), chan(L1_cond_w)], axis=1)),
        "ub": np.ascontiguousarray(np.concatenate([chan(L0_cond_u)] * B + [chan(L1_cond_u)] * B, axis=1)),
        "gates0": np.ascontiguousarray(gate_cols(L0_ffn_gate_w)),
        "gates1": np.ascontiguousarray(gate_cols(np.concatenate([a(L1_ffn_cls_w), a(L1_ffn_gate_w)]))),
        "bias0": rep(L0_ffn_router_bias, NT),
        "bias1": rep(L1_ffn_extra_bias, NT),
        "scale1": rep(L1_ffn_extra_scale, NT),
        "wts0": pack_experts(
            np.concatenate([a(L0_ffn_W3), halves(L0_ffn_sw3).transpose(0, 2, 1)]),
            np.concatenate([a(L0_ffn_W1), halves(L0_ffn_sw1).transpose(0, 2, 1)]),
            np.concatenate([a(L0_ffn_W2), a(L0_ffn_sw2).T.reshape(2, F, D)])),
        "wts1": pack_experts(
            np.concatenate([a(L1_ffn_wu), halves(L1_ffn_su)]).transpose(0, 2, 1),
            np.concatenate([a(L1_ffn_wg), halves(L1_ffn_sg)]).transpose(0, 2, 1),
            np.concatenate([a(L1_ffn_wd).transpose(0, 2, 1), a(L1_ffn_sd).T.reshape(2, F, D)])),
    }
    nc = bacc.Bacc("TRN2", target_bir_lowering=False, num_devices=1)
    ap = {n: nc.dram_tensor(f"in_{n}", v.shape, mybir.dt.float32, kind="ExternalInput").ap() for n, v in ins.items()}
    out = nc.dram_tensor("out_x", (N, D), mybir.dt.float32, kind="ExternalOutput").ap()
    build(nc, ap["x"], ap["kt"], ap["cond"], ap["wdec"], ap["ub"], (ap["gates0"], ap["gates1"]),
          (ap["bias0"], ap["bias1"]), ap["scale1"], (ap["wts0"], ap["wts1"]), out)
    r = run_bass_kernel_spmd(nc, [{f"in_{n}": v for n, v in ins.items()}], core_ids=[0])
    return r.results[0]["out_x"].reshape(B, T, D)
```

```python
from contextlib import ExitStack

import numpy as np
import concourse.bass as bass
from concourse import mybir

P = 128
B, T, D = 4, 512, 512
N = B * T
NT = N // P
C = D // P
F = 352
FC = -(-F // P)
EXPERTS = (8, 14)
K = 2
SLOTS = tuple(N * K // P + e for e in EXPERTS)
UP = C * 2 * F
WC = UP + FC * D
NP = 4
PIECE = -(-WC // NP)
PIECES = tuple((p * PIECE, min(WC, (p + 1) * PIECE)) for p in range(NP))
UPP = -(-UP // PIECE)
EM, SM = max(EXPERTS), max(SLOTS)
LAYERS = len(EXPERTS)
NW = LAYERS * B * C
E30 = float(np.float32(np.exp(np.float32(30.0))))


def build(nc, x, kt, cond, wdec, ub, gates, bias, scale1, wts, out):
    f32, i32, f32r = mybir.dt.float32, mybir.dt.int32, mybir.dt.float32r
    ALU, ACT, AX = mybir.AluOpType, mybir.ActivationFunctionType, mybir.AxisListType
    ds = bass.ds
    ctx = ExitStack()
    with ctx:
        def sb(name, shape, dt=f32):
            return ctx.enter_context(nc.sbuf_tensor(name, shape, dt))

        def ps(name):
            return ctx.enter_context(nc.psum_tensor(name, [P, 512], f32))

        def sem(name):
            return ctx.enter_context(nc.semaphore(name))

        slot_x = nc.dram_tensor("slot_x", [SM * P, D], f32, kind="Internal").ap()
        slot_y = [nc.dram_tensor(f"slot_y{l}", [SLOTS[l] * P, D], f32, kind="Internal").ap() for l in range(LAYERS)]
        base_d = nc.dram_tensor("base_d", [N, D], f32, kind="Internal").ap()

        xacc = sb("xacc", [P, NT, D])
        ratio = sb("ratio", [P, B, C, T])
        raw = sb("raw", [P, WC])
        w_hi = sb("w_hi", [P, 2 * WC], f32r)
        w_lo = sb("w_lo", [P, 2 * WC], f32r)
        ident = sb("ident", [P, P])
        before = sb("before", [P, P])
        ones = sb("ones", [P, P])
        xin = [sb(f"xin{i}", [P, D]) for i in range(2)]
        bTs = sb("bTs", [P, 4 * D])
        bT = [bTs[:, i * D:(i + 1) * D] for i in range(4)]
        xs = bT
        xTh = [sb(f"xTh{i}", [P, C * P], f32r) for i in range(2)]
        xTl = [sb(f"xTl{i}", [P, C * P], f32r) for i in range(2)]
        g = [sb(f"g{i}", [P, FC * P]) for i in range(2)]
        gTh = sb("gTh", [P, FC * P], f32r)
        gTl = sb("gTl", [P, FC * P], f32r)
        yb = [sb(f"yb{i}", [P, D]) for i in range(2)]
        btok = yb
        kb = [sb(f"kb{i}", [P, T]) for i in range(2)]
        ek = [sb(f"ek{i}", [P, T]) for i in range(2)]
        euk = [sb(f"euk{i}", [P, T]) for i in range(2)]
        ekv, eukv = sb("ekv", [P, T]), sb("eukv", [P, T])
        fwd = sb("fwd", [P, T])
        bwd = sb("bwd", [P, T + 1])
        rec = sb("rec", [P, T])
        ga, gb = ek, euk
        condb = ekv[:, :].rearrange("p (b n) -> p b n", b=B)
        wl = sb("wl", [P, LAYERS, C])
        ul = sb("ul", [P, NW])
        dec = sb("dec", [P, LAYERS, B, C])
        osc = sb("osc", [P, LAYERS, B, C])
        tf = sb("tf", [P, B])
        dfac, sfac = sb("dfac", [P, B]), sb("sfac", [P, B])
        gw = [sb("gw0", [P, C, EXPERTS[0]]), sb("gw1", [P, C, 2 * EXPERTS[1]])]
        biasb = [sb(f"biasb{l}", [P, EXPERTS[l]]) for l in range(LAYERS)]
        scaleb = sb("scaleb", [P, EXPERTS[1]])
        iota_e = sb("iota_e", [P, EM])
        rows_j = sb("rows_j", [P, NT])
        iota_s = sb("iota_s", [P, SM])
        seg = sb("seg", [P, EM, NT])
        rA, rB, rC, rD = xin[0], fwd, rec, bTs
        oh = [ekv, eukv]
        both = bwd
        m16 = [sb(f"m16{i}", [P, NT]) for i in range(3)]
        cnt = [sb(f"cnt{i}", [P, EM]) for i in range(4)]
        wsel = [sb(f"wsel{i}", [P, NT]) for i in range(2)]
        pos = [sb(f"pos{i}", [P, NT], i32) for i in range(2)]
        CHANGED, ORD, UPWAIT, DOWNWAIT, BUF, OTHER = range(6)
        tab = sb("tab", [P, 6, SM], i32)
        tabf = xin[1][:, 0:6 * SM].rearrange("p (r s) -> p r s", r=6)
        chosen = sb("chosen", [P, EM + 2], i32)

        h1 = [ps(f"h1_{i}") for i in range(2)]
        h3 = [ps(f"h3_{i}") for i in range(2)]
        XT, GT, Y, LG = ps("XT"), ps("GT"), ps("Y"), ps("LG")

        params_in = sem("params_in")
        wkv_p_in = sem("wkv_p_in")
        xacc_in = sem("xacc_in")
        consts = sem("consts")
        zeroed = sem("zeroed")
        x_in = [sem(f"x_in{i}") for i in range(2)]
        sh_in = [sem(f"sh_in{p}") for p in range(NP)]
        sh_hi, sh_lo = sem("sh_hi"), sem("sh_lo")
        dw_in = [sem(f"dw_in{p}") for p in range(NP)]
        dw_hi, dw_lo = sem("dw_hi"), sem("dw_lo")
        ex_in = [[sem(f"ex_in{l}_{p}") for p in range(NP)] for l in range(LAYERS)]
        ex_hi = [sem(f"ex_hi{l}") for l in range(LAYERS)]
        ex_lo = [sem(f"ex_lo{l}") for l in range(LAYERS)]
        raw_free = sem("raw_free")
        xs_in = [sem(f"xs_in{i}") for i in range(2)]
        y_out = [sem(f"y_out{i}") for i in range(2)]
        k_in = [sem(f"k_in{i}") for i in range(2)]
        base_out = [sem(f"base_out{i}") for i in range(2)]
        d_in = [sem(f"d_in{i}") for i in range(2)]
        scattered = [sem(f"scattered{i}") for i in range(2)]
        gathered = [sem(f"gathered{i}") for i in range(2)]
        out_st = [sem(f"out_st{i}") for i in range(2)]
        h1_ps, h3_ps = sem("h1_ps"), sem("h3_ps")
        tanh_sb = sem("tanh_sb")
        g_sb = sem("g_sb")
        gT_ps = sem("gT_ps")
        gT_hi, gT_lo = sem("gT_hi"), sem("gT_lo")
        unit_done = sem("unit_done")
        y_added = sem("y_added")
        y_copied = sem("y_copied")
        xT_ps, xT_sb = sem("xT_ps"), sem("xT_sb")
        x_hi, x_lo = sem("x_hi"), sem("x_lo")
        bT_sb = sem("bT_sb")
        logits = sem("logits")
        xnew = sem("xnew")
        xcopied = sem("xcopied")
        exp_k, exp_u = sem("exp_k"), sem("exp_u")
        min_k, min_u = sem("min_k"), sem("min_u")
        kv, ukv = sem("kv"), sem("ukv")
        wkv = sem("wkv")
        step = sem("step")
        astep = sem("astep")
        rt_dve, rt_act, rt_pe = sem("rt_dve"), sem("rt_act"), sem("rt_pe")
        routed = sem("routed")
        act_on, pool_on, pe_on = sem("act_on"), sem("pool_on"), sem("pe_on")

        U = [0, 2 * NT + SLOTS[0]]
        X = [0, 2 * NT + SLOTS[0]]
        V = [0, NT + SLOTS[0]]

        PARTS = {0: (("fin", 1),), 1: (("x", 0),), 2: (("fin", 2),), 3: (("x", 1),), 4: (("fin", 3),),
                 5: (("x", 2),), 7: (("fin", 4), ("x", 3))}
        LAST = {0: (("fin", 1), ("fin", 2), ("fin", 3))}
        AHEAD = 5

        def parts(b, k):
            table = LAST if isinstance(b, int) and b == B - 1 else PARTS
            before_k = sum(len(table.get(i, ())) for i in range(k))
            return [(kind, j, b * 8 + (AHEAD + before_k + n)) for n, (kind, j) in enumerate(table.get(k, ()))]

        block = ctx.enter_context(nc.Block())

        @block.sync
        def _(sp):
            def load_x(t, par):
                sp.dma_start(xin[par][:, :], x[ds(t * P, P), :]).then_inc(x_in[par], 16)

            def load_w(l, e, p):
                lo, hi = PIECES[p]
                sp.dma_start(raw[:, lo:hi], wts[l][ds(e, 1), :, lo:hi].rearrange("e p n -> (e p) n")).then_inc(dw_in[p], 16)

            def load_slot(l, s, par):
                sp.dma_start(xs[par], slot_x[ds(s * P, P), :]).then_inc(xs_in[par], 16)

            def store_y(l, s, par):
                sp.wait_ge(y_copied, (SLOTS[0] if l else 0) + s + 1)
                sp.dma_start(slot_y[l][ds(s * P, P), :], yb[par][:, :]).then_inc(y_out[par], 16)

            def part(l, kind, t, j, q):
                if kind == "fin":
                    sp.wait_ge(xT_sb, q + (2 * NT * l + 1))
                    sp.dma_start(base_d[ds(t * P, P), :], btok[j % 2][:, :]).then_inc(base_out[j % 2], 16)
                elif l == 0 and not (isinstance(t, int) and t + 2 >= NT):
                    sp.wait_ge(xT_sb, q + 1)
                    load_x(t + 2, j % 2)

            def batch(l, b):
                for k in range(8):
                    for kind, j, q in parts(b, k):
                        part(l, kind, b * 4 + (j if kind == "fin" else 4 + j), j, q)

            def load_base(l, t, par):
                sp.dma_start(yb[par][:, :], base_d[ds(t * P, P), :]).then_inc(d_in[par], 16)

            for l in range(LAYERS):
                E, NS = EXPERTS[l], SLOTS[l]
                if l == 0:
                    for par in range(2):
                        sp.sem_inc(base_out[par], 16)
                    sp.dma_start(condb, cond.rearrange("p (b n) -> p b n", b=B)).then_inc(wkv_p_in, 16)
                    sp.dma_start(wl[:, :, :], wdec.rearrange("p (l c) -> p l c", l=LAYERS)).then_inc(wkv_p_in, 16)
                    sp.dma_start(ul[:, :], ub).then_inc(wkv_p_in, 16)
                    for t in range(2):
                        load_x(t, t)
                    for i in range(2):
                        sp.dma_start(gw[i][:, :, :], gates[i].rearrange("p (c e) -> p c e", c=C)).then_inc(params_in, 16)
                        sp.dma_start(biasb[i][:, :], bias[i]).then_inc(params_in, 16)
                    sp.dma_start(scaleb[:, :], scale1).then_inc(params_in, 16)
                    for b in range(B):
                        sp.dma_start(xacc[:, 4 * b:4 * b + 4, :],
                                     x[b * T:(b + 1) * T, :].rearrange("(t p) n -> p t n", p=P)).then_inc(xacc_in, 16)
                else:
                    sp.wait_ge(raw_free, NP)
                    for p in range(NP):
                        load_w(l, E, p)
                    for p in range(NP):
                        sp.wait_ge(dw_lo, NP + p + 1)
                        load_w(l, E + 1, p)
                for t in range(4):
                    part(l, "x", t, t, t)
                part(l, "fin", 0, 0, 4)
                with sp.Fori(0, B - 2) as b:
                    batch(l, b)
                batch(l, B - 2)
                batch(l, B - 1)
                for par in range(2):
                    sp.wait_ge(base_out[par], 16 * (NT // 2) * (l + 1) + 16)
                for t in range(2):
                    load_base(l, t, t)
                sp.wait_ge(routed, l + 1)
                first = sp.value_load(chosen[0:1, 0:1], min_val=0, max_val=E - 1)
                if l == 0:
                    sp.wait_ge(sh_lo, 2 * NP)
                else:
                    sp.wait_ge(dw_lo, 3 * NP)
                for p in range(NP):
                    load_w(l, first, p)
                for t in range(2, NT):
                    sp.wait_ge(scattered[t % 2], 16 * K * (l * (NT // 2) + t // 2))
                    load_base(l, t, t % 2)
                for par in range(2):
                    sp.wait_ge(scattered[par], 16 * K * (NT // 2) * (l + 1))
                for s in range(2):
                    load_slot(l, s, s)
                with sp.Fori(0, NS // 2 - 1) as i:
                    for par in range(2):
                        s = 2 * i + par
                        sp.wait_ge(xT_ps, s + (X[l] + 2 * NT + 1))
                        load_slot(l, s + 2, par)
                        store_y(l, s, par)
                for par in range(2):
                    store_y(l, NS - 2 + par, par)
            with sp.Fori(0, NT // 2) as i:
                for par in range(2):
                    t = 2 * i + par
                    sp.wait_ge(xnew, NT + t + 1)
                    sp.dma_start(out[ds(t * P, P), :], xin[par][:, :]).then_inc(out_st[par], 16)
            for par in range(2):
                sp.wait_ge(out_st[par], 16 * (NT // 2))

        @block.gpsimd
        def _(pool):
            nc.gpsimd.memset(ones[:, :], 1.0).then_inc(consts, 1)
            nc.gpsimd.memset(ident[:, :], 0.0).then_inc(consts, 1)
            zeros = xTh[1][:, :].bitcast(f32)
            nc.gpsimd.memset(zeros, 0.0).then_inc(consts, 1)
            for n in range(2):
                pool.dma_start(kb[n][:, :], kt[n, :, :]).then_inc(k_in[n], 16)

            def load_w(l, e, p, loaded):
                lo, hi = PIECES[p]
                pool.dma_start(raw[:, lo:hi], wts[l][ds(e, 1), :, lo:hi].rearrange("e p n -> (e p) n")).then_inc(loaded[p], 16)

            for p in range(NP):
                load_w(0, EXPERTS[0], p, sh_in)
            pool.wait_ge(consts, 3)
            pool.dma_start(slot_x.rearrange("(s p) n -> p s n", p=P),
                           zeros.rearrange("p (s n) -> p s n", s=1).to_broadcast([P, SM, D])).then_inc(zeroed, 16)
            nc.gpsimd.affine_select(out=ident[:, :], in_=ident[:, :], compare_op=ALU.not_equal, fill=1.0, base=0,
                                    pattern=[[-1, P]], channel_multiplier=1).then_inc(consts, 1)
            nc.gpsimd.affine_select(out=before[:, :], in_=ones[:, :], compare_op=ALU.is_gt, fill=0.0, base=0,
                                    pattern=[[1, P]], channel_multiplier=-1).then_inc(consts, 1)

            def iota(dst, pattern, base=0):
                nc.gpsimd.iota(dst, pattern, base=base, channel_multiplier=0,
                               allow_small_or_imprecise_dtypes=True).then_inc(consts, 1)
            iota(iota_e[:, :], [[1, EM]])
            iota(rows_j[:, :], [[P, NT]])
            iota(iota_s[:, :], [[1, SM]], 1)
            iota(seg[:, :, :], [[0, EM], [1, NT]])

            def products(n, par, load=True):
                pool.wait_ge(min_k, n + 1)
                if not (isinstance(n, int) and n == 0):
                    pool.wait_ge(wkv, n)
                nc.gpsimd.tensor_tensor(ekv[:, :], ek[par][:, :], kb[par][:, :], ALU.mult).then_inc(kv, 1)
                pool.wait_ge(min_u, n + 1)
                nc.gpsimd.tensor_tensor(eukv[:, :], euk[par][:, :], kb[par][:, :], ALU.mult).then_inc(ukv, 1)
                if load:
                    pool.wait_ge(ukv, n + 1)
                    pool.wait_ge(kv, n + 1)
                    pool.dma_start(kb[par][:, :], kt[ds(n + 2, 1), :, :].rearrange("n p t -> (n p) t")).then_inc(k_in[par], 16)

            def shared_lo(m):
                p, (lo, hi) = m % NP, PIECES[m % NP]
                at = m // NP * WC
                pool.wait_ge(sh_hi, m + 1)
                nc.gpsimd.tensor_tensor(w_lo[:, at + lo:at + hi], raw[:, lo:hi],
                                        w_hi[:, at + lo:at + hi].bitcast(f32), ALU.subtract).then_inc(sh_lo, 1)
                if m < NP:
                    pool.wait_ge(sh_lo, m + 1)
                    load_w(0, EXPERTS[0] + 1, p, sh_in)

            def split(l, s, pieces):
                changed = pool.value_load(tab[0:1, CHANGED, ds(s, 1)], min_val=0, max_val=1)
                with pool.If(changed > 0):
                    o = pool.value_load(tab[0:1, ORD, ds(s, 1)], min_val=0, max_val=EM - 1)
                    at = pool.value_load(tab[0:1, OTHER, ds(s, 1)], min_val=0, max_val=WC)
                    e = pool.value_load(chosen[0:1, ds(o + 2, 1)], min_val=0, max_val=EXPERTS[l] - 1)
                    for p in pieces:
                        lo, hi = PIECES[p]
                        pool.wait_ge(ex_hi[l], o * NP + (p + 1))
                        pool.sem_inc(pool_on, 1)
                        nc.gpsimd.tensor_tensor(w_lo[:, ds(at + lo, hi - lo)], raw[:, lo:hi],
                                                w_hi[:, ds(at + lo, hi - lo)].bitcast(f32), ALU.subtract).then_inc(ex_lo[l], 1)
                    for p in pieces:
                        pool.wait_ge(ex_lo[l], o * NP + (p + 2))
                        pool.sem_inc(pool_on, 1)
                        load_w(l, e, p, ex_in[l])

            def scatter(l, t, par):
                pool.wait_ge(d_in[par], 16 * (l * (NT // 2) + t // 2 + 1))
                for j in range(K):
                    nc.gpsimd.indirect_dma_start(slot_x[:, :], bass.IndirectOffsetOnAxis(ap=pos[j][:, t:t + 1], axis=0),
                                                 yb[par][:, :], None).then_inc(scattered[par], 16)

            def gather(l, t, par):
                if t >= 2:
                    pool.wait_ge(xnew, NT * l + t - 1)
                for j, dst in enumerate((ga, gb)):
                    nc.gpsimd.indirect_dma_start(dst[par][:, :], None, slot_y[l][:, :],
                                                 bass.IndirectOffsetOnAxis(ap=pos[j][:, t:t + 1], axis=0)
                                                 ).then_inc(gathered[par], 16)

            for c in range(C):
                products(c, c % 2)
                for m in range(2 * NP * c // C, 2 * NP * (c + 1) // C):
                    shared_lo(m)
            with pool.Fori(0, B - 1) as b:
                for c in range(C):
                    products(b * C + C + c, c % 2)
            for l in range(LAYERS):
                NS = SLOTS[l]
                if l == 0:
                    pool.wait_ge(zeroed, 16)
                pool.wait_ge(routed, l + 1)
                for t in range(NT):
                    scatter(l, t, t % 2)
                pool.wait_ge(dw_lo, NP if l == 0 else 4 * NP)
                e = pool.value_load(chosen[0:1, 1:2], min_val=0, max_val=EXPERTS[l] - 1)
                for p in range(NP):
                    load_w(l, e, p, ex_in[l])
                pool.sem_inc(ex_lo[l], 1)
                first = 0
                if l == 0:
                    for s in range(2):
                        split(l, s, range(NP))

                    def pair(s, n, par, load=True):
                        split(l, s, range(NP // 2))
                        products(n, par, load)
                        split(l, s, range(NP // 2, NP))
                        split(l, s + 1, range(NP))

                    with pool.Fori(0, NW // 4 - 1) as i:
                        for j in range(2):
                            pair(i * 4 + (2 + 2 * j), 2 * i + (NW // 2 + j), j)
                    for j in range(2):
                        pair(NW - 2 + 2 * j, NW - 2 + j, j, load=False)
                    first = 2 + NW
                with pool.Fori(first, NS) as s:
                    split(l, s, range(NP))
                o = pool.value_load(tab[0:1, ORD, NS - 1:NS], min_val=0, max_val=EM - 1)
                for p in range(NP):
                    pool.wait_ge(ex_in[l][p], o * 16 + 32)
                    pool.sem_inc(raw_free, 1)
                for par in range(2):
                    pool.wait_ge(y_out[par], 16 * (sum(SLOTS[:l + 1]) // 2))
                if l == 0:
                    pool.wait_ge(wkv, NW)
                for t in range(NT):
                    gather(l, t, t % 2)

        @block.scalar
        def _(act):
            def exps(n, par):
                act.wait_ge(k_in[par], 16 * (n // 2 + 1) if isinstance(n, int) else n * 8 + (16 - 8 * par))
                if not (isinstance(n, int) and n < 2):
                    act.wait_ge(wkv, n - 1)
                nc.scalar.activation(ek[par][:, :], kb[par][:, :], ACT.Exp).then_inc(exp_k, 1)
                nc.scalar.activation(euk[par][:, :], kb[par][:, :], ACT.Exp, bias=ul[:, ds(n, 1)]).then_inc(exp_u, 1)

            def part(l, kind, t, j, q):
                if kind == "x":
                    if l:
                        act.wait_ge(xnew, t + 1)
                        nc.scalar.activation(xacc[:, ds(t, 1), :].rearrange("p a n -> p (a n)"), xin[j % 2][:, :], ACT.Copy).then_inc(xcopied, 1)
                    act.wait_ge(xT_ps, q + (X[l] + 1))
                    if not (isinstance(t, int) and t < 4):
                        act.wait_ge(x_lo, t + (V[l] - 3))
                    nc.scalar.activation(bT[j], XT[:, :], ACT.Tanh, scale=0.5).then_inc(xT_sb, 1)
                else:
                    act.wait_ge(xT_ps, q + (X[l] + 1))
                    par = j % 2
                    if isinstance(t, int) and t < 2:
                        if l:
                            act.wait_ge(y_out[par], 16 * (SLOTS[0] // 2))
                    else:
                        act.wait_ge(base_out[par], (t - par) * 8 + (16 * l * (NT // 2) + 16))
                    nc.scalar.activation(btok[par][:, :], XT[:, :], ACT.Copy).then_inc(xT_sb, 1)

            def split_tile(l, t, j):
                act.wait_ge(bT_sb, t + (NT * l + 1))
                if not (isinstance(t, int) and t < 2):
                    act.wait_ge(h3_ps, t * 2 + (U[l] - 1))
                elif l:
                    act.wait_ge(h3_ps, U[l])
                elif t == 1:
                    act.wait_ge(zeroed, 16)
                nc.scalar.activation(xTh[j % 2][:, :], bT[j % 4], ACT.Copy).then_inc(x_hi, 1)

            def tanh(u, par):
                act.wait_ge(h1_ps, u + 1)
                nc.scalar.activation(g[par][:, 0:F], h1[par][:, 0:F], ACT.Tanh, scale=0.5).then_inc(tanh_sb, 1)

            def split_g(u):
                act.wait_ge(gT_ps, u + 1)
                nc.scalar.activation(gTh[:, :], GT[:, 0:FC * P], ACT.Copy).then_inc(gT_hi, 1)

            def split_slot(l, s, par):
                act.wait_ge(xT_ps, s + (X[l] + 2 * NT + 1))
                if isinstance(s, int) and s == 0:
                    act.wait_ge(h3_ps, U[l] + 2 * NT - 2)
                else:
                    act.wait_ge(h3_ps, s + (U[l] + 2 * NT - 1))
                nc.scalar.activation(xTh[par][:, :], XT[:, :], ACT.Copy).then_inc(x_hi, 1)

            def copy_y(l, s, par, first=False):
                act.wait_ge(unit_done, U[l] + 2 * NT + s + 1)
                if first:
                    act.wait_ge(scattered[par], 16 * K * (NT // 2) * (l + 1))
                else:
                    act.wait_ge(y_out[par], 16 * (l * SLOTS[0] // 2) + 8 * (s - par))
                nc.scalar.activation(yb[par][:, :], Y[:, :], ACT.Copy).then_inc(y_copied, 1)

            def static_hi(m, at, loaded, split):
                p, (lo, hi) = m % NP, PIECES[m % NP]
                act.wait_ge(loaded[p], 16 * (m // NP + 1))
                nc.scalar.activation(w_hi[:, at + lo:at + hi], raw[:, lo:hi], ACT.Copy).then_inc(split, 1)

            def split_w(l, s):
                changed = act.value_load(tab[0:1, CHANGED, ds(s, 1)], min_val=0, max_val=1)
                with act.If(changed > 0):
                    o = act.value_load(tab[0:1, ORD, ds(s, 1)], min_val=0, max_val=EM - 1)
                    at = act.value_load(tab[0:1, OTHER, ds(s, 1)], min_val=0, max_val=WC)
                    for p, (lo, hi) in enumerate(PIECES):
                        act.wait_ge(ex_in[l][p], o * 16 + 16)
                        act.sem_inc(act_on, 1)
                        nc.scalar.activation(w_hi[:, ds(at + lo, hi - lo)], raw[:, lo:hi], ACT.Copy).then_inc(ex_hi[l], 1)

            act.wait_ge(wkv_p_in, 48)
            nc.scalar.activation(wl[:, :, :], wl[:, :, :], ACT.Exp).then_inc(astep, 1)
            act.wait_ge(astep, 1)
            nc.scalar.activation(wl[:, :, :], wl[:, :, :], ACT.Exp, scale=-1.0).then_inc(astep, 1)
            act.wait_ge(step, 1)
            nc.scalar.activation(tf[:, :], tf[:, :], ACT.Tanh, scale=0.5).then_inc(astep, 1)
            for n in range(2):
                exps(n, n)
            for m in range(NP):
                static_hi(m, 0, sh_in, sh_hi)
            for l in range(LAYERS):
                NS = SLOTS[l]
                if l:
                    act.wait_ge(unit_done, U[l])
                    for m in range(NP, 2 * NP):
                        static_hi(m, 0, dw_in, dw_hi)
                for t in range(4):
                    part(l, "x", t, t, t)
                if l == 0:
                    exps(2, 0)
                    for m in range(NP, NP + NP // 2):
                        static_hi(m, WC, sh_in, sh_hi)
                    exps(3, 1)
                    for m in range(NP + NP // 2, 2 * NP):
                        static_hi(m, WC, sh_in, sh_hi)
                    exps(4, 0)
                split_tile(l, 0, 0)
                part(l, "fin", 0, 0, 4)
                tanh(U[l], 0)
                if l:
                    for m in range(2 * NP, 3 * NP):
                        static_hi(m, WC, dw_in, dw_hi)

                def batch(b):
                    for k in range(8):
                        u = b * 8 + (U[l] + k)
                        last = isinstance(b, int)
                        todo = parts(b, k)
                        if k == 7 and not last:
                            split_tile(l, b * 4 + 4, 4)
                        split_g(u)
                        if k in (0, 2, 4):
                            split_tile(l, b * 4 + (1 + k // 2), 1 + k // 2)
                        if k == 7 and not last:
                            kind, j, q = todo[0]
                            part(l, kind, b * 4 + 4, j, q)
                        if not (last and k == 7):
                            tanh(u + 1, (k + 1) % 2)
                        for kind, j, q in (todo[1:] if k == 7 else todo):
                            part(l, kind, b * 4 + (j if kind == "fin" else 4 + j), j, q)
                        if l == 0 and k % 2 == 0 and not last:
                            exps(b * C + (C + k // 2 + 1), (k // 2 + 1) % 2)
                        if last and k == 0:
                            route(l)

                def route(l):
                    n = NT * EXPERTS[l]
                    act.wait_ge(rt_dve, 2 * l + 1)
                    if l == 0:
                        nc.scalar.activation(rB[:, 0:n], rA[:, 0:n], ACT.Tanh, scale=0.5).then_inc(rt_act, 1)
                    else:
                        nc.scalar.activation(rB[:, 0:n].rearrange("p (t e) -> p t e", t=NT),
                                             rA[:, 0:2 * n].rearrange("p (t e) -> p t e", t=NT)[:, :, EM:], ACT.Tanh, scale=0.5).then_inc(rt_act, 1)
                        act.wait_ge(rt_dve, 5)
                        nc.scalar.activation(rB[:, 0:n], rB[:, 0:n], ACT.Exp).then_inc(rt_act, 1)

                with act.Fori(0, B - 1) as b:
                    batch(b)
                batch(B - 1)
                act.wait_ge(unit_done, U[l] + 2 * NT - 1)
                for m in range((0, 3 * NP)[l], (NP, 4 * NP)[l]):
                    static_hi(m, 0, dw_in, dw_hi)
                for s in range(2):
                    split_slot(l, s, s)
                u0 = U[l] + 2 * NT
                tanh(u0, 0)

                def slot(s, par, up=True, ahead=True, first=False):
                    split_g(s + u0)
                    split_w(l, s)
                    if up:
                        tanh(s + (u0 + 1), 1 - par)
                    if ahead:
                        split_slot(l, s + 2, par)
                    copy_y(l, s, par, first)

                for s in range(2):
                    slot(s, s, first=True)
                if l == 0:
                    with act.Fori(0, NW // 4 - 1) as i:
                        for k in range(4):
                            if k % 2 == 0:
                                exps(i * 2 + (NW // 2 + 1 + k // 2), (k // 2 + 1) % 2)
                            slot(i * 4 + (2 + k), k % 2)
                    for k in range(4):
                        if k == 0:
                            exps(NW - 1, 1)
                        slot(2 + NW - 4 + k, k % 2)
                    done = 2 + NW
                else:
                    done = 2
                with act.Fori(done // 2, NS // 2 - 1) as i:
                    for k in range(2):
                        slot(i * 2 + k, k)
                slot(NS - 2, 0, ahead=False)
                slot(NS - 1, 1, up=False, ahead=False)

        @block.vector
        def _(dve):
            done = {"n": 0}

            def link(ins):
                done["n"] += 1
                ins.then_inc(step, 1)
                dve.wait_ge(step, done["at"] + done["n"])

            done["at"] = 0

            def enter(i, per_round):
                done["base"], done["outer"], done["n"] = done["n"], done["at"], 0
                done["at"] = i * per_round + done["base"]

            def leave(rounds, per_round):
                assert done["n"] == per_round, done["n"]
                done["at"], done["n"] = done["outer"], done["base"] + rounds * per_round

            flat_dec = dec[:, :, :, :].rearrange("p l b c -> p (l b c)")
            flat_osc = osc[:, :, :, :].rearrange("p l b c -> p (l b c)")
            flat_ratio = ratio[:, :, :, :].rearrange("p b c t -> p (b c t)")

            WKV_LINKS = 9

            def wkv_part(n, par, q, part):
                dec_n, osc_n = flat_dec[:, ds(n, 1)], flat_osc[:, ds(n, 1)]
                if part == 0:
                    dve.wait_ge(exp_k, n + 1)
                    nc.vector.tensor_scalar(ek[par][:, :], ek[par][:, :], E30, None, ALU.min).then_inc(min_k, 1)
                    dve.wait_ge(exp_u, n + 1)
                    nc.vector.tensor_scalar(euk[par][:, :], euk[par][:, :], E30, None, ALU.min).then_inc(min_u, 1)
                elif part in (1, 5):
                    src = ek[par] if part == 1 else ekv
                    if part == 1:
                        dve.wait_ge(min_k, n + 1)
                    else:
                        dve.wait_ge(kv, n + 1)
                    nc.vector.tensor_tensor_scan(fwd[:, :], dec_n.to_broadcast([P, T]), src[:, :], 0.0, ALU.mult, ALU.add)
                    link(nc.vector.tensor_tensor_scan(bwd[:, 0:T][:, ::-1], dec_n.to_broadcast([P, T]),
                                                      src[:, ::-1], 0.0, ALU.mult, ALU.add))
                elif part in (2, 6):
                    link(nc.vector.scalar_tensor_tensor(fwd[:, :], bwd[:, 1:T + 1], dec_n, fwd[:, :], ALU.mult, ALU.add))
                    if part == 2:
                        dve.wait_ge(min_u, n + 1)
                    else:
                        dve.wait_ge(ukv, n + 1)
                    link(nc.vector.tensor_tensor(fwd[:, :], fwd[:, :], (euk[par] if part == 2 else eukv)[:, :], ALU.add))
                elif part in (3, 4):
                    if part == 3:
                        link(nc.vector.tensor_scalar(fwd[:, :], fwd[:, :], 1e-8, None, ALU.max))
                    half = slice((part - 3) * T // 2, (part - 2) * T // 2)
                    link(nc.vector.reciprocal(rec[:, half], fwd[:, half]))
                else:
                    nc.vector.scalar_tensor_tensor(flat_ratio[:, ds(q * T, T)], fwd[:, :], osc_n, rec[:, :],
                                                   ALU.mult, ALU.mult).then_inc(wkv, 1)

            def finish(l, t, b, j):
                dve.wait_ge(xT_sb, use_x(t, b, j) + (2 * NT * l + 1))
                if l == 0:
                    dve.wait_ge(wkv, b * C + C)
                else:
                    dve.wait_ge(wkv, NW)
                nc.vector.scalar_tensor_tensor(bT[j].rearrange("p (c t) -> p c t", c=C), bT[j].rearrange("p (c t) -> p c t", c=C), 1.0,
                                               ratio[:, ds(b, 1), :, j * P:(j + 1) * P].rearrange("p a c t -> p (a c) t"),
                                               ALU.add, ALU.mult).then_inc(bT_sb, 1)

            def use_x(t, b, j):
                if isinstance(t, int) and t < 4:
                    return t
                return (b - 1) * 8 + (AHEAD + (1, 3, 5, 7)[j])

            def split_tile(l, t, j):
                dve.wait_ge(x_hi, t + (V[l] + 1))
                nc.vector.tensor_tensor(xTl[j % 2][:, :], bT[j % 4], xTh[j % 2][:, :].bitcast(f32), ALU.subtract).then_inc(x_lo, 1)

            def split_slot(l, s, par):
                dve.wait_ge(x_hi, s + (V[l] + NT + 1))
                nc.vector.tensor_tensor(xTl[par][:, :], XT[:, :], xTh[par][:, :].bitcast(f32), ALU.subtract).then_inc(x_lo, 1)

            def split_g(u):
                dve.wait_ge(gT_hi, u + 1)
                nc.vector.tensor_tensor(gTl[:, :], GT[:, 0:FC * P], gTh[:, :].bitcast(f32), ALU.subtract).then_inc(gT_lo, 1)

            def static_lo(m, at):
                p, (lo, hi) = m % NP, PIECES[m % NP]
                dve.wait_ge(dw_hi, m + 1)
                nc.vector.tensor_tensor(w_lo[:, at + lo:at + hi], raw[:, lo:hi],
                                        w_hi[:, at + lo:at + hi].bitcast(f32), ALU.subtract).then_inc(dw_lo, 1)

            def gate(u, par):
                dve.wait_ge(tanh_sb, u + 1)
                link(nc.vector.scalar_tensor_tensor(g[par][:, 0:F], g[par][:, 0:F], 1.0, h1[par][:, 0:F], ALU.add, ALU.mult))
                dve.wait_ge(h3_ps, u + 1)
                nc.vector.scalar_tensor_tensor(g[par][:, 0:F], g[par][:, 0:F], 0.5, h3[par][:, 0:F], ALU.mult, ALU.mult).then_inc(g_sb, 1)

            def add_shared(l, t):
                dve.wait_ge(unit_done, U[l] + 2 * t + 2)
                if l == 0:
                    dve.wait_ge(xacc_in, 16 * B)
                else:
                    dve.wait_ge(xcopied, t + 1)
                acc = xacc[:, ds(t, 1), :].rearrange("p a n -> p (a n)")
                nc.vector.tensor_tensor(acc, acc, Y[:, :], ALU.add).then_inc(y_added, 1)

            def combine(l, t, par, transposed=None):
                acc = xacc[:, ds(t, 1), :].rearrange("p a n -> p (a n)")
                dve.wait_ge(gathered[par], (t - par) * 16 + (32 + 32 * l * (NT // 2)))
                if l == 0:
                    if not (isinstance(t, int) and t < 2):
                        dve.wait_ge(xcopied, t - 1)
                        dve.wait_ge(xT_ps, transposed + (X[1] + 1))
                    dve.wait_ge(y_added, NT + 1)
                elif t >= 2:
                    dve.wait_ge(out_st[par], 8 * (t - par))
                link(nc.vector.scalar_tensor_tensor(acc, ga[par][:, :], wsel[0][:, ds(t, 1)], acc, ALU.mult, ALU.add))
                nc.vector.scalar_tensor_tensor(xin[par][:, :], gb[par][:, :], wsel[1][:, ds(t, 1)], acc, ALU.mult, ALU.add).then_inc(xnew, 1)

            def route_choose(l):
                E = EXPERTS[l]
                n = NT * E
                v3 = lambda a: a[:, 0:n].rearrange("p (t e) -> p t e", t=NT)
                wide = lambda a: a[:, :].rearrange("p (t a) -> p t a", a=1).to_broadcast([P, NT, E])
                row = lambda a: a[:, 0:E].rearrange("p (a e) -> p a e", a=1).to_broadcast([P, NT, E])
                dve.wait_ge(logits, NT * (l + 1))
                if l == 0:
                    nc.vector.tensor_copy(rA[:, 0:n], LG[:, 0:n]).then_inc(rt_dve, 1)
                    dve.wait_ge(rt_act, 1)
                    link(nc.vector.tensor_scalar(v3(rB), v3(rB), 0.5, 0.5, ALU.mult, ALU.add))
                    link(nc.vector.tensor_tensor(v3(rA), v3(rB), row(biasb[0]), ALU.add))
                else:
                    dve.wait_ge(xcopied, NT)
                    both3 = rA[:, 0:2 * n].rearrange("p (t e) -> p t e", t=NT)
                    nc.vector.tensor_copy(rA[:, 0:2 * n], LG[:, 0:2 * n]).then_inc(rt_dve, 1)
                    dve.wait_ge(rt_act, 2)
                    link(nc.vector.scalar_tensor_tensor(v3(rB), v3(rB), 1.0, both3[:, :, E:], ALU.add, ALU.mult))
                    link(nc.vector.scalar_tensor_tensor(v3(rB), v3(rB), 0.5, both3[:, :, 0:E], ALU.mult, ALU.mult))
                    link(nc.vector.scalar_tensor_tensor(rB[:, 0:n], rB[:, 0:n], -1.0, rB[:, 0:n], ALU.mult, ALU.max))
                    link(nc.vector.tensor_reduce(m16[0][:, :], v3(rB), AX.X, ALU.max))
                    nc.vector.tensor_tensor(v3(rB), v3(rB), wide(m16[0]), ALU.subtract).then_inc(rt_dve, 2)
                    dve.wait_ge(rt_act, 3)
                    link(nc.vector.tensor_reduce(m16[0][:, :], v3(rB), AX.X, ALU.add))
                    link(nc.vector.reciprocal(m16[1][:, :], m16[0][:, :]))
                    link(nc.vector.tensor_tensor(v3(rB), v3(rB), wide(m16[1]), ALU.mult))
                    link(nc.vector.tensor_tensor(v3(rA), v3(rB), row(biasb[1]), ALU.add))
                    link(nc.vector.tensor_tensor(v3(rC), v3(rB), row(scaleb), ALU.mult))
                    link(nc.vector.tensor_scalar(rB[:, 0:n], rC[:, 0:n], 1.0, None, ALU.add))
                for j in range(K):
                    link(nc.vector.tensor_reduce(m16[0][:, :], v3(rA), AX.X, ALU.max))
                    link(nc.vector.tensor_tensor(v3(rC), v3(rA), wide(m16[0]), ALU.is_equal))
                    link(nc.vector.tensor_scalar(v3(rC), v3(rC), -float(EM), float(EM), ALU.mult, ALU.add))
                    link(nc.vector.tensor_tensor(v3(rC), v3(rC), row(iota_e), ALU.add))
                    link(nc.vector.tensor_reduce(m16[1][:, :], v3(rC), AX.X, ALU.min))
                    link(nc.vector.tensor_tensor(v3(oh[j]), row(iota_e), wide(m16[1]), ALU.is_equal))
                    if j + 1 < K:
                        link(nc.vector.scalar_tensor_tensor(v3(rA), v3(oh[j]), -3e38, v3(rA), ALU.mult, ALU.add))
                    link(nc.vector.tensor_tensor(v3(rC), v3(oh[j]), v3(rB), ALU.mult))
                    link(nc.vector.tensor_reduce(wsel[j][:, :], v3(rC), AX.X, ALU.add))
                if l == 0:
                    link(nc.vector.tensor_tensor(m16[0][:, :], wsel[0][:, :], wsel[1][:, :], ALU.add))
                    link(nc.vector.tensor_scalar(m16[0][:, :], m16[0][:, :], 1e-12, None, ALU.max))
                    link(nc.vector.reciprocal(m16[1][:, :], m16[0][:, :]))
                    nc.vector.tensor_tensor(wsel[0][:, :], wsel[0][:, :], m16[1][:, :], ALU.mult)
                    link(nc.vector.tensor_tensor(wsel[1][:, :], wsel[1][:, :], m16[1][:, :], ALU.mult))
                nc.vector.tensor_tensor(v3(both), v3(oh[0]), v3(oh[1]), ALU.add).then_inc(rt_dve, 1)

            def route_place(l):
                E, NS = EXPERTS[l], SLOTS[l]
                te = lambda a: a[:, 0:NT * E].rearrange("p (t e) -> p t e", t=NT)
                et = lambda a: a[:, 0:NT * E].rearrange("p (e t) -> p e t", e=E)
                swap = lambda a: a[:, 0:NT * E].rearrange("p (e t) -> p t e", e=E)
                over = lambda a, n: a[:, 0:E].rearrange("p (a e) -> p a e", a=1).to_broadcast([P, n, E])
                by_slot = lambda n: iota_s[:, 0:n].rearrange("p (s a) -> p s a", a=1).to_broadcast([P, n, E])
                counts, ntiles, ends, filled = cnt
                dve.wait_ge(rt_pe, l + 1)
                link(nc.vector.tensor_copy(et(rA), LG[:, 256:256 + NT * E].rearrange("p (t e) -> p e t", t=NT)))
                link(nc.vector.tensor_tensor_scan(rC[:, 0:NT * E], seg[:, :, :].rearrange("p e t -> p (e t)")[:, 0:NT * E],
                                                  rA[:, 0:NT * E], 0.0, ALU.mult, ALU.add))
                link(nc.vector.tensor_copy(counts[:, 0:E], et(rC)[:, :, NT - 1]))
                link(nc.vector.tensor_tensor(et(rB), counts[:, 0:E].rearrange("p (e a) -> p e a", a=1).to_broadcast([P, E, NT]),
                                             rows_j[:, :].rearrange("p (a t) -> p a t", a=1).to_broadcast([P, E, NT]), ALU.is_gt))
                link(nc.vector.tensor_reduce(ntiles[:, 0:E], et(rB), AX.X, ALU.add))
                link(nc.vector.tensor_tensor_scan(ends[:, 0:E], ones[:, 0:E], ntiles[:, 0:E], 0.0, ALU.mult, ALU.add))
                link(nc.vector.tensor_scalar(counts[:, 0:E], ntiles[:, 0:E], 1.0, None, ALU.min))
                link(nc.vector.tensor_tensor_scan(filled[:, 0:E], ones[:, 0:E], counts[:, 0:E], 0.0, ALU.mult, ALU.add))
                NO = EM + 2
                ro = rD[:, 0:NO * E].rearrange("p (s e) -> p s e", s=NO)
                link(nc.vector.tensor_tensor(ro, by_slot(NO), over(filled, NO), ALU.is_gt))
                link(nc.vector.tensor_reduce(rB[:, 0:NO], ro, AX.X, ALU.add))
                nc.vector.tensor_scalar(chosen[:, :], rB[:, 0:NO], float(E - 1), None, ALU.min)
                rs = rD[:, 0:NS * E].rearrange("p (s e) -> p s e", s=NS)
                link(nc.vector.tensor_tensor(rs, by_slot(NS), over(ends, NS), ALU.is_gt))
                link(nc.vector.tensor_tensor(rs, rs, over(counts, NS), ALU.mult))
                link(nc.vector.tensor_reduce(rB[:, 0:NS], rs, AX.X, ALU.add))
                link(nc.vector.tensor_scalar(filled[:, E - 1:E], filled[:, E - 1:E], -1.0, None, ALU.add))
                order, changed = tabf[:, ORD, 0:NS], tabf[:, CHANGED, 0:NS]
                link(nc.vector.tensor_scalar(order, rB[:, 0:NS], filled[:, E - 1:E], None, ALU.min))
                nc.vector.memset(tabf[:, CHANGED, 0:1], 0.0)
                link(nc.vector.tensor_tensor(tabf[:, CHANGED, 1:NS], tabf[:, ORD, 1:NS], tabf[:, ORD, 0:NS - 1], ALU.subtract))
                link(nc.vector.tensor_scalar(rB[:, 0:NS], changed, -2.0, 1.0, ALU.mult, ALU.add))
                link(nc.vector.tensor_tensor_scan(tabf[:, BUF, 0:NS], rB[:, 0:NS], changed, 0.0, ALU.mult, ALU.add))
                nc.vector.tensor_scalar(tabf[:, OTHER, 0:NS], tabf[:, BUF, 0:NS], -float(WC), float(WC), ALU.mult, ALU.add)
                link(nc.vector.tensor_scalar(tabf[:, DOWNWAIT, 0:NS], order, float(NP), 1.0, ALU.mult, ALU.add))
                link(nc.vector.tensor_scalar(tabf[:, UPWAIT, 0:NS], tabf[:, DOWNWAIT, 0:NS], float(UPP - NP), 1.0, ALU.add, ALU.max))
                link(nc.vector.memset(tabf[:, CHANGED, 0:1], 1.0))
                nc.vector.tensor_copy(tab[:, :, 0:NS], tabf[:, :, 0:NS])
                link(nc.vector.tensor_tensor(ntiles[:, 0:E], ends[:, 0:E], ntiles[:, 0:E], ALU.subtract))
                link(nc.vector.tensor_tensor(et(rC), et(rC), et(rA), ALU.subtract))
                link(nc.vector.tensor_tensor(te(rB), swap(rC), LG[:, 0:NT * E].rearrange("p (t e) -> p t e", t=NT), ALU.add))
                link(nc.vector.scalar_tensor_tensor(te(rB), over(ntiles, NT), float(P), te(rB), ALU.mult, ALU.add))
                for j in range(K):
                    link(nc.vector.tensor_tensor(te(rC), te(oh[j]), te(rB), ALU.mult))
                    link(nc.vector.tensor_reduce(m16[j][:, :], te(rC), AX.X, ALU.add))
                    last = nc.vector.tensor_copy(pos[j][:, :], m16[j][:, :])
                last.then_inc(routed, 1)

            dve.sem_inc(y_added, 1)
            nc.vector.memset(bwd[:, T:T + 1], 0.0)
            for i in range(2):
                nc.vector.memset(g[i][:, F:FC * P], 0.0)
            dve.wait_ge(wkv_p_in, 48)
            link(nc.vector.tensor_reduce(tf[:, :], condb, AX.X, ALU.add))
            dve.wait_ge(astep, 3)
            link(nc.vector.tensor_scalar(tf[:, :], tf[:, :], 0.5, 0.5, ALU.mult, ALU.add))
            nc.vector.tensor_scalar(dfac[:, :], tf[:, :], 0.5, 0.5, ALU.mult, ALU.add)
            link(nc.vector.tensor_scalar(sfac[:, :], tf[:, :], 0.1, 0.4, ALU.mult, ALU.add))
            over_c = lambda a: a[:, :].rearrange("p (b a) -> p b a", a=1).to_broadcast([P, B, C])
            for l in range(LAYERS):
                nc.vector.tensor_tensor(dec[:, l, :, :], over_c(dfac),
                                        wl[:, l, :].rearrange("p (a c) -> p a c", a=1).to_broadcast([P, B, C]), ALU.mult)
                last = nc.vector.tensor_copy(osc[:, l, :, :], over_c(sfac))
            link(last)
            for c in range(C):
                for part in range(8):
                    wkv_part(c, c % 2, c, part)
                if c == 0:
                    dve.wait_ge(consts, 9)
                    nc.vector.tensor_scalar(seg[:, :, :], seg[:, :, :], 1.0, None, ALU.min)
            turns = [range(32 * i // 14, 32 * (i + 1) // 14) for i in range(14)] + [range(0)] * 2
            for l in range(LAYERS):
                NS = SLOTS[l]
                if l == 0:
                    dve.wait_ge(params_in, 80)
                else:
                    dve.wait_ge(wkv, NW)
                    for m in range(NP, 2 * NP):
                        static_lo(m, 0)
                    for t in range(4):
                        combine(0, t, t % 2, t - 2)
                finish(l, 0, 0, 0)
                split_tile(l, 0, 0)
                gate(U[l], 0)
                if l:
                    for m in range(2 * NP, 3 * NP):
                        static_lo(m, WC)

                def wkv_turn(b, turn):
                    for i in turns[turn]:
                        c = i // 8
                        wkv_part(b * C + (C + c), c % 2, b * C + (C + c), i % 8)

                def batch(b):
                    last = isinstance(b, int)
                    for k in range(8):
                        u = b * 8 + (U[l] + k)
                        if k == 7 and not last:
                            finish(l, b * 4 + 4, b + 1, 0)
                        split_g(u)
                        if k == 7 and not last:
                            split_tile(l, b * 4 + 4, 4)
                        for kind, j, q in parts(b, k):
                            if kind == "fin" and j < 4:
                                finish(l, b * 4 + j, b, j)
                            elif kind == "x" and l:
                                t = b * 4 + 4 + j
                                combine(0, t, j % 2, (b - 1) * 8 + (AHEAD + (5, 7)[j]) if j < 2 else b * 8 + (AHEAD + (1, 3)[j - 2]))
                        if l == 0 and not last:
                            wkv_turn(b, 2 * k)
                        if not (last and k == 7):
                            gate(u + 1, (k + 1) % 2)
                        if k in (0, 2, 4):
                            split_tile(l, b * 4 + (1 + k // 2), 1 + k // 2)
                        if k % 2:
                            add_shared(l, b * 4 + k // 2)
                        if l == 0 and not last:
                            wkv_turn(b, 2 * k + 1)
                        if last and k == 0:
                            route_choose(l)
                        if last and k == 1:
                            route_place(l)

                per = 8 + (4 * WKV_LINKS if l == 0 else 4)
                with dve.Fori(0, B - 1) as b:
                    enter(b, per)
                    batch(b)
                leave(B - 1, per)
                batch(B - 1)
                for m in range((0, 3 * NP)[l], (NP, 4 * NP)[l]):
                    static_lo(m, 0)
                u0 = U[l] + 2 * NT
                for s in range(2):
                    split_slot(l, s, s)
                gate(u0, 0)

                def slot(s, par, n=None, q=None, first=False, mid=(), end=()):
                    split_g(s + u0)
                    for part in mid:
                        wkv_part(n, first, q, part)
                    gate(s + (u0 + 1), 1 - par)
                    if not (isinstance(s, int) and s + 2 >= NS):
                        split_slot(l, s + 2, par)
                    for part in end:
                        wkv_part(n, first, q, part)

                for s in range(2):
                    slot(s, s)
                if l == 0:
                    halves_of_unit = (dict(mid=(0, 1), end=(2, 3)), dict(mid=(4,), end=(5, 6, 7)))
                    per = 4 + 2 * WKV_LINKS
                    with dve.Fori(0, NW // 4 - 1) as i:
                        enter(i, per)
                        for k in range(4):
                            slot(i * 4 + (2 + k), k % 2, i * 2 + (NW // 2 + k // 2), i * 2 + k // 2, k // 2, **halves_of_unit[k % 2])
                    leave(NW // 4 - 1, per)
                    for k in range(4):
                        n = NW - 2 + k // 2
                        slot(2 + NW - 4 + k, k % 2, n, n - NW // 2, k // 2, **halves_of_unit[k % 2])
                    start = 2 + NW
                else:
                    start = 2
                rounds = NS // 2 - 1 - start // 2
                with dve.Fori(0, rounds) as i:
                    enter(i, 2)
                    for k in range(2):
                        slot(i * 2 + (start + k), k)
                leave(rounds, 2)
                slot(NS - 2, 0)
                split_g(NS - 1 + u0)
            for t in range(NT):
                combine(1, t, t % 2)

        @block.tensor
        def _(pe):
            def part(l, kind, t, j, q):
                if isinstance(q, int) and q == 0:
                    if l:
                        pe.wait_ge(x_lo, V[l])
                else:
                    pe.wait_ge(xT_sb, q + 2 * NT * l)
                if kind == "x":
                    par = j % 2
                    if l == 0:
                        pe.wait_ge(x_in[par], (t - par) * 8 + 16)
                    else:
                        pe.wait_ge(xnew, t + 1)
                    src = xin[par]
                else:
                    n = EXPERTS[0] if l == 0 else 2 * EXPERTS[1]
                    pe.wait_ge(bT_sb, t + (NT * l + 1))
                    src = bT[j % 4]
                    for c in range(C):
                        last = nc.tensor.matmul(LG[:, ds(t * n, n)], src[:, c * P:(c + 1) * P], gw[l][:, c, :], start=(c == 0), stop=(c == C - 1))
                    last.then_inc(logits, 1)
                for c in range(C):
                    last = nc.tensor.transpose(XT[:, c * P:(c + 1) * P], src[:, c * P:(c + 1) * P], ident[:, :])
                last.then_inc(xT_ps, 1)

            def up(par, xpar, buf):
                for ps_, off, s in ((h1, 0, h1_ps), (h3, F, h3_ps)):
                    for c in range(C):
                        at = buf * WC + c * 2 * F + off
                        hi, lo = (a[xpar][:, c * P:(c + 1) * P] for a in (xTh, xTl))
                        nc.tensor.matmul(ps_[par][:, 0:F], hi, w_hi[:, at:at + F], start=(c == 0), stop=False)
                        nc.tensor.matmul(ps_[par][:, 0:F], hi, w_lo[:, at:at + F], start=False, stop=False)
                        last = nc.tensor.matmul(ps_[par][:, 0:F], lo, w_hi[:, at:at + F], start=False, stop=(c == C - 1))
                    last.then_inc(s, 1)

            def transpose_g(u, par):
                pe.wait_ge(g_sb, u + 1)
                for j in range(FC):
                    last = nc.tensor.transpose(GT[:, j * P:(j + 1) * P], g[par][:, j * P:(j + 1) * P], ident[:, :])
                last.then_inc(gT_ps, 1)

            def down(u, buf, first, last_of):
                at = lambda j: buf * WC + UP + j * D
                for j in range(FC):
                    hi = gTh[:, j * P:(j + 1) * P]
                    nc.tensor.matmul(Y[:, :], hi, w_hi[:, at(j):at(j) + D], start=(first and j == 0), stop=False)
                    nc.tensor.matmul(Y[:, :], hi, w_lo[:, at(j):at(j) + D], start=False, stop=False)
                pe.wait_ge(gT_lo, u + 1)
                for j in range(FC):
                    last = nc.tensor.matmul(Y[:, :], gTl[:, j * P:(j + 1) * P], w_hi[:, at(j):at(j) + D],
                                            start=False, stop=(last_of and j == FC - 1))
                last.then_inc(unit_done, 1)

            def transpose_slot(l, s, par):
                pe.wait_ge(xs_in[par], 8 * (s - par) + 16 + 16 * (l * SLOTS[0] // 2))
                if isinstance(s, int) and s == 0:
                    pe.wait_ge(xT_sb, 2 * NT * (l + 1))
                else:
                    pe.wait_ge(x_lo, s + (V[l] + NT))
                for c in range(C):
                    last = nc.tensor.transpose(XT[:, c * P:(c + 1) * P], xs[par][:, c * P:(c + 1) * P], ident[:, :])
                last.then_inc(xT_ps, 1)

            pe.wait_ge(consts, 9)
            pe.wait_ge(params_in, 80)
            for l in range(LAYERS):
                NS = SLOTS[l]
                if l:
                    pe.wait_ge(rt_dve, 1)
                for t in range(4):
                    part(l, "x", t, t, t)
                part(l, "fin", 0, 0, 4)

                def weights(n):
                    if l == 0:
                        pe.wait_ge(sh_lo, n)
                    else:
                        pe.wait_ge(dw_lo, NP + n)

                def shared_up(u, k, t):
                    if k % 2 == 0:
                        pe.wait_ge(x_lo, t + (V[l] + 1))
                    up(k % 2, k // 2 % 2, k % 2)

                def batch(b):
                    last = isinstance(b, int)
                    for k in range(8):
                        u = b * 8 + (U[l] + k)
                        todo = parts(b, k)
                        transpose_g(u, k % 2)
                        if k == 7 and not last:
                            kind, j, q = todo[0]
                            part(l, kind, b * 4 + 4, j, q)
                        if k == 0:
                            weights(NP + UPP)
                        if not (last and k == 7):
                            shared_up(u + 1, k + 1, b * 4 + (k + 1) // 2)
                        if k % 2 == 0:
                            if l and k == 0:
                                pe.wait_ge(y_copied, SLOTS[0])
                            pe.wait_ge(y_added, b * 4 + (NT * l + k // 2 + 1))
                        weights(2 * NP)
                        pe.wait_ge(gT_hi, u + 1)
                        down(u, k % 2, k % 2 == 0, k % 2 == 1)
                        for kind, j, q in (todo[1:] if k == 7 else todo):
                            part(l, kind, b * 4 + (j if kind == "fin" else 4 + j), j, q)
                        if last and k == 1:
                            pe.wait_ge(rt_dve, 2 if l == 0 else 6)
                            n = NT * EXPERTS[l]
                            nc.tensor.matmul(LG[:, 0:n], before[:, :], both[:, 0:n], start=True, stop=True)
                            nc.tensor.matmul(LG[:, 256:256 + n], ones[:, :], both[:, 0:n], start=True, stop=True).then_inc(rt_pe, 1)

                weights(UPP)
                shared_up(U[l], 0, 0)
                with pe.Fori(0, B - 1) as b:
                    batch(b)
                batch(B - 1)

                for s in range(2):
                    transpose_slot(l, s, s)
                u0 = U[l] + 2 * NT

                def slot_up(s, par):
                    buf = pe.value_load(tab[0:1, BUF, ds(s, 1)], min_val=0, max_val=1)
                    ready = pe.value_load(tab[0:1, UPWAIT, ds(s, 1)], min_val=1, max_val=NP * EM)
                    pe.wait_ge(x_lo, s + (V[l] + NT + 1))
                    pe.sem_inc(pe_on, 1)
                    pe.wait_ge(ex_lo[l], ready)
                    pe.sem_inc(pe_on, 1)
                    with pe.If(buf > 0):
                        up(par, par, 1)
                    with pe.Else():
                        up(par, par, 0)

                def slot_down(s, par, first=False):
                    buf = pe.value_load(tab[0:1, BUF, ds(s, 1)], min_val=0, max_val=1)
                    ready = pe.value_load(tab[0:1, DOWNWAIT, ds(s, 1)], min_val=1, max_val=NP * EM)
                    if first:
                        pe.wait_ge(y_added, NT * (l + 1) + 1)
                    else:
                        pe.wait_ge(y_copied, s + SLOTS[0] * l)
                    pe.sem_inc(pe_on, 1)
                    pe.wait_ge(ex_lo[l], ready)
                    pe.sem_inc(pe_on, 1)
                    pe.wait_ge(gT_hi, s + (u0 + 1))
                    pe.sem_inc(pe_on, 1)
                    with pe.If(buf > 0):
                        down(s + u0, 1, True, True)
                    with pe.Else():
                        down(s + u0, 0, True, True)

                def slot(s, par, ahead_up=True, ahead_x=True, first=False):
                    transpose_g(s + u0, par)
                    if ahead_up:
                        slot_up(s + 1, 1 - par)
                    if ahead_x:
                        transpose_slot(l, s + 2, par)
                    slot_down(s, par, first)

                pe.wait_ge(routed, l + 1)
                pe.wait_ge(dw_lo, NP if l == 0 else 4 * NP)
                slot_up(0, 0)
                slot(0, 0, first=True)
                slot(1, 1)
                with pe.Fori(1, NS // 2 - 1) as i:
                    for k in range(2):
                        slot(i * 2 + k, k)
                slot(NS - 2, 0, ahead_x=False)
                slot(NS - 1, 1, ahead_up=False, ahead_x=False)


def pack_experts(up, gate, down):
    e = up.shape[0]
    both = np.concatenate([gate, up], axis=2).reshape(e, C, P, 2 * F).transpose(0, 2, 1, 3).reshape(e, P, UP)
    padded = np.zeros((e, FC * P, D), np.float32)
    padded[:, :F] = down
    low = padded.reshape(e, FC, P, D).transpose(0, 2, 1, 3).reshape(e, P, FC * D)
    return np.ascontiguousarray(np.concatenate([both, low], axis=2))


def kernel(x, fside_BxSxS_0, cond_512, L0_cond_w, L0_cond_u, L0_ffn_gate_w, L0_ffn_router_bias, L0_ffn_W1,
           L0_ffn_W3, L0_ffn_W2, L0_ffn_sw1, L0_ffn_sw3, L0_ffn_sw2, L1_cond_w, L1_cond_u, L1_ffn_gate_w,
           L1_ffn_cls_w, L1_ffn_extra_scale, L1_ffn_extra_bias, L1_ffn_wg, L1_ffn_wu, L1_ffn_wd, L1_ffn_sg,
           L1_ffn_su, L1_ffn_sd):
    import concourse.bacc as bacc
    from concourse.bass_utils import run_bass_kernel_spmd

    a = lambda v: np.asarray(v)
    chan = lambda v: a(v).reshape(C, P).T
    rep = lambda v, n: np.ascontiguousarray(np.broadcast_to(np.tile(a(v), n), (P, n * a(v).size)))
    halves = lambda w: a(w).reshape(2, F, D)
    gate_cols = lambda w: a(w).T.reshape(C, P, -1).transpose(1, 0, 2).reshape(P, -1)
    k = a(fside_BxSxS_0).transpose(0, 2, 1).reshape(B * C, P, T)
    ins = {
        "x": a(x).reshape(N, D),
        "kt": np.ascontiguousarray(np.concatenate([k] * LAYERS)),
        "cond": rep(a(cond_512).reshape(-1), 1),
        "wdec": np.ascontiguousarray(np.concatenate([chan(L0_cond_w), chan(L1_cond_w)], axis=1)),
        "ub": np.ascontiguousarray(np.concatenate([chan(L0_cond_u)] * B + [chan(L1_cond_u)] * B, axis=1)),
        "gates0": np.ascontiguousarray(gate_cols(L0_ffn_gate_w)),
        "gates1": np.ascontiguousarray(gate_cols(np.concatenate([a(L1_ffn_cls_w), a(L1_ffn_gate_w)]))),
        "bias0": rep(L0_ffn_router_bias, 1),
        "bias1": rep(L1_ffn_extra_bias, 1),
        "scale1": rep(L1_ffn_extra_scale, 1),
        "wts0": pack_experts(
            np.concatenate([a(L0_ffn_W3), halves(L0_ffn_sw3).transpose(0, 2, 1)]),
            np.concatenate([a(L0_ffn_W1), halves(L0_ffn_sw1).transpose(0, 2, 1)]),
            np.concatenate([a(L0_ffn_W2), a(L0_ffn_sw2).T.reshape(2, F, D)])),
        "wts1": pack_experts(
            np.concatenate([a(L1_ffn_wu), halves(L1_ffn_su)]).transpose(0, 2, 1),
            np.concatenate([a(L1_ffn_wg), halves(L1_ffn_sg)]).transpose(0, 2, 1),
            np.concatenate([a(L1_ffn_wd).transpose(0, 2, 1), a(L1_ffn_sd).T.reshape(2, F, D)])),
    }
    nc = bacc.Bacc("TRN2", target_bir_lowering=False, num_devices=1)
    ap = {n: nc.dram_tensor(f"in_{n}", v.shape, mybir.dt.float32, kind="ExternalInput").ap() for n, v in ins.items()}
    out = nc.dram_tensor("out_x", (N, D), mybir.dt.float32, kind="ExternalOutput").ap()
    build(nc, ap["x"], ap["kt"], ap["cond"], ap["wdec"], ap["ub"], (ap["gates0"], ap["gates1"]),
          (ap["bias0"], ap["bias1"]), ap["scale1"], (ap["wts0"], ap["wts1"]), out)
    r = run_bass_kernel_spmd(nc, [{f"in_{n}": v for n, v in ins.items()}], core_ids=[0])
    return r.results[0]["out_x"].reshape(B, T, D)
```

```python
from contextlib import ExitStack

import numpy as np
import concourse.bass as bass
from concourse import mybir

P = 128
B, T, D = 4, 512, 512
N = B * T
NT = N // P
C = D // P
F = 352
FC = -(-F // P)
EXPERTS = (8, 14)
K = 2
SLOTS = tuple(N * K // P + e for e in EXPERTS)
UP = C * 2 * F
WC = UP + FC * D
PIECES = ((0, UP // 2), (UP // 2, UP), (UP, WC))
NP, UPP = len(PIECES), 2
UP_PIECES, DOWN_PIECES = range(UPP), range(UPP, NP)
EM, SM = max(EXPERTS), max(SLOTS)
LAYERS = len(EXPERTS)
NW = LAYERS * B * C
E30 = float(np.float32(np.exp(np.float32(30.0))))


def build(nc, x, kt, cond, wdec, ub, gates, bias, scale1, wts, out):
    f32, i32, f32r = mybir.dt.float32, mybir.dt.int32, mybir.dt.float32r
    ALU, ACT, AX = mybir.AluOpType, mybir.ActivationFunctionType, mybir.AxisListType
    ds = bass.ds
    ctx = ExitStack()
    with ctx:
        def sb(name, shape, dt=f32):
            return ctx.enter_context(nc.sbuf_tensor(name, shape, dt))

        def ps(name):
            return ctx.enter_context(nc.psum_tensor(name, [P, 512], f32))

        def sem(name):
            return ctx.enter_context(nc.semaphore(name))

        slot_x = nc.dram_tensor("slot_x", [(B - 1) * C * T, D], f32, kind="Internal").ap()
        slot_y = [nc.dram_tensor(f"slot_y{l}", [SLOTS[l] * P, D], f32, kind="Internal").ap() for l in range(LAYERS)]
        base_d = nc.dram_tensor("base_d", [N, D], f32, kind="Internal").ap()

        xacc = sb("xacc", [P, NT, D])
        ratio = sb("ratio", [P, B, C, T])
        raw = sb("raw", [P, WC])
        w_hi = sb("w_hi", [P, 2 * WC], f32r)
        w_lo = sb("w_lo", [P, 2 * WC], f32r)
        ident = sb("ident", [P, P])
        before = sb("before", [P, P])
        ones = sb("ones", [P, P])
        xin = [sb(f"xin{i}", [P, D]) for i in range(2)]
        bTs = sb("bTs", [P, 4 * D])
        bT = [bTs[:, i * D:(i + 1) * D] for i in range(4)]
        xs = bT
        xTh = [sb(f"xTh{i}", [P, C * P], f32r) for i in range(2)]
        xTl = [sb(f"xTl{i}", [P, C * P], f32r) for i in range(2)]
        g = [sb(f"g{i}", [P, FC * P]) for i in range(2)]
        gTh = sb("gTh", [P, FC * P], f32r)
        gTl = sb("gTl", [P, FC * P], f32r)
        yb = [sb(f"yb{i}", [P, D]) for i in range(2)]
        btok = yb
        kb = [sb(f"kb{i}", [P, T]) for i in range(2)]
        ek = [sb(f"ek{i}", [P, T]) for i in range(2)]
        euk = [sb(f"euk{i}", [P, T]) for i in range(2)]
        ekv, eukv = sb("ekv", [P, T]), sb("eukv", [P, T])
        fwd = sb("fwd", [P, T])
        bwd = sb("bwd", [P, T + 1])
        rec = sb("rec", [P, T])
        bases = ratio[:, :, :, :].rearrange("p b c t -> p (b c) t")
        pairs = (ek, euk, kb, [ekv, eukv])

        def results(l, t, j, i):
            if l == 0:
                return pairs[i][j][:, :]
            return (ratio[:, :, :, :].rearrange("p b c t -> p (b c t)") if j == 0 else w_lo[:, :].bitcast(f32))[:, t * D:(t + 1) * D]

        condb = ekv[:, :].rearrange("p (b n) -> p b n", b=B)
        wl = sb("wl", [P, LAYERS, C])
        ul = sb("ul", [P, NW])
        dec = sb("dec", [P, LAYERS, B, C])
        osc = sb("osc", [P, LAYERS, B, C])
        tf = sb("tf", [P, B])
        dfac, sfac = sb("dfac", [P, B]), sb("sfac", [P, B])
        gw = [sb("gw0", [P, C, EXPERTS[0]]), sb("gw1", [P, C, 2 * EXPERTS[1]])]
        biasb = [sb(f"biasb{l}", [P, EXPERTS[l]]) for l in range(LAYERS)]
        scaleb = sb("scaleb", [P, EXPERTS[1]])
        iota_e = sb("iota_e", [P, EM])
        rows_j = sb("rows_j", [P, NT])
        iota_s = sb("iota_s", [P, SM])
        seg = sb("seg", [P, EM, NT])
        rA, rB, rC, rD = xin[0], fwd, rec, bTs
        oh = [ekv, eukv]
        both = bwd
        m16 = [sb(f"m16{i}", [P, NT]) for i in range(3)]
        cnt = [sb(f"cnt{i}", [P, EM]) for i in range(4)]
        wsel = [sb(f"wsel{i}", [P, NT]) for i in range(2)]
        pos = [sb(f"pos{i}", [P, NT], i32) for i in range(2)]
        CHANGED, ORD, UPCODE, DOWNCODE, OTHER, BUF = range(6)
        BUF1 = 1024
        tab = sb("tab", [P, 5, SM], i32)
        tabf = xin[1][:, 0:6 * SM].rearrange("p (r s) -> p r s", r=6)
        chosen = sb("chosen", [P, EM + 2], i32)

        h1 = [ps(f"h1_{i}") for i in range(2)]
        h3 = [ps(f"h3_{i}") for i in range(2)]
        XT, GT, Y, LG = ps("XT"), ps("GT"), ps("Y"), ps("LG")

        params_in = sem("params_in")
        wkv_p_in = sem("wkv_p_in")
        xacc_in = sem("xacc_in")
        consts = sem("consts")
        filled_x = sem("filled_x")
        x_in = [sem(f"x_in{i}") for i in range(2)]
        dw_in = [sem(f"dw_in{p}") for p in range(NP)]
        dw_hi, dw_lo = sem("dw_hi"), sem("dw_lo")
        ex_in = [[sem(f"ex_in{l}_{p}") for p in range(NP)] for l in range(LAYERS)]
        ex_hi = [sem(f"ex_hi{l}") for l in range(LAYERS)]
        ex_lo = [sem(f"ex_lo{l}") for l in range(LAYERS)]
        raw_free = sem("raw_free")
        xs_in = [sem(f"xs_in{i}") for i in range(2)]
        y_out = [sem(f"y_out{i}") for i in range(2)]
        k_in = [sem(f"k_in{i}") for i in range(2)]
        base_out = [sem(f"base_out{i}") for i in range(2)]
        base_in = [sem(f"base_in{b}") for b in range(B)]
        scattered = sem("scattered")
        gathered = [[sem(f"gathered{l}_{i}") for i in range((4, 8)[l])] for l in range(LAYERS)]
        out_st = sem("out_st")
        h1_ps, h3_ps = sem("h1_ps"), sem("h3_ps")
        tanh_sb = sem("tanh_sb")
        g_sb = sem("g_sb")
        gT_ps = sem("gT_ps")
        gT_hi, gT_lo = sem("gT_hi"), sem("gT_lo")
        unit_done = sem("unit_done")
        y_added = sem("y_added")
        y_copied = sem("y_copied")
        xT_ps, xT_sb = sem("xT_ps"), sem("xT_sb")
        x_hi, x_lo = sem("x_hi"), sem("x_lo")
        bT_sb = sem("bT_sb")
        logits = sem("logits")
        xnew = sem("xnew")
        xcopied = sem("xcopied")
        exp_k, exp_u = sem("exp_k"), sem("exp_u")
        min_k, min_u = sem("min_k"), sem("min_u")
        kv, ukv = sem("kv"), sem("ukv")
        den_sum, num_sum = sem("den_sum"), sem("num_sum")
        den, num = sem("den"), sem("num")
        wkv = sem("wkv")
        step = sem("step")
        astep = sem("astep")
        rt_dve, rt_act, rt_pe = sem("rt_dve"), sem("rt_act"), sem("rt_pe")
        routed = sem("routed")
        act_on, pool_on, pe_on = sem("act_on"), sem("pool_on"), sem("pe_on")

        U = [0, 2 * NT + SLOTS[0]]
        X = [0, 2 * NT + SLOTS[0]]
        V = [0, NT + SLOTS[0]]
        W = [0, 3 * NP]

        def static_buffer(m):
            return WC if m // NP % 3 == 1 else 0

        PARTS = {0: (("fin", 1),), 1: (("x", 0),), 2: (("fin", 2),), 3: (("x", 1),), 4: (("fin", 3),),
                 5: (("x", 2),), 7: (("fin", 4), ("x", 3))}
        LAST = {0: (("fin", 1), ("fin", 2), ("fin", 3))}
        AHEAD = 5

        def parts(b, k):
            table = LAST if isinstance(b, int) and b == B - 1 else PARTS
            before_k = sum(len(table.get(i, ())) for i in range(k))
            return [(kind, j, b * 8 + (AHEAD + before_k + n)) for n, (kind, j) in enumerate(table.get(k, ()))]

        block = ctx.enter_context(nc.Block())

        @block.sync
        def _(sp):
            def load_x(t, par):
                sp.dma_start(xin[par][:, :], x[ds(t * P, P), :]).then_inc(x_in[par], 16)

            def load_w(l, e, p):
                lo, hi = PIECES[p]
                sp.dma_start(raw[:, lo:hi], wts[l][ds(e, 1), :, lo:hi].rearrange("e p n -> (e p) n")).then_inc(dw_in[p], 16)

            def load_slot(l, s, par):
                sp.dma_start(xs[par], slot_x[ds(s * P, P), :]).then_inc(xs_in[par], 16)

            def store_y(l, s, par):
                sp.wait_ge(y_copied, (SLOTS[0] if l else 0) + s + 1)
                sp.dma_start(slot_y[l][ds(s * P, P), :], yb[par][:, :]).then_inc(y_out[par], 16)

            def part(l, kind, t, j, q):
                if kind == "fin":
                    sp.wait_ge(xT_sb, q + (2 * NT * l + 1))
                    sp.dma_start(base_d[ds(t * P, P), :], btok[j % 2][:, :]).then_inc(base_out[j % 2], 16)
                elif l == 0 and not (isinstance(t, int) and t + 2 >= NT):
                    sp.wait_ge(xT_sb, q + 1)
                    load_x(t + 2, j % 2)

            def batch(l, b):
                for k in range(8):
                    for kind, j, q in parts(b, k):
                        part(l, kind, b * 4 + (j if kind == "fin" else 4 + j), j, q)

            def load_base(l, b, sem_b):
                for par in range(2):
                    sp.wait_ge(base_out[par], b * 32 + (16 * (NT // 2) * l + 48))
                sp.dma_start(ratio[:, ds(b, 1), :, :].rearrange("p a c t -> p (a c) t"),
                             base_d[ds(b * T, T), :].rearrange("(t p) n -> p t n", p=P)).then_inc(sem_b, 16)

            for l in range(LAYERS):
                E, NS = EXPERTS[l], SLOTS[l]
                if l == 0:
                    for par in range(2):
                        sp.sem_inc(base_out[par], 16)
                    sp.dma_start(condb, cond.rearrange("p (b n) -> p b n", b=B)).then_inc(wkv_p_in, 16)
                    sp.dma_start(wl[:, :, :], wdec.rearrange("p (l c) -> p l c", l=LAYERS)).then_inc(wkv_p_in, 16)
                    sp.dma_start(ul[:, :], ub).then_inc(wkv_p_in, 16)
                    for p in range(NP):
                        load_w(l, E, p)
                    for t in range(2):
                        load_x(t, t)
                    for i in range(2):
                        sp.dma_start(gw[i][:, :, :], gates[i].rearrange("p (c e) -> p c e", c=C)).then_inc(params_in, 16)
                        sp.dma_start(biasb[i][:, :], bias[i]).then_inc(params_in, 16)
                    sp.dma_start(scaleb[:, :], scale1).then_inc(params_in, 16)
                else:
                    sp.wait_ge(raw_free, NP)
                    for p in range(NP):
                        load_w(l, E, p)
                for t in range(4):
                    part(l, "x", t, t, t)
                    if t == (1, 0)[l]:
                        for p in range(NP):
                            sp.wait_ge(dw_lo, W[l] + p + 1)
                            load_w(l, E + 1, p)
                if l == 0:
                    for b in range(B):
                        sp.dma_start(xacc[:, 4 * b:4 * b + 4, :],
                                     x[b * T:(b + 1) * T, :].rearrange("(t p) n -> p t n", p=P)).then_inc(xacc_in, 16)
                part(l, "fin", 0, 0, 4)
                with sp.Fori(0, B - 2) as b:
                    batch(l, b)
                for b in range(B - 2, B):
                    batch(l, b)
                for b in range(B):
                    load_base(l, b, base_in[b])
                sp.wait_ge(routed, l + 1)
                first = sp.value_load(chosen[0:1, 0:1], min_val=0, max_val=E - 1)
                sp.wait_ge(dw_lo, W[l] + 2 * NP)
                for p in range(NP):
                    load_w(l, first, p)
                sp.wait_ge(scattered, 16 * K * NT * (l + 1))
                for s in range(2):
                    load_slot(l, s, s)
                def next_slot(s, par):
                    sp.wait_ge(xT_ps, s + (X[l] + 2 * NT + 1))
                    load_slot(l, s + 2, par)

                for s in range(2):
                    next_slot(s, s)
                with sp.Fori(0, NS // 2 - 2) as i:
                    for par in range(2):
                        next_slot(2 * i + (2 + par), par)
                        store_y(l, 2 * i + par, par)
                for s in range(NS - 4, NS):
                    store_y(l, s, s % 2)
            with sp.Fori(0, NT // 2) as i:
                for par in range(2):
                    t = 2 * i + par
                    sp.wait_ge(xnew, NT + t + 1)
                    sp.dma_start(out[ds(t * P, P), :], xacc[:, ds(t, 1), :].rearrange("p a n -> p (a n)")).then_inc(out_st, 16)
            sp.wait_ge(out_st, 16 * NT)

        @block.gpsimd
        def _(pool):
            nc.gpsimd.memset(ones[:, :], 1.0).then_inc(consts, 1)
            nc.gpsimd.memset(ident[:, :], 0.0).then_inc(consts, 1)
            for n in range(2):
                pool.dma_start(kb[n][:, :], kt[n, :, :]).then_inc(k_in[n], 16)

            def load_w(l, e, p, loaded):
                lo, hi = PIECES[p]
                pool.dma_start(raw[:, lo:hi], wts[l][ds(e, 1), :, lo:hi].rearrange("e p n -> (e p) n")).then_inc(loaded[p], 16)

            pool.wait_ge(consts, 2)
            nc.gpsimd.affine_select(out=ident[:, :], in_=ident[:, :], compare_op=ALU.not_equal, fill=1.0, base=0,
                                    pattern=[[-1, P]], channel_multiplier=1).then_inc(consts, 1)
            nc.gpsimd.affine_select(out=before[:, :], in_=ones[:, :], compare_op=ALU.is_gt, fill=0.0, base=0,
                                    pattern=[[1, P]], channel_multiplier=-1).then_inc(consts, 1)

            def iota(dst, pattern, base=0):
                nc.gpsimd.iota(dst, pattern, base=base, channel_multiplier=0,
                               allow_small_or_imprecise_dtypes=True).then_inc(consts, 1)
            iota(iota_e[:, :], [[1, EM]])
            iota(rows_j[:, :], [[P, NT]])
            iota(iota_s[:, :], [[1, SM]], 1)
            iota(seg[:, :, :], [[0, EM], [1, NT]])

            def clamp(n, par):
                pool.wait_ge(exp_k, n + 1)
                pool.sem_inc(pool_on, 1)
                nc.gpsimd.tensor_scalar(ek[par][:, :], ek[par][:, :], E30, None, ALU.min).then_inc(min_k, 1)
                pool.wait_ge(exp_u, n + 1)
                pool.sem_inc(pool_on, 1)
                nc.gpsimd.tensor_scalar(euk[par][:, :], euk[par][:, :], E30, None, ALU.min).then_inc(min_u, 1)

            def products(n, par, load=True):
                pool.wait_ge(min_k, n + 1)
                if not (isinstance(n, int) and n == 0):
                    pool.wait_ge(wkv, n)
                nc.gpsimd.tensor_tensor(ekv[:, :], ek[par][:, :], kb[par][:, :], ALU.mult).then_inc(kv, 1)
                pool.wait_ge(min_u, n + 1)
                nc.gpsimd.tensor_tensor(eukv[:, :], euk[par][:, :], kb[par][:, :], ALU.mult).then_inc(ukv, 1)
                if load:
                    pool.wait_ge(ukv, n + 1)
                    pool.wait_ge(kv, n + 1)
                    pool.dma_start(kb[par][:, :], kt[ds(n + 2, 1), :, :].rearrange("n p t -> (n p) t")).then_inc(k_in[par], 16)

            def add_den(n, par):
                pool.wait_ge(min_u, n + 1)
                pool.wait_ge(den_sum, n + 1)
                nc.gpsimd.tensor_tensor(rec[:, :], rec[:, :], euk[par][:, :], ALU.add).then_inc(den, 1)

            def add_num(n):
                pool.wait_ge(num_sum, n + 1)
                pool.wait_ge(ukv, n + 1)
                nc.gpsimd.tensor_tensor(fwd[:, :], fwd[:, :], eukv[:, :], ALU.add).then_inc(num, 1)

            def load_ahead(l, s, pieces):
                changed = pool.value_load(tab[0:1, CHANGED, ds(s, 1)])
                with pool.If(changed > 0):
                    o = pool.value_load(tab[0:1, ORD, ds(s, 1)], min_val=0, max_val=EM - 1)
                    e = pool.value_load(chosen[0:1, ds(o + 2, 1)], min_val=0, max_val=EXPERTS[l] - 1)
                    for p in pieces:
                        pool.wait_ge(ex_lo[l], o * NP + (p + 2))
                        pool.sem_inc(pool_on, 1)
                        load_w(l, e, p, ex_in[l])

            def scatter(l, t):
                pool.wait_ge(base_in[t // 4], 16 * (l + 1))
                for j in range(K):
                    nc.gpsimd.indirect_dma_start(slot_x[:, :], bass.IndirectOffsetOnAxis(ap=pos[j][:, t:t + 1], axis=0),
                                                 bases[:, t, :], None).then_inc(scattered, 16)

            def gather(l, t):
                deep = len(gathered[l])
                if t >= deep:
                    pool.wait_ge(xnew, NT * l + t - deep + 1)
                for j in range(K):
                    nc.gpsimd.indirect_dma_start(results(l, t, j, t % deep), None, slot_y[l][:, :],
                                                 bass.IndirectOffsetOnAxis(ap=pos[j][:, t:t + 1], axis=0)
                                                 ).then_inc(gathered[l][t % deep], 16)

            clamp(0, 0)
            for c in range(C):
                products(c, c % 2)
                add_den(c, c % 2)
                add_num(c)
                clamp(c + 1, (c + 1) % 2)
            with pool.Fori(0, B - 1) as b:
                for c in range(C):
                    products(b * C + C + c, c % 2)
                    add_den(b * C + C + c, c % 2)
                    add_num(b * C + C + c)
                    clamp(b * C + (C + 1 + c), (c + 1) % 2)
                    pool.dma_start(slot_x[ds((b * C + c) * T, T), :], x[c % B * T:(c % B + 1) * T, :]).then_inc(filled_x, 16)
            for l in range(LAYERS):
                NS = SLOTS[l]
                if l == 0:
                    pool.wait_ge(filled_x, 16 * (B - 1) * C)
                pool.wait_ge(routed, l + 1)
                for t in range(NT):
                    scatter(l, t)
                pool.wait_ge(dw_lo, W[l] + 3 * NP)
                e = pool.value_load(chosen[0:1, 1:2], min_val=0, max_val=EXPERTS[l] - 1)
                for p in range(NP):
                    load_w(l, e, p, ex_in[l])
                first = 0
                load_ahead(l, 0, UP_PIECES)
                if l == 0:
                    for s in range(2):
                        load_ahead(l, s, DOWN_PIECES)
                        load_ahead(l, s + 1, UP_PIECES)

                    def pair(s, n, par, load=True):
                        load_ahead(l, s, DOWN_PIECES)
                        products(n, par, load)
                        add_den(n, par)
                        load_ahead(l, s + 1, UP_PIECES)
                        load_ahead(l, s + 1, DOWN_PIECES)
                        add_num(n)
                        if load or par == 0:
                            clamp(n + 1, 1 - par)
                        load_ahead(l, s + 2, UP_PIECES)

                    with pool.Fori(0, NW // 4 - 1) as i:
                        for j in range(2):
                            pair(i * 4 + (2 + 2 * j), 2 * i + (NW // 2 + j), j)
                    for j in range(2):
                        pair(NW - 2 + 2 * j, NW - 2 + j, j, load=False)
                    first = 2 + NW
                with pool.Fori(first, NS - 1) as s:
                    load_ahead(l, s, DOWN_PIECES)
                    load_ahead(l, s + 1, UP_PIECES)
                load_ahead(l, NS - 1, DOWN_PIECES)
                o = pool.value_load(tab[0:1, ORD, NS - 1:NS], min_val=0, max_val=EM - 1)
                for p in range(NP):
                    pool.wait_ge(ex_in[l][p], o * 16 + 32)
                    pool.sem_inc(raw_free, 1)
                for par in range(2):
                    pool.wait_ge(y_out[par], 16 * (sum(SLOTS[:l + 1]) // 2))
                if l == 0:
                    pool.wait_ge(wkv, NW)
                for t in range(NT):
                    gather(l, t)

        @block.scalar
        def _(act):
            def exps(n, par):
                act.wait_ge(k_in[par], 16 * (n // 2 + 1) if isinstance(n, int) else n * 8 + (16 - 8 * par))
                if not (isinstance(n, int) and n < 2):
                    act.wait_ge(wkv, n - 1)
                nc.scalar.activation(ek[par][:, :], kb[par][:, :], ACT.Exp).then_inc(exp_k, 1)
                nc.scalar.activation(euk[par][:, :], kb[par][:, :], ACT.Exp, bias=ul[:, ds(n, 1)]).then_inc(exp_u, 1)

            def part(l, kind, t, j, q):
                if kind == "x":
                    if l:
                        act.wait_ge(xnew, t + 1)
                        nc.scalar.activation(xacc[:, ds(t, 1), :].rearrange("p a n -> p (a n)"), xin[j % 2][:, :], ACT.Copy).then_inc(xcopied, 1)
                    act.wait_ge(xT_ps, q + (X[l] + 1))
                    if not (isinstance(t, int) and t < 4):
                        act.wait_ge(x_lo, t + (V[l] - 3))
                    nc.scalar.activation(bT[j], XT[:, :], ACT.Tanh, scale=0.5).then_inc(xT_sb, 1)
                else:
                    act.wait_ge(xT_ps, q + (X[l] + 1))
                    par = j % 2
                    if isinstance(t, int) and t < 2:
                        if l:
                            act.wait_ge(y_out[par], 16 * (SLOTS[0] // 2))
                    else:
                        act.wait_ge(base_out[par], (t - par) * 8 + (16 * l * (NT // 2) + 16))
                    nc.scalar.activation(btok[par][:, :], XT[:, :], ACT.Copy).then_inc(xT_sb, 1)

            def split_tile(l, t, j):
                act.wait_ge(bT_sb, t + (NT * l + 1))
                if not (isinstance(t, int) and t < 2):
                    act.wait_ge(h3_ps, t * 2 + (U[l] - 1))
                elif l:
                    act.wait_ge(h3_ps, U[l])
                nc.scalar.activation(xTh[j % 2][:, :], bT[j % 4], ACT.Copy).then_inc(x_hi, 1)

            def tanh(u, par):
                act.wait_ge(h1_ps, u + 1)
                nc.scalar.activation(g[par][:, 0:F], h1[par][:, 0:F], ACT.Tanh, scale=0.5).then_inc(tanh_sb, 1)

            def split_g(u):
                act.wait_ge(gT_ps, u + 1)
                nc.scalar.activation(gTh[:, :], GT[:, 0:FC * P], ACT.Copy).then_inc(gT_hi, 1)

            def split_slot(l, s, par):
                act.wait_ge(xT_ps, s + (X[l] + 2 * NT + 1))
                if isinstance(s, int) and s == 0:
                    act.wait_ge(h3_ps, U[l] + 2 * NT - 2)
                else:
                    act.wait_ge(h3_ps, s + (U[l] + 2 * NT - 1))
                nc.scalar.activation(xTh[par][:, :], XT[:, :], ACT.Copy).then_inc(x_hi, 1)

            def copy_y(l, s, par, first=False):
                act.wait_ge(unit_done, U[l] + 2 * NT + s + 1)
                if first:
                    act.wait_ge(base_out[par], 16 * (NT // 2) * (l + 1) + 16)
                else:
                    act.wait_ge(y_out[par], 16 * (l * SLOTS[0] // 2) + 8 * (s - par))
                nc.scalar.activation(yb[par][:, :], Y[:, :], ACT.Copy).then_inc(y_copied, 1)

            def static_hi(m):
                p, (lo, hi), at = m % NP, PIECES[m % NP], static_buffer(m)
                act.wait_ge(dw_in[p], 16 * (m // NP + 1))
                nc.scalar.activation(w_hi[:, at + lo:at + hi], raw[:, lo:hi], ACT.Copy).then_inc(dw_hi, 1)

            def changed(s):
                return act.value_load(tab[0:1, CHANGED, ds(s, 1)])

            def split_w(l, s, pieces, is_changed):
                with act.If(is_changed > 0):
                    o = act.value_load(tab[0:1, ORD, ds(s, 1)], min_val=0, max_val=EM - 1)
                    at = act.value_load(tab[0:1, OTHER, ds(s, 1)], min_val=0, max_val=WC)
                    for p in pieces:
                        lo, hi = PIECES[p]
                        act.wait_ge(ex_in[l][p], o * 16 + 16)
                        act.sem_inc(act_on, 1)
                        nc.scalar.activation(w_hi[:, ds(at + lo, hi - lo)], raw[:, lo:hi], ACT.Copy).then_inc(ex_hi[l], 1)

            act.wait_ge(wkv_p_in, 48)
            nc.scalar.activation(wl[:, :, :], wl[:, :, :], ACT.Exp).then_inc(astep, 1)
            act.wait_ge(astep, 1)
            nc.scalar.activation(wl[:, :, :], wl[:, :, :], ACT.Exp, scale=-1.0).then_inc(astep, 1)
            act.wait_ge(step, 1)
            nc.scalar.activation(tf[:, :], tf[:, :], ACT.Tanh, scale=0.5).then_inc(astep, 1)
            for n in range(2):
                exps(n, n)
            for l in range(LAYERS):
                NS = SLOTS[l]
                if l:
                    act.wait_ge(unit_done, U[l])
                    for m in range(NP):
                        static_hi(W[l] + m)
                    for t in range(4):
                        part(l, "x", t, t, t)
                else:
                    for m in range(NP):
                        static_hi(m)
                    exps(2, 0)
                    for t in range(2):
                        part(l, "x", t, t, t)
                    for m in range(NP, 2 * NP - 1):
                        static_hi(m)
                    exps(3, 1)
                    for t in range(2, 4):
                        part(l, "x", t, t, t)
                    static_hi(2 * NP - 1)
                    exps(4, 0)
                split_tile(l, 0, 0)
                part(l, "fin", 0, 0, 4)
                tanh(U[l], 0)
                if l:
                    for m in range(NP, 2 * NP):
                        static_hi(W[l] + m)

                def batch(b):
                    for k in range(8):
                        u = b * 8 + (U[l] + k)
                        last = isinstance(b, int)
                        todo = parts(b, k)
                        if k == 7 and not last:
                            split_tile(l, b * 4 + 4, 4)
                        split_g(u)
                        if k in (0, 2, 4):
                            split_tile(l, b * 4 + (1 + k // 2), 1 + k // 2)
                        if k == 7 and not last:
                            kind, j, q = todo[0]
                            part(l, kind, b * 4 + 4, j, q)
                        if not (last and k == 7):
                            tanh(u + 1, (k + 1) % 2)
                        for kind, j, q in (todo[1:] if k == 7 else todo):
                            part(l, kind, b * 4 + (j if kind == "fin" else 4 + j), j, q)
                        if l == 0 and k % 2 == 0 and not last:
                            exps(b * C + (C + k // 2 + 1), (k // 2 + 1) % 2)
                        if last and k == 0:
                            route(l)

                def route(l):
                    n = NT * EXPERTS[l]
                    act.wait_ge(rt_dve, 2 * l + 1)
                    if l == 0:
                        nc.scalar.activation(rB[:, 0:n], rA[:, 0:n], ACT.Tanh, scale=0.5).then_inc(rt_act, 1)
                    else:
                        nc.scalar.activation(rB[:, 0:n].rearrange("p (t e) -> p t e", t=NT),
                                             rA[:, 0:2 * n].rearrange("p (t e) -> p t e", t=NT)[:, :, EM:], ACT.Tanh, scale=0.5).then_inc(rt_act, 1)
                        act.wait_ge(rt_dve, 5)
                        nc.scalar.activation(rB[:, 0:n], rB[:, 0:n], ACT.Exp).then_inc(rt_act, 1)

                with act.Fori(0, B - 1) as b:
                    batch(b)
                batch(B - 1)
                act.wait_ge(unit_done, U[l] + 2 * NT - 1)
                for m in range(2 * NP, 3 * NP):
                    static_hi(W[l] + m)
                for s in range(2):
                    split_slot(l, s, s)
                u0 = U[l] + 2 * NT
                tanh(u0, 0)

                def slot(s, par, up=True, ahead=True, first=False):
                    here = changed(s)
                    if up:
                        next_one = changed(s + 1)
                    split_g(s + u0)
                    split_w(l, s, DOWN_PIECES, here)
                    if up:
                        tanh(s + (u0 + 1), 1 - par)
                        split_w(l, s + 1, UP_PIECES[:1], next_one)
                    if ahead:
                        split_slot(l, s + 2, par)
                    if up:
                        split_w(l, s + 1, UP_PIECES[1:], next_one)
                    copy_y(l, s, par, first)

                split_w(l, 0, UP_PIECES, changed(0))
                for s in range(2):
                    slot(s, s, first=True)
                if l == 0:
                    with act.Fori(0, NW // 4 - 1) as i:
                        for k in range(4):
                            slot(i * 4 + (2 + k), k % 2)
                            if k % 2 == 0:
                                exps(i * 2 + (NW // 2 + 1 + k // 2), (k // 2 + 1) % 2)
                    for k in range(4):
                        slot(2 + NW - 4 + k, k % 2)
                        if k == 0:
                            exps(NW - 1, 1)
                    done = 2 + NW
                else:
                    done = 2
                with act.Fori(done // 2, NS // 2 - 1) as i:
                    for k in range(2):
                        slot(i * 2 + k, k)
                slot(NS - 2, 0, ahead=False)
                slot(NS - 1, 1, up=False, ahead=False)

        @block.vector
        def _(dve):
            done = {"n": 0}

            def link(ins):
                done["n"] += 1
                ins.then_inc(step, 1)
                dve.wait_ge(step, done["at"] + done["n"])

            done["at"] = 0

            def enter(i, per_round):
                done["base"], done["outer"], done["n"] = done["n"], done["at"], 0
                done["at"] = i * per_round + done["base"]

            def leave(rounds, per_round):
                assert done["n"] == per_round, done["n"]
                done["at"], done["n"] = done["outer"], done["base"] + rounds * per_round

            flat_dec = dec[:, :, :, :].rearrange("p l b c -> p (l b c)")
            flat_osc = osc[:, :, :, :].rearrange("p l b c -> p (l b c)")
            flat_ratio = ratio[:, :, :, :].rearrange("p b c t -> p (b c t)")

            WKV_LINKS = 5

            def wkv_part(n, par, q, part):
                dec_n, osc_n = flat_dec[:, ds(n, 1)], flat_osc[:, ds(n, 1)]
                if part in (1, 3):
                    src = ek[par] if part == 1 else ekv
                    if part == 1:
                        if not (isinstance(n, int) and n == 0):
                            dve.wait_ge(wkv, n)
                        dve.wait_ge(min_k, n + 1)
                    else:
                        dve.wait_ge(den_sum, n + 1)
                        dve.wait_ge(kv, n + 1)
                    nc.vector.tensor_tensor_scan(fwd[:, :], dec_n.to_broadcast([P, T]), src[:, :], 0.0, ALU.mult, ALU.add)
                    link(nc.vector.tensor_tensor_scan(bwd[:, 0:T][:, ::-1], dec_n.to_broadcast([P, T]),
                                                      src[:, ::-1], 0.0, ALU.mult, ALU.add))
                elif part == 2:
                    nc.vector.scalar_tensor_tensor(rec[:, :], bwd[:, 1:T + 1], dec_n, fwd[:, :], ALU.mult, ALU.add).then_inc(den_sum, 1)
                elif part == 4:
                    nc.vector.scalar_tensor_tensor(fwd[:, :], bwd[:, 1:T + 1], dec_n, fwd[:, :], ALU.mult, ALU.add).then_inc(num_sum, 1)
                elif part in (5, 6):
                    if part == 5:
                        dve.wait_ge(den, n + 1)
                        link(nc.vector.tensor_scalar(rec[:, :], rec[:, :], 1e-8, None, ALU.max))
                    half = slice((part - 5) * T // 2, (part - 4) * T // 2)
                    link(nc.vector.reciprocal(rec[:, half], rec[:, half]))
                else:
                    dve.wait_ge(num, n + 1)
                    nc.vector.scalar_tensor_tensor(flat_ratio[:, ds(q * T, T)], fwd[:, :], osc_n, rec[:, :],
                                                   ALU.mult, ALU.mult).then_inc(wkv, 1)

            def finish(l, t, b, j):
                dve.wait_ge(xT_sb, use_x(t, b, j) + (2 * NT * l + 1))
                if l == 0:
                    dve.wait_ge(wkv, b * C + C)
                else:
                    dve.wait_ge(wkv, NW)
                nc.vector.scalar_tensor_tensor(bT[j].rearrange("p (c t) -> p c t", c=C), bT[j].rearrange("p (c t) -> p c t", c=C), 1.0,
                                               ratio[:, ds(b, 1), :, j * P:(j + 1) * P].rearrange("p a c t -> p (a c) t"),
                                               ALU.add, ALU.mult).then_inc(bT_sb, 1)

            def use_x(t, b, j):
                if isinstance(t, int) and t < 4:
                    return t
                return (b - 1) * 8 + (AHEAD + (1, 3, 5, 7)[j])

            def split_tile(l, t, j):
                dve.wait_ge(x_hi, t + (V[l] + 1))
                nc.vector.tensor_tensor(xTl[j % 2][:, :], bT[j % 4], xTh[j % 2][:, :].bitcast(f32), ALU.subtract).then_inc(x_lo, 1)

            def split_slot(l, s, par):
                dve.wait_ge(x_hi, s + (V[l] + NT + 1))
                nc.vector.tensor_tensor(xTl[par][:, :], XT[:, :], xTh[par][:, :].bitcast(f32), ALU.subtract).then_inc(x_lo, 1)

            def split_g(u):
                dve.wait_ge(gT_hi, u + 1)
                nc.vector.tensor_tensor(gTl[:, :], GT[:, 0:FC * P], gTh[:, :].bitcast(f32), ALU.subtract).then_inc(gT_lo, 1)

            def static_lo(m):
                p, (lo, hi), at = m % NP, PIECES[m % NP], static_buffer(m)
                dve.wait_ge(dw_hi, m + 1)
                nc.vector.tensor_tensor(w_lo[:, at + lo:at + hi], raw[:, lo:hi],
                                        w_hi[:, at + lo:at + hi].bitcast(f32), ALU.subtract).then_inc(dw_lo, 1)

            def changed(s):
                return dve.value_load(tab[0:1, CHANGED, ds(s, 1)])

            def split_w(l, s, pieces, is_changed):
                with dve.If(is_changed > 0):
                    o = dve.value_load(tab[0:1, ORD, ds(s, 1)], min_val=0, max_val=EM - 1)
                    at = dve.value_load(tab[0:1, OTHER, ds(s, 1)], min_val=0, max_val=WC)
                    for p in pieces:
                        lo, hi = PIECES[p]
                        dve.wait_ge(ex_hi[l], o * NP + (p + 1))
                        nc.vector.tensor_tensor(w_lo[:, ds(at + lo, hi - lo)], raw[:, lo:hi],
                                                w_hi[:, ds(at + lo, hi - lo)].bitcast(f32), ALU.subtract).then_inc(ex_lo[l], 1)

            def gate(u, par):
                dve.wait_ge(tanh_sb, u + 1)
                link(nc.vector.scalar_tensor_tensor(g[par][:, 0:F], g[par][:, 0:F], 1.0, h1[par][:, 0:F], ALU.add, ALU.mult))
                dve.wait_ge(h3_ps, u + 1)
                nc.vector.scalar_tensor_tensor(g[par][:, 0:F], g[par][:, 0:F], 0.5, h3[par][:, 0:F], ALU.mult, ALU.mult).then_inc(g_sb, 1)

            def add_shared(l, t):
                dve.wait_ge(unit_done, U[l] + 2 * t + 2)
                if l == 0:
                    dve.wait_ge(xacc_in, 16 * B)
                else:
                    dve.wait_ge(xcopied, t + 1)
                acc = xacc[:, ds(t, 1), :].rearrange("p a n -> p (a n)")
                nc.vector.tensor_tensor(acc, acc, Y[:, :], ALU.add).then_inc(y_added, 1)

            def combine(l, t, j, transposed=None):
                acc = xacc[:, ds(t, 1), :].rearrange("p a n -> p (a n)")
                deep = len(gathered[l])
                dve.wait_ge(gathered[l][j], (t - j) * (16 * K // deep) + 16 * K)
                if l == 0:
                    if not (isinstance(t, int) and t < 2):
                        dve.wait_ge(xcopied, t - 1)
                        dve.wait_ge(xT_ps, transposed + (X[1] + 1))
                dve.wait_ge(y_added, NT * (l + 1) + 1)
                link(nc.vector.scalar_tensor_tensor(acc, results(l, t, 0, j), wsel[0][:, ds(t, 1)], acc, ALU.mult, ALU.add))
                nc.vector.scalar_tensor_tensor(acc if l else xin[j % 2][:, :], results(l, t, 1, j), wsel[1][:, ds(t, 1)], acc,
                                               ALU.mult, ALU.add).then_inc(xnew, 1)

            def route_choose(l):
                E = EXPERTS[l]
                n = NT * E
                v3 = lambda a: a[:, 0:n].rearrange("p (t e) -> p t e", t=NT)
                wide = lambda a: a[:, :].rearrange("p (t a) -> p t a", a=1).to_broadcast([P, NT, E])
                row = lambda a: a[:, 0:E].rearrange("p (a e) -> p a e", a=1).to_broadcast([P, NT, E])
                dve.wait_ge(logits, NT * (l + 1))
                if l == 0:
                    nc.vector.tensor_copy(rA[:, 0:n], LG[:, 0:n]).then_inc(rt_dve, 1)
                    dve.wait_ge(rt_act, 1)
                    link(nc.vector.tensor_scalar(v3(rB), v3(rB), 0.5, 0.5, ALU.mult, ALU.add))
                    link(nc.vector.tensor_tensor(v3(rA), v3(rB), row(biasb[0]), ALU.add))
                else:
                    dve.wait_ge(xcopied, NT)
                    both3 = rA[:, 0:2 * n].rearrange("p (t e) -> p t e", t=NT)
                    nc.vector.tensor_copy(rA[:, 0:2 * n], LG[:, 0:2 * n]).then_inc(rt_dve, 1)
                    dve.wait_ge(rt_act, 2)
                    link(nc.vector.scalar_tensor_tensor(v3(rB), v3(rB), 1.0, both3[:, :, E:], ALU.add, ALU.mult))
                    link(nc.vector.scalar_tensor_tensor(v3(rB), v3(rB), 0.5, both3[:, :, 0:E], ALU.mult, ALU.mult))
                    link(nc.vector.scalar_tensor_tensor(rB[:, 0:n], rB[:, 0:n], -1.0, rB[:, 0:n], ALU.mult, ALU.max))
                    link(nc.vector.tensor_reduce(m16[0][:, :], v3(rB), AX.X, ALU.max))
                    nc.vector.tensor_tensor(v3(rB), v3(rB), wide(m16[0]), ALU.subtract).then_inc(rt_dve, 2)
                    dve.wait_ge(rt_act, 3)
                    link(nc.vector.tensor_reduce(m16[0][:, :], v3(rB), AX.X, ALU.add))
                    link(nc.vector.reciprocal(m16[1][:, :], m16[0][:, :]))
                    link(nc.vector.tensor_tensor(v3(rB), v3(rB), wide(m16[1]), ALU.mult))
                    link(nc.vector.tensor_tensor(v3(rA), v3(rB), row(biasb[1]), ALU.add))
                    link(nc.vector.tensor_tensor(v3(rC), v3(rB), row(scaleb), ALU.mult))
                    link(nc.vector.tensor_scalar(rB[:, 0:n], rC[:, 0:n], 1.0, None, ALU.add))
                for j in range(K):
                    link(nc.vector.tensor_reduce(m16[0][:, :], v3(rA), AX.X, ALU.max))
                    link(nc.vector.tensor_tensor(v3(rC), v3(rA), wide(m16[0]), ALU.is_equal))
                    link(nc.vector.tensor_scalar(v3(rC), v3(rC), -float(EM), float(EM), ALU.mult, ALU.add))
                    link(nc.vector.tensor_tensor(v3(rC), v3(rC), row(iota_e), ALU.add))
                    link(nc.vector.tensor_reduce(m16[1][:, :], v3(rC), AX.X, ALU.min))
                    link(nc.vector.tensor_tensor(v3(oh[j]), row(iota_e), wide(m16[1]), ALU.is_equal))
                    if j + 1 < K:
                        link(nc.vector.scalar_tensor_tensor(v3(rA), v3(oh[j]), -3e38, v3(rA), ALU.mult, ALU.add))
                    link(nc.vector.tensor_tensor(v3(rC), v3(oh[j]), v3(rB), ALU.mult))
                    link(nc.vector.tensor_reduce(wsel[j][:, :], v3(rC), AX.X, ALU.add))
                if l == 0:
                    link(nc.vector.tensor_tensor(m16[0][:, :], wsel[0][:, :], wsel[1][:, :], ALU.add))
                    link(nc.vector.tensor_scalar(m16[0][:, :], m16[0][:, :], 1e-12, None, ALU.max))
                    link(nc.vector.reciprocal(m16[1][:, :], m16[0][:, :]))
                    nc.vector.tensor_tensor(wsel[0][:, :], wsel[0][:, :], m16[1][:, :], ALU.mult)
                    link(nc.vector.tensor_tensor(wsel[1][:, :], wsel[1][:, :], m16[1][:, :], ALU.mult))
                nc.vector.tensor_tensor(v3(both), v3(oh[0]), v3(oh[1]), ALU.add).then_inc(rt_dve, 1)

            def route_place(l):
                E, NS = EXPERTS[l], SLOTS[l]
                te = lambda a: a[:, 0:NT * E].rearrange("p (t e) -> p t e", t=NT)
                et = lambda a: a[:, 0:NT * E].rearrange("p (e t) -> p e t", e=E)
                swap = lambda a: a[:, 0:NT * E].rearrange("p (e t) -> p t e", e=E)
                over = lambda a, n: a[:, 0:E].rearrange("p (a e) -> p a e", a=1).to_broadcast([P, n, E])
                by_slot = lambda n: iota_s[:, 0:n].rearrange("p (s a) -> p s a", a=1).to_broadcast([P, n, E])
                counts, ntiles, ends, filled = cnt
                dve.wait_ge(rt_pe, l + 1)
                link(nc.vector.tensor_copy(et(rA), LG[:, 256:256 + NT * E].rearrange("p (t e) -> p e t", t=NT)))
                link(nc.vector.tensor_tensor_scan(rC[:, 0:NT * E], seg[:, :, :].rearrange("p e t -> p (e t)")[:, 0:NT * E],
                                                  rA[:, 0:NT * E], 0.0, ALU.mult, ALU.add))
                link(nc.vector.tensor_copy(counts[:, 0:E], et(rC)[:, :, NT - 1]))
                link(nc.vector.tensor_tensor(et(rB), counts[:, 0:E].rearrange("p (e a) -> p e a", a=1).to_broadcast([P, E, NT]),
                                             rows_j[:, :].rearrange("p (a t) -> p a t", a=1).to_broadcast([P, E, NT]), ALU.is_gt))
                link(nc.vector.tensor_reduce(ntiles[:, 0:E], et(rB), AX.X, ALU.add))
                link(nc.vector.tensor_tensor_scan(ends[:, 0:E], ones[:, 0:E], ntiles[:, 0:E], 0.0, ALU.mult, ALU.add))
                link(nc.vector.tensor_scalar(counts[:, 0:E], ntiles[:, 0:E], 1.0, None, ALU.min))
                link(nc.vector.tensor_tensor_scan(filled[:, 0:E], ones[:, 0:E], counts[:, 0:E], 0.0, ALU.mult, ALU.add))
                NO = EM + 2
                ro = rD[:, 0:NO * E].rearrange("p (s e) -> p s e", s=NO)
                link(nc.vector.tensor_tensor(ro, by_slot(NO), over(filled, NO), ALU.is_gt))
                link(nc.vector.tensor_reduce(rB[:, 0:NO], ro, AX.X, ALU.add))
                nc.vector.tensor_scalar(chosen[:, :], rB[:, 0:NO], float(E - 1), None, ALU.min)
                rs = rD[:, 0:NS * E].rearrange("p (s e) -> p s e", s=NS)
                link(nc.vector.tensor_tensor(rs, by_slot(NS), over(ends, NS), ALU.is_gt))
                link(nc.vector.tensor_tensor(rs, rs, over(counts, NS), ALU.mult))
                link(nc.vector.tensor_reduce(rB[:, 0:NS], rs, AX.X, ALU.add))
                link(nc.vector.tensor_scalar(filled[:, E - 1:E], filled[:, E - 1:E], -1.0, None, ALU.add))
                order, changed = tabf[:, ORD, 0:NS], tabf[:, CHANGED, 0:NS]
                link(nc.vector.tensor_scalar(order, rB[:, 0:NS], filled[:, E - 1:E], None, ALU.min))
                nc.vector.memset(tabf[:, CHANGED, 0:1], 0.0)
                link(nc.vector.tensor_tensor(tabf[:, CHANGED, 1:NS], tabf[:, ORD, 1:NS], tabf[:, ORD, 0:NS - 1], ALU.subtract))
                link(nc.vector.tensor_scalar(rB[:, 0:NS], changed, -2.0, 1.0, ALU.mult, ALU.add))
                link(nc.vector.tensor_tensor_scan(tabf[:, BUF, 0:NS], rB[:, 0:NS], changed, 0.0, ALU.mult, ALU.add))
                nc.vector.tensor_scalar(tabf[:, OTHER, 0:NS], tabf[:, BUF, 0:NS], -float(WC), float(WC), ALU.mult, ALU.add)
                link(nc.vector.tensor_scalar(rB[:, 0:NS], iota_s[:, 0:NS], ends[:, E - 1:E], None, ALU.is_le))
                link(nc.vector.tensor_scalar(tabf[:, DOWNCODE, 0:NS], order, float(NP), 1.0, ALU.mult, ALU.add))
                link(nc.vector.tensor_scalar(tabf[:, UPCODE, 0:NS], tabf[:, DOWNCODE, 0:NS], float(UPP - NP), 1.0, ALU.add, ALU.max))
                for row in (UPCODE, DOWNCODE):
                    link(nc.vector.scalar_tensor_tensor(tabf[:, row, 0:NS], tabf[:, BUF, 0:NS], float(BUF1), tabf[:, row, 0:NS], ALU.mult, ALU.add))
                    link(nc.vector.tensor_tensor(tabf[:, row, 0:NS], tabf[:, row, 0:NS], rB[:, 0:NS], ALU.mult))
                link(nc.vector.memset(tabf[:, CHANGED, 0:1], 1.0))
                nc.vector.tensor_copy(tab[:, :, 0:NS], tabf[:, 0:BUF, 0:NS])
                link(nc.vector.tensor_tensor(ntiles[:, 0:E], ends[:, 0:E], ntiles[:, 0:E], ALU.subtract))
                link(nc.vector.tensor_tensor(et(rC), et(rC), et(rA), ALU.subtract))
                link(nc.vector.tensor_tensor(te(rB), swap(rC), LG[:, 0:NT * E].rearrange("p (t e) -> p t e", t=NT), ALU.add))
                link(nc.vector.scalar_tensor_tensor(te(rB), over(ntiles, NT), float(P), te(rB), ALU.mult, ALU.add))
                for j in range(K):
                    link(nc.vector.tensor_tensor(te(rC), te(oh[j]), te(rB), ALU.mult))
                    link(nc.vector.tensor_reduce(m16[j][:, :], te(rC), AX.X, ALU.add))
                    last = nc.vector.tensor_copy(pos[j][:, :], m16[j][:, :])
                last.then_inc(routed, 1)

            for started in (y_added, *ex_lo):
                dve.sem_inc(started, 1)
            nc.vector.memset(bwd[:, T:T + 1], 0.0)
            for i in range(2):
                nc.vector.memset(g[i][:, F:FC * P], 0.0)
            dve.wait_ge(wkv_p_in, 48)
            link(nc.vector.tensor_reduce(tf[:, :], condb, AX.X, ALU.add))
            dve.wait_ge(astep, 3)
            link(nc.vector.tensor_scalar(tf[:, :], tf[:, :], 0.5, 0.5, ALU.mult, ALU.add))
            nc.vector.tensor_scalar(dfac[:, :], tf[:, :], 0.5, 0.5, ALU.mult, ALU.add)
            link(nc.vector.tensor_scalar(sfac[:, :], tf[:, :], 0.1, 0.4, ALU.mult, ALU.add))
            over_c = lambda a: a[:, :].rearrange("p (b a) -> p b a", a=1).to_broadcast([P, B, C])
            for l in range(LAYERS):
                nc.vector.tensor_tensor(dec[:, l, :, :], over_c(dfac),
                                        wl[:, l, :].rearrange("p (a c) -> p a c", a=1).to_broadcast([P, B, C]), ALU.mult)
                last = nc.vector.tensor_copy(osc[:, l, :, :], over_c(sfac))
            link(last)
            for c in range(C):
                for part in range(1, 8):
                    wkv_part(c, c % 2, c, part)
                for m in (range(NP), range(NP, 2 * NP - 1), range(2 * NP - 1, 2 * NP), ())[c]:
                    static_lo(m)
                if c == 0:
                    dve.wait_ge(consts, 8)
                    nc.vector.tensor_scalar(seg[:, :, :], seg[:, :, :], 1.0, None, ALU.min)
            turns = [range(2 * i, 2 * (i + 1)) for i in range(14)] + [range(0)] * 2
            for l in range(LAYERS):
                NS = SLOTS[l]
                if l == 0:
                    dve.wait_ge(params_in, 80)
                else:
                    dve.wait_ge(wkv, NW)
                    for m in range(NP):
                        static_lo(W[l] + m)
                    for t in range(4):
                        combine(0, t, t, t - 2)
                finish(l, 0, 0, 0)
                split_tile(l, 0, 0)
                gate(U[l], 0)
                if l:
                    for m in range(NP, 2 * NP):
                        static_lo(W[l] + m)

                def wkv_turn(b, turn):
                    for i in turns[turn]:
                        c = i // 7
                        wkv_part(b * C + (C + c), c % 2, b * C + (C + c), i % 7 + 1)

                def batch(b):
                    last = isinstance(b, int)
                    for k in range(8):
                        u = b * 8 + (U[l] + k)
                        if k == 7 and not last:
                            finish(l, b * 4 + 4, b + 1, 0)
                        split_g(u)
                        if k == 7 and not last:
                            split_tile(l, b * 4 + 4, 4)
                        for kind, j, q in parts(b, k):
                            if kind == "fin" and j < 4:
                                finish(l, b * 4 + j, b, j)
                            elif kind == "x" and l:
                                t = b * 4 + 4 + j
                                combine(0, t, j, (b - 1) * 8 + (AHEAD + (5, 7)[j]) if j < 2 else b * 8 + (AHEAD + (1, 3)[j - 2]))
                        if l == 0 and not last:
                            wkv_turn(b, 2 * k)
                        if not (last and k == 7):
                            gate(u + 1, (k + 1) % 2)
                        if k in (0, 2, 4):
                            split_tile(l, b * 4 + (1 + k // 2), 1 + k // 2)
                        if k % 2:
                            add_shared(l, b * 4 + k // 2)
                        if l == 0 and not last:
                            wkv_turn(b, 2 * k + 1)
                        if last and k == 0:
                            route_choose(l)
                        if last and k == 1:
                            route_place(l)

                per = 8 + (4 * WKV_LINKS if l == 0 else 4)
                with dve.Fori(0, B - 1) as b:
                    enter(b, per)
                    batch(b)
                leave(B - 1, per)
                batch(B - 1)
                for m in range(2 * NP, 3 * NP):
                    static_lo(W[l] + m)
                u0 = U[l] + 2 * NT
                for s in range(2):
                    split_slot(l, s, s)
                gate(u0, 0)

                def slot(s, par, n=None, q=None, first=False, mid=(), end=()):
                    here, next_one = changed(s), changed(s + 1)
                    split_g(s + u0)
                    split_w(l, s, DOWN_PIECES, here)
                    for part in mid:
                        wkv_part(n, first, q, part)
                    gate(s + (u0 + 1), 1 - par)
                    split_w(l, s + 1, UP_PIECES[:1], next_one)
                    if not (isinstance(s, int) and s + 2 >= NS):
                        split_slot(l, s + 2, par)
                    split_w(l, s + 1, UP_PIECES[1:], next_one)
                    for part in end:
                        wkv_part(n, first, q, part)

                split_w(l, 0, UP_PIECES, changed(0))
                for s in range(2):
                    slot(s, s)
                if l == 0:
                    halves_of_unit = (dict(mid=(1,), end=(2, 3, 4)), dict(mid=(5,), end=(6, 7)))
                    per = 4 + 2 * WKV_LINKS
                    with dve.Fori(0, NW // 4 - 1) as i:
                        enter(i, per)
                        for k in range(4):
                            slot(i * 4 + (2 + k), k % 2, i * 2 + (NW // 2 + k // 2), i * 2 + k // 2, k // 2, **halves_of_unit[k % 2])
                    leave(NW // 4 - 1, per)
                    for k in range(4):
                        n = NW - 2 + k // 2
                        slot(2 + NW - 4 + k, k % 2, n, n - NW // 2, k // 2, **halves_of_unit[k % 2])
                    start = 2 + NW
                else:
                    start = 2
                rounds = NS // 2 - 1 - start // 2
                with dve.Fori(0, rounds) as i:
                    enter(i, 2)
                    for k in range(2):
                        slot(i * 2 + (start + k), k)
                leave(rounds, 2)
                slot(NS - 2, 0)
                split_g(NS - 1 + u0)
                split_w(l, NS - 1, DOWN_PIECES, changed(NS - 1))
            for t in range(NT):
                combine(1, t, t % len(gathered[1]))

        @block.tensor
        def _(pe):
            def part(l, kind, t, j, q):
                if isinstance(q, int) and q == 0:
                    if l:
                        pe.wait_ge(x_lo, V[l])
                else:
                    pe.wait_ge(xT_sb, q + 2 * NT * l)
                if kind == "x":
                    par = j % 2
                    if l == 0:
                        pe.wait_ge(x_in[par], (t - par) * 8 + 16)
                    else:
                        pe.wait_ge(xnew, t + 1)
                    src = xin[par]
                else:
                    n = EXPERTS[0] if l == 0 else 2 * EXPERTS[1]
                    pe.wait_ge(bT_sb, t + (NT * l + 1))
                    src = bT[j % 4]
                    for c in range(C):
                        last = nc.tensor.matmul(LG[:, ds(t * n, n)], src[:, c * P:(c + 1) * P], gw[l][:, c, :], start=(c == 0), stop=(c == C - 1))
                    last.then_inc(logits, 1)
                for c in range(C):
                    last = nc.tensor.transpose(XT[:, c * P:(c + 1) * P], src[:, c * P:(c + 1) * P], ident[:, :])
                last.then_inc(xT_ps, 1)

            def up(par, xpar, buf):
                for ps_, off, s in ((h1, 0, h1_ps), (h3, F, h3_ps)):
                    for c in range(C):
                        at = buf * WC + c * 2 * F + off
                        hi, lo = (a[xpar][:, c * P:(c + 1) * P] for a in (xTh, xTl))
                        nc.tensor.matmul(ps_[par][:, 0:F], hi, w_hi[:, at:at + F], start=(c == 0), stop=False)
                        nc.tensor.matmul(ps_[par][:, 0:F], hi, w_lo[:, at:at + F], start=False, stop=False)
                        last = nc.tensor.matmul(ps_[par][:, 0:F], lo, w_hi[:, at:at + F], start=False, stop=(c == C - 1))
                    last.then_inc(s, 1)

            def transpose_g(u, par):
                pe.wait_ge(g_sb, u + 1)
                for j in range(FC):
                    last = nc.tensor.transpose(GT[:, j * P:(j + 1) * P], g[par][:, j * P:(j + 1) * P], ident[:, :])
                last.then_inc(gT_ps, 1)

            def down(u, buf, first, last_of):
                at = lambda j: buf * WC + UP + j * D
                for j in range(FC):
                    hi = gTh[:, j * P:(j + 1) * P]
                    nc.tensor.matmul(Y[:, :], hi, w_hi[:, at(j):at(j) + D], start=(first and j == 0), stop=False)
                    nc.tensor.matmul(Y[:, :], hi, w_lo[:, at(j):at(j) + D], start=False, stop=False)
                pe.wait_ge(gT_lo, u + 1)
                for j in range(FC):
                    last = nc.tensor.matmul(Y[:, :], gTl[:, j * P:(j + 1) * P], w_hi[:, at(j):at(j) + D],
                                            start=False, stop=(last_of and j == FC - 1))
                last.then_inc(unit_done, 1)

            def transpose_slot(l, s, par):
                pe.wait_ge(xs_in[par], 8 * (s - par) + 16 + 16 * (l * SLOTS[0] // 2))
                if isinstance(s, int) and s == 0:
                    pe.wait_ge(xT_sb, 2 * NT * (l + 1))
                else:
                    pe.wait_ge(x_lo, s + (V[l] + NT))
                for c in range(C):
                    last = nc.tensor.transpose(XT[:, c * P:(c + 1) * P], xs[par][:, c * P:(c + 1) * P], ident[:, :])
                last.then_inc(xT_ps, 1)

            pe.wait_ge(consts, 8)
            pe.wait_ge(params_in, 80)
            for l in range(LAYERS):
                NS = SLOTS[l]
                if l:
                    pe.wait_ge(rt_dve, 1)
                for t in range(4):
                    part(l, "x", t, t, t)
                part(l, "fin", 0, 0, 4)

                def weights(n):
                    pe.wait_ge(dw_lo, W[l] + n)

                def shared_up(u, k, t):
                    if k % 2 == 0:
                        pe.wait_ge(x_lo, t + (V[l] + 1))
                    up(k % 2, k // 2 % 2, k % 2)

                def batch(b):
                    last = isinstance(b, int)
                    for k in range(8):
                        u = b * 8 + (U[l] + k)
                        todo = parts(b, k)
                        transpose_g(u, k % 2)
                        if k == 7 and not last:
                            kind, j, q = todo[0]
                            part(l, kind, b * 4 + 4, j, q)
                        if k == 0:
                            weights(NP + UPP)
                        if not (last and k == 7):
                            shared_up(u + 1, k + 1, b * 4 + (k + 1) // 2)
                        if k % 2 == 0:
                            if l and k == 0:
                                pe.wait_ge(y_copied, SLOTS[0])
                            pe.wait_ge(y_added, b * 4 + (NT * l + k // 2 + 1))
                        weights(2 * NP)
                        pe.wait_ge(gT_hi, u + 1)
                        down(u, k % 2, k % 2 == 0, k % 2 == 1)
                        for kind, j, q in (todo[1:] if k == 7 else todo):
                            part(l, kind, b * 4 + (j if kind == "fin" else 4 + j), j, q)
                        if last and k == 1:
                            pe.wait_ge(rt_dve, 2 if l == 0 else 6)
                            n = NT * EXPERTS[l]
                            nc.tensor.matmul(LG[:, 0:n], before[:, :], both[:, 0:n], start=True, stop=True)
                            nc.tensor.matmul(LG[:, 256:256 + n], ones[:, :], both[:, 0:n], start=True, stop=True).then_inc(rt_pe, 1)

                weights(UPP)
                shared_up(U[l], 0, 0)
                with pe.Fori(0, B - 1) as b:
                    batch(b)
                batch(B - 1)

                for s in range(2):
                    transpose_slot(l, s, s)
                u0 = U[l] + 2 * NT

                def load(row, s):
                    return pe.value_load(tab[0:1, row, ds(s, 1)])

                def slot_up(s, par, code):
                    pe.wait_ge(x_lo, s + (V[l] + NT + 1))
                    pe.sem_inc(pe_on, 1)
                    with pe.If(code > BUF1):
                        pe.wait_ge(ex_lo[l], code & (BUF1 - 1))
                        pe.sem_inc(pe_on, 1)
                        up(par, par, 1)
                    with pe.Else():
                        with pe.If(code > 0):
                            pe.wait_ge(ex_lo[l], code & (BUF1 - 1))
                            pe.sem_inc(pe_on, 1)
                            up(par, par, 0)
                        with pe.Else():
                            pe.sem_inc(h1_ps, 1)
                            pe.sem_inc(h3_ps, 1)

                def slot(s, par, ahead=True, first=False):
                    code = load(DOWNCODE, s)
                    if ahead:
                        ahead_code = load(UPCODE, s + 2)
                        transpose_slot(l, s + 2, par)
                    if first:
                        pe.wait_ge(y_added, NT * (l + 1) + 1)
                    else:
                        pe.wait_ge(y_copied, s + SLOTS[0] * l)
                    pe.wait_ge(gT_hi, s + (u0 + 1))
                    with pe.If(code > BUF1):
                        pe.wait_ge(ex_lo[l], code & (BUF1 - 1))
                        pe.sem_inc(pe_on, 1)
                        down(s + u0, 1, True, True)
                    with pe.Else():
                        with pe.If(code > 0):
                            pe.wait_ge(ex_lo[l], code & (BUF1 - 1))
                            pe.sem_inc(pe_on, 1)
                            down(s + u0, 0, True, True)
                        with pe.Else():
                            pe.wait_ge(gT_lo, s + (u0 + 1))
                            pe.sem_inc(unit_done, 1)
                    if not (isinstance(s, int) and s == NS - 1):
                        transpose_g(s + (u0 + 1), 1 - par)
                    if ahead:
                        slot_up(s + 2, par, ahead_code)

                pe.wait_ge(routed, l + 1)
                pe.wait_ge(dw_lo, W[l] + 3 * NP)
                for s in range(2):
                    if s:
                        transpose_g(u0, 0)
                    slot_up(s, s, load(UPCODE, s))
                slot(0, 0, first=True)
                slot(1, 1)
                with pe.Fori(1, NS // 2 - 1) as i:
                    for k in range(2):
                        slot(i * 2 + k, k)
                slot(NS - 2, 0, ahead=False)
                slot(NS - 1, 1, ahead=False)


def pack_experts(up, gate, down):
    e = up.shape[0]
    both = np.concatenate([gate, up], axis=2).reshape(e, C, P, 2 * F).transpose(0, 2, 1, 3).reshape(e, P, UP)
    padded = np.zeros((e, FC * P, D), np.float32)
    padded[:, :F] = down
    low = padded.reshape(e, FC, P, D).transpose(0, 2, 1, 3).reshape(e, P, FC * D)
    return np.ascontiguousarray(np.concatenate([both, low], axis=2))


def kernel(x, fside_BxSxS_0, cond_512, L0_cond_w, L0_cond_u, L0_ffn_gate_w, L0_ffn_router_bias, L0_ffn_W1,
           L0_ffn_W3, L0_ffn_W2, L0_ffn_sw1, L0_ffn_sw3, L0_ffn_sw2, L1_cond_w, L1_cond_u, L1_ffn_gate_w,
           L1_ffn_cls_w, L1_ffn_extra_scale, L1_ffn_extra_bias, L1_ffn_wg, L1_ffn_wu, L1_ffn_wd, L1_ffn_sg,
           L1_ffn_su, L1_ffn_sd):
    import concourse.bacc as bacc
    from concourse.bass_utils import run_bass_kernel_spmd

    a = lambda v: np.asarray(v)
    chan = lambda v: a(v).reshape(C, P).T
    rep = lambda v, n: np.ascontiguousarray(np.broadcast_to(np.tile(a(v), n), (P, n * a(v).size)))
    halves = lambda w: a(w).reshape(2, F, D)
    gate_cols = lambda w: a(w).T.reshape(C, P, -1).transpose(1, 0, 2).reshape(P, -1)
    k = a(fside_BxSxS_0).transpose(0, 2, 1).reshape(B * C, P, T)
    ins = {
        "x": a(x).reshape(N, D),
        "kt": np.ascontiguousarray(np.concatenate([k] * LAYERS)),
        "cond": rep(a(cond_512).reshape(-1), 1),
        "wdec": np.ascontiguousarray(np.concatenate([chan(L0_cond_w), chan(L1_cond_w)], axis=1)),
        "ub": np.ascontiguousarray(np.concatenate([chan(L0_cond_u)] * B + [chan(L1_cond_u)] * B, axis=1)),
        "gates0": np.ascontiguousarray(gate_cols(L0_ffn_gate_w)),
        "gates1": np.ascontiguousarray(gate_cols(np.concatenate([a(L1_ffn_cls_w), a(L1_ffn_gate_w)]))),
        "bias0": rep(L0_ffn_router_bias, 1),
        "bias1": rep(L1_ffn_extra_bias, 1),
        "scale1": rep(L1_ffn_extra_scale, 1),
        "wts0": pack_experts(
            np.concatenate([a(L0_ffn_W3), halves(L0_ffn_sw3).transpose(0, 2, 1)]),
            np.concatenate([a(L0_ffn_W1), halves(L0_ffn_sw1).transpose(0, 2, 1)]),
            np.concatenate([a(L0_ffn_W2), a(L0_ffn_sw2).T.reshape(2, F, D)])),
        "wts1": pack_experts(
            np.concatenate([a(L1_ffn_wu), halves(L1_ffn_su)]).transpose(0, 2, 1),
            np.concatenate([a(L1_ffn_wg), halves(L1_ffn_sg)]).transpose(0, 2, 1),
            np.concatenate([a(L1_ffn_wd).transpose(0, 2, 1), a(L1_ffn_sd).T.reshape(2, F, D)])),
    }
    nc = bacc.Bacc("TRN2", target_bir_lowering=False, num_devices=1)
    ap = {n: nc.dram_tensor(f"in_{n}", v.shape, mybir.dt.float32, kind="ExternalInput").ap() for n, v in ins.items()}
    out = nc.dram_tensor("out_x", (N, D), mybir.dt.float32, kind="ExternalOutput").ap()
    build(nc, ap["x"], ap["kt"], ap["cond"], ap["wdec"], ap["ub"], (ap["gates0"], ap["gates1"]),
          (ap["bias0"], ap["bias1"]), ap["scale1"], (ap["wts0"], ap["wts1"]), out)
    r = run_bass_kernel_spmd(nc, [{f"in_{n}": v for n, v in ins.items()}], core_ids=[0])
    return r.results[0]["out_x"].reshape(B, T, D)
```
